# Optimizing a Trainium2 kernel written in Bass

```python
import numpy as np
import jax
import jax.numpy as jnp

def _softmax(x, axis=-1):
    return jax.nn.softmax(x, axis=axis)

def _gelu(x):
    return jax.nn.gelu(x, approximate=True)

def _silu(x):
    return jax.nn.silu(x)

def _sigmoid(x):
    return jax.nn.sigmoid(x)

def _layernorm(x, axis=-1, eps=1e-05):
    m = jnp.mean(x, axis=axis, keepdims=True)
    v = jnp.var(x, axis=axis, keepdims=True)
    return (x - m) / jnp.sqrt(v + eps)

def _scatter_add(tgt, idx, src, axis=0):
    return tgt.at[idx].add(src)

def _segment_sum(src, seg, n):
    return jax.ops.segment_sum(src, seg, n)
kernel_name = 'mk_gnn_resnorm_d4_gnn_r64_9f25eb'

def setup_inputs(seed: int=0):
    np.random.seed(seed)
    _w = jnp.asarray

    def _rec_inputs():
        import jax
        import jax.numpy as jnp
        _gk = jax.random.key(seed)
        x = -0.0002117 + 1 * jax.random.normal(jax.random.fold_in(_gk, 1), (50000, 256), jnp.float32)
        src = jax.random.randint(jax.random.fold_in(_gk, 2), (25000,), 0, 50000, jnp.int32)
        dst = jnp.minimum((50000 * jax.random.uniform(jax.random.fold_in(_gk, 3), (25000,)) ** 2.0).astype(jnp.int32), 49999)
        _o = jnp.argsort(dst, stable=True)
        src = src[_o]
        dst = dst[_o]
        edge_type_16 = jax.random.randint(jax.random.fold_in(_gk, 12), (25000,), 0, 16, jnp.int32)
        edge_weight = jax.random.uniform(jax.random.fold_in(_gk, 13), (25000,), jnp.float32, 0.0, 0.999998)
        return (x, src, dst, edge_type_16, edge_weight)
    x, src, dst, edge_type_16, edge_weight = _rec_inputs()

    def _L0_gnn_setup():
        import jax, jax.numpy as jnp
        import numpy as np
        N = 100000
        E = 300000
        D = 256

        def _mean_aggregate(x, edge_index, num_nodes):
            src, dst = (edge_index[0], edge_index[1])
            msgs = x[src]
            summed = jax.ops.segment_sum(msgs, dst, num_segments=num_nodes)
            counts = jax.ops.segment_sum(jnp.ones((edge_index.shape[1],), x.dtype), dst, num_segments=num_nodes)
            return summed / jnp.maximum(counts, 1.0)[:, None]
        key = jax.random.key(seed)
        k1, k2, k3, k4, k5, k6 = jax.random.split(key, 6)
        x = jax.random.normal(k1, (N, D), dtype=jnp.float32)
        edge_index = jax.random.randint(k2, (2, E), 0, N, dtype=jnp.int64)
        edge_weight = jax.random.uniform(k3, (E,), dtype=jnp.float32)
        lim = 1.0 / np.sqrt(D)
        W_l = jax.random.uniform(k4, (D, D), dtype=jnp.float32, minval=-lim, maxval=lim)
        b_l = jax.random.uniform(k5, (D,), dtype=jnp.float32, minval=-lim, maxval=lim)
        W_r = jax.random.uniform(k6, (D, D), dtype=jnp.float32, minval=-lim, maxval=lim)
        return {'x': x, 'edge_index': edge_index, 'edge_weight': edge_weight, 'W_l': W_l, 'b_l': b_l, 'W_r': W_r}
    _L0_gnn_all = _L0_gnn_setup()
    _L0_gnn_in = {k: v for k, v in _L0_gnn_all.items() if k in ('W_l', 'b_l', 'W_r')}
    del _L0_gnn_all

    def _L1_gnn_setup():
        import jax, jax.numpy as jnp
        import numpy as np
        NUM_BLOCKS = 64

        def rgcn_layer(x, src, dst, edge_type, W, root, bias):
            N, d = x.shape
            xj = x[src]
            out0 = x @ root + bias

            def body(out, inputs):
                r, Wr = inputs
                mask = (edge_type == r).astype(x.dtype)
                s = jax.ops.segment_sum(xj * mask[:, None], dst, num_segments=N)
                cnt = jax.ops.segment_sum(mask, dst, num_segments=N)
                h = s / jnp.maximum(cnt, 1.0)[:, None]
                hb = h.reshape(N, NUM_BLOCKS, d // NUM_BLOCKS)
                out = out + jnp.einsum('nbi,bio->nbo', hb, Wr).reshape(N, d)
                return (out, None)
            R = W.shape[0]
            out, _ = jax.lax.scan(body, out0, (jnp.arange(R), W))
            return out
        key = jax.random.key(seed)
        ks = jax.random.split(key, 9)
        N, d, R, E = (50000, 256, 16, 12500)
        db = d // NUM_BLOCKS
        return {'node_emb': jax.random.normal(ks[0], (N, d), jnp.float32), 'edge_index': jax.random.randint(ks[1], (2, E), 0, N), 'edge_type': jax.random.randint(ks[2], (E,), 0, R), 'W1': jax.random.normal(ks[3], (R, NUM_BLOCKS, db, db), jnp.float32) * 0.1, 'root1': jax.random.normal(ks[4], (d, d), jnp.float32) * 0.05, 'bias1': jnp.zeros((d,), jnp.float32), 'W2': jax.random.normal(ks[5], (R, NUM_BLOCKS, db, db), jnp.float32) * 0.1, 'root2': jax.random.normal(ks[6], (d, d), jnp.float32) * 0.05, 'bias2': jnp.zeros((d,), jnp.float32)}
    _L1_gnn_all = _L1_gnn_setup()
    _L1_gnn_in = {k: v for k, v in _L1_gnn_all.items() if k in ('W1', 'root1', 'bias1', 'W2', 'root2', 'bias2')}
    del _L1_gnn_all

    def _L2_gnn_setup():
        import jax, jax.numpy as jnp
        import numpy as np
        N_NODES = 100000
        IN_FEATS = 256
        OUT_FEATS = 256
        N_EDGES = 50000
        key = jax.random.key(seed)
        k1, k2, k3, k4 = jax.random.split(key, 4)
        x = jax.random.normal(k1, (N_NODES, IN_FEATS), dtype=jnp.float32)
        edge_index = jax.random.randint(k2, (2, N_EDGES), 0, N_NODES, dtype=jnp.int64)
        scale = 1.0 / np.sqrt(IN_FEATS)
        W = jax.random.uniform(k3, (IN_FEATS, OUT_FEATS), dtype=jnp.float32, minval=-scale, maxval=scale)
        b = jax.random.uniform(k4, (OUT_FEATS,), dtype=jnp.float32, minval=-scale, maxval=scale)
        return {'x': x, 'edge_index': edge_index, 'W': W, 'b': b}
    _L2_gnn_all = _L2_gnn_setup()
    _L2_gnn_in = {k: v for k, v in _L2_gnn_all.items() if k in ('W', 'b')}
    del _L2_gnn_all

    def _L3_gnn_setup():
        import jax, jax.numpy as jnp
        import numpy as np
        N, E, D = (10000, 5000, 256)

        def _add_self_loops(src, dst, n):
            loop = jnp.arange(n, dtype=src.dtype)
            return (jnp.concatenate([src, loop]), jnp.concatenate([dst, loop]))

        def _gcn_conv(x, W, b, src, dst, n):
            xw = x @ W
            deg = jax.ops.segment_sum(jnp.ones(src.shape[0], x.dtype), dst, num_segments=n)
            dinv = jnp.where(deg > 0, jax.lax.rsqrt(deg), 0.0)
            norm = dinv[src] * dinv[dst]
            agg = jax.ops.segment_sum(xw[src] * norm[:, None], dst, num_segments=n)
            return agg + b

        def _gat_conv(x, W, a_src, a_dst, b, src, dst, n):
            xw = x @ W
            e = jax.nn.leaky_relu((xw @ a_src)[src] + (xw @ a_dst)[dst], 0.2)
            m = jax.ops.segment_max(e, dst, num_segments=n)
            ex = jnp.exp(e - m[dst])
            s = jax.ops.segment_sum(ex, dst, num_segments=n)
            alpha = ex / (s[dst] + 1e-16)
            agg = jax.ops.segment_sum(alpha[:, None] * xw[src], dst, num_segments=n)
            return agg + b
        key = jax.random.key(seed)
        ks = jax.random.split(key, 6)
        return {'event_emb': jax.random.normal(ks[0], (N, D), jnp.float32), 'edge_index': jax.random.randint(ks[1], (2, E), 0, N), 'W1': jax.random.normal(ks[2], (D, D), jnp.float32) / np.sqrt(D).astype(np.float32), 'b1': jnp.zeros((D,), jnp.float32), 'W2': jax.random.normal(ks[3], (D, D), jnp.float32) / np.sqrt(D).astype(np.float32), 'att_src': jax.random.normal(ks[4], (D,), jnp.float32) / np.sqrt(D).astype(np.float32), 'att_dst': jax.random.normal(ks[5], (D,), jnp.float32) / np.sqrt(D).astype(np.float32), 'b2': jnp.zeros((D,), jnp.float32)}
    _L3_gnn_all = _L3_gnn_setup()
    _L3_gnn_in = {k: v for k, v in _L3_gnn_all.items() if k in ('W1', 'b1', 'W2', 'att_src', 'att_dst', 'b2')}
    del _L3_gnn_all
    return {'x': x, 'src': src, 'dst': dst, 'edge_type_16': edge_type_16, 'edge_weight': edge_weight, 'L0_gnn_W_l': _L0_gnn_in['W_l'], 'L0_gnn_b_l': _L0_gnn_in['b_l'], 'L0_gnn_W_r': _L0_gnn_in['W_r'], 'L1_gnn_W1': _L1_gnn_in['W1'], 'L1_gnn_root1': _L1_gnn_in['root1'], 'L1_gnn_bias1': _L1_gnn_in['bias1'], 'L1_gnn_W2': _L1_gnn_in['W2'], 'L1_gnn_root2': _L1_gnn_in['root2'], 'L1_gnn_bias2': _L1_gnn_in['bias2'], 'L2_gnn_W': _L2_gnn_in['W'], 'L2_gnn_b': _L2_gnn_in['b'], 'L3_gnn_W1': _L3_gnn_in['W1'], 'L3_gnn_b1': _L3_gnn_in['b1'], 'L3_gnn_W2': _L3_gnn_in['W2'], 'L3_gnn_att_src': _L3_gnn_in['att_src'], 'L3_gnn_att_dst': _L3_gnn_in['att_dst'], 'L3_gnn_b2': _L3_gnn_in['b2']}

def reference(x, src, dst, edge_type_16, edge_weight, L0_gnn_W_l, L0_gnn_b_l, L0_gnn_W_r, L1_gnn_W1, L1_gnn_root1, L1_gnn_bias1, L1_gnn_W2, L1_gnn_root2, L1_gnn_bias2, L2_gnn_W, L2_gnn_b, L3_gnn_W1, L3_gnn_b1, L3_gnn_W2, L3_gnn_att_src, L3_gnn_att_dst, L3_gnn_b2):
    import jax
    import jax.numpy as jnp

    def _L0_gnn_ref(x, edge_index, edge_weight, W_l, b_l, W_r):
        import jax, jax.numpy as jnp
        import numpy as np
        N = 100000
        E = 300000
        D = 256

        def _mean_aggregate(x, edge_index, num_nodes):
            src, dst = (edge_index[0], edge_index[1])
            msgs = x[src]
            summed = jax.ops.segment_sum(msgs, dst, num_segments=num_nodes)
            counts = jax.ops.segment_sum(jnp.ones((edge_index.shape[1],), x.dtype), dst, num_segments=num_nodes)
            return summed / jnp.maximum(counts, 1.0)[:, None]
        h = x
        agg = _mean_aggregate(x, edge_index, x.shape[0])
        out = agg @ W_l.T + b_l
        out = out + x @ W_r.T
        out = jax.nn.relu(out)
        return out + h

    def _L1_gnn_ref(node_emb, edge_index, edge_type, W1, root1, bias1, W2, root2, bias2):
        import jax, jax.numpy as jnp
        import numpy as np
        NUM_BLOCKS = 64

        def rgcn_layer(x, src, dst, edge_type, W, root, bias):
            N, d = x.shape
            xj = x[src]
            out0 = x @ root + bias

            def body(out, inputs):
                r, Wr = inputs
                mask = (edge_type == r).astype(x.dtype)
                s = jax.ops.segment_sum(xj * mask[:, None], dst, num_segments=N)
                cnt = jax.ops.segment_sum(mask, dst, num_segments=N)
                h = s / jnp.maximum(cnt, 1.0)[:, None]
                hb = h.reshape(N, NUM_BLOCKS, d // NUM_BLOCKS)
                out = out + jnp.einsum('nbi,bio->nbo', hb, Wr).reshape(N, d)
                return (out, None)
            R = W.shape[0]
            out, _ = jax.lax.scan(body, out0, (jnp.arange(R), W))
            return out
        src, dst = (edge_index[0], edge_index[1])
        x = jax.nn.relu(rgcn_layer(node_emb, src, dst, edge_type, W1, root1, bias1))
        x = rgcn_layer(x, src, dst, edge_type, W2, root2, bias2)
        return x

    def _L2_gnn_ref(x, edge_index, W, b):
        import jax, jax.numpy as jnp
        import numpy as np
        N_NODES = 100000
        IN_FEATS = 256
        OUT_FEATS = 256
        N_EDGES = 50000
        n = x.shape[0]
        row = edge_index[0]
        col = edge_index[1]
        h = x @ W + b
        agg = jax.ops.segment_sum(h[col], row, num_segments=n)
        deg = jax.ops.segment_sum(jnp.ones((edge_index.shape[1],), dtype=h.dtype), row, num_segments=n)
        inv_deg = jnp.where(deg > 0, 1.0 / jnp.where(deg > 0, deg, 1.0), 0.0)
        return agg * inv_deg[:, None]

    def _L3_gnn_ref(event_emb, edge_index, W1, b1, W2, att_src, att_dst, b2):
        import jax, jax.numpy as jnp
        import numpy as np
        N, E, D = (10000, 5000, 256)

        def _add_self_loops(src, dst, n):
            loop = jnp.arange(n, dtype=src.dtype)
            return (jnp.concatenate([src, loop]), jnp.concatenate([dst, loop]))

        def _gcn_conv(x, W, b, src, dst, n):
            xw = x @ W
            deg = jax.ops.segment_sum(jnp.ones(src.shape[0], x.dtype), dst, num_segments=n)
            dinv = jnp.where(deg > 0, jax.lax.rsqrt(deg), 0.0)
            norm = dinv[src] * dinv[dst]
            agg = jax.ops.segment_sum(xw[src] * norm[:, None], dst, num_segments=n)
            return agg + b

        def _gat_conv(x, W, a_src, a_dst, b, src, dst, n):
            xw = x @ W
            e = jax.nn.leaky_relu((xw @ a_src)[src] + (xw @ a_dst)[dst], 0.2)
            m = jax.ops.segment_max(e, dst, num_segments=n)
            ex = jnp.exp(e - m[dst])
            s = jax.ops.segment_sum(ex, dst, num_segments=n)
            alpha = ex / (s[dst] + 1e-16)
            agg = jax.ops.segment_sum(alpha[:, None] * xw[src], dst, num_segments=n)
            return agg + b
        n = event_emb.shape[0]
        src, dst = _add_self_loops(edge_index[0], edge_index[1], n)
        x = jax.nn.relu(_gcn_conv(event_emb, W1, b1, src, dst, n))
        x = jax.nn.relu(_gat_conv(x, W2, att_src, att_dst, b2, src, dst, n))
        return x
    edge_index = jnp.stack([src, dst])
    x = _layernorm(x + _L0_gnn_ref(x, edge_index, edge_weight, L0_gnn_W_l, L0_gnn_b_l, L0_gnn_W_r), axis=-1)
    x = _layernorm(x + _L1_gnn_ref(x, edge_index, edge_type_16, L1_gnn_W1, L1_gnn_root1, L1_gnn_bias1, L1_gnn_W2, L1_gnn_root2, L1_gnn_bias2), axis=-1)
    x = _layernorm(x + _L2_gnn_ref(x, edge_index, L2_gnn_W, L2_gnn_b), axis=-1)
    x = _layernorm(x + _L3_gnn_ref(x, edge_index, L3_gnn_W1, L3_gnn_b1, L3_gnn_W2, L3_gnn_att_src, L3_gnn_att_dst, L3_gnn_b2), axis=-1)
    return x

_drawn_inputs = setup_inputs


def setup_inputs(seed=0):
    import zlib

    import numpy as np

    out = dict(_drawn_inputs(seed))
    spreads = {'L1_gnn_bias1': (0.0, 0.1),
     'L1_gnn_bias2': (0.0, 0.1),
     'L3_gnn_b1': (0.0, 0.1),
     'L3_gnn_b2': (0.0, 0.1)}
    factors = {'L0_gnn_b_l': 4.44, 'L2_gnn_b': 2.771, 'L3_gnn_att_src': 4.618, 'L3_gnn_att_dst': 8.0}
    for name, (base, spread) in spreads.items():
        noise = np.random.default_rng([zlib.crc32(name.encode()), seed]).standard_normal(out[name].shape)
        drawn = base * np.exp(spread * noise) if base else spread * noise
        out[name] = jnp.asarray(drawn.astype(out[name].dtype))
    for name, factor in factors.items():
        out[name] = (out[name] * factor).astype(out[name].dtype)
    return out
```

```python
from contextlib import ExitStack

import concourse.bass as bass
from concourse import mybir

F32 = mybir.dt.float32
BF16 = mybir.dt.bfloat16
I32 = mybir.dt.int32
ALU = mybir.AluOpType
ACT = mybir.ActivationFunctionType
AX = mybir.AxisListType

P = 128
SLOTS = 4
R = 6
PAIRS = R // 2
EPS = 1e-5
FAR = 1000000.0
RELS = 16


class Counter:

    def __init__(self, sem):
        self.sem = sem
        self.base = 0

    def at(self, n):
        return n + self.base

    def close(self, steps):
        self.base += steps


def gnn_kernel(nc, A, out):
    x_in = A["x"]
    N, D = x_in.shape
    E = A["src"].shape[0]
    T = -(-E // P)
    EP = P * T
    FULLP = E // T
    RESTE = E - FULLP * T
    assert D == 256 and T % SLOTS == 0 and N < 256 * 256
    ITERS = T // SLOTS
    AUX = 4
    DW = D + AUX
    HEAD = N + 1
    AGGR = -(-(HEAD + P) // P) * P
    BATCH = P * R
    NBATCH = N // BATCH
    PEEL = NBATCH % 2
    LOOPS = NBATCH // 2
    REST = N - NBATCH * BATCH
    assert 0 < REST <= P
    NT = NBATCH * R + 1
    C2 = D // P

    ctx = ExitStack()
    with ctx:
        def sb(name, shape, dt=F32, stack=ctx):
            return stack.enter_context(nc.sbuf_tensor(name, shape, dt))

        def counter(name):
            return Counter(ctx.enter_context(nc.semaphore(name)))

        def dram(name, shape, dt=F32):
            return nc.dram_tensor(name, shape, dt, kind="Internal").ap()

        sorted_lo = dram("sorted_lo", [EP + 2, 4])
        by_dst = dram("by_dst", [EP + 2, 4])
        by_src = dram("by_src", [EP + 2, 4])
        agg_d = dram("agg_d", [AGGR, DW])
        agg_s = dram("agg_s", [AGGR, D])
        x1 = dram("x1", [N, D])
        y1 = dram("y1", [N, D])
        x2 = dram("x2", [N, D])
        x3 = dram("x3", [N, DW])
        y3 = dram("y3", [N, D])
        att = dram("att", [N, 2])

        ident = sb("ident", [P, P])
        identb = sb("identb", [P, P], BF16)
        lower = sb("lower", [P, P])
        lowerb = sb("lowerb", [P, P], BF16)
        upper = sb("upper", [P, P])
        ones = sb("ones", [P, P])
        onesb = sb("onesb", [P, P], BF16)
        iota = sb("iota", [P, D], BF16)
        rel_iota = sb("rel_iota", [P, 96], BF16)
        part = sb("part", [P, 1])
        zero_b = sb("zero_b", [P, D], BF16)
        mats = {n: sb("w_" + n, [P, C2, D]) for n in ("wl", "wr", "root1", "root2", "l2", "g1", "g2")}
        rel_w = [sb(f"rel_w{i}", [96, 1024], BF16) for i in range(2)]
        bias3 = {n: sb("b_" + n, [3, D], BF16) for n in ("bl", "bias1", "bias2", "b2")}
        b_l2 = sb("b_l2", [P, D])
        b_g1 = sb("b_g1", [P, D])
        va = sb("va", [P, D])
        vb = sb("vb", [P, D])
        eps_col = sb("eps_col", [P, 2])
        cnt_nodes = sb("cnt_nodes", [P, NT])
        dinv = sb("dinv", [P, NT])

        class Edges:
            pass
        ed, es = Edges(), Edges()
        for o, s in ((ed, "d"), (es, "s")):
            o.same = sb("same_" + s, [P, T])
            o.gather = sb("gather_" + s, [P, T], I32)
            o.scatter = sb("scatter_" + s, [P, T], I32)
            o.head = sb("head_" + s, [P, 1], I32)
            o.carry = sb("carry_" + s, [P, P])
            o.weight = sb("weight_" + s, [P, T])
        ed.samen = sb("samen", [P, T])
        ed.end = sb("end", [P, T])
        ed.inhead = sb("inhead", [P, T])
        ed.intail = sb("intail", [P, T])
        ed.back = sb("back", [P, P])
        ed.dst = sb("dst_idx", [P, T], I32)
        ed.rel = sb("rel", [P, T])
        w_rel = sb("w_rel", [P, T])
        rel_hot = sb("rel_hot", [96, T * P], BF16)
        aux = sb("aux", [P, T, AUX])

        load = [counter(f"load{i}") for i in range(4)]
        stored = [counter(f"stored{i}") for i in range(3)]
        idx_ready = [counter(f"idx_ready{k}") for k in range(SLOTS)]
        gathered = [counter(f"gathered{k}") for k in range(SLOTS)]
        scattered = [counter(f"scattered{k}") for k in range(SLOTS)]
        msg_ready = [counter(f"msg_ready{k}") for k in range(SLOTS)]
        acc_ready = [counter(f"acc_ready{k}") for k in range(SLOTS)]
        row_ready = [counter(f"row_ready{k}") for k in range(SLOTS)]
        relw_ready = [counter(f"relw_ready{k}") for k in range(SLOTS)]
        prod_ready = [counter(f"prod_ready{k}") for k in range(SLOTS)]
        turned = [counter(f"turned{k}") for k in range(SLOTS)]
        turned_sb = [counter(f"turned_sb{k}") for k in range(SLOTS)]
        product = [counter(f"product{k}") for k in range(SLOTS)]
        pre_ready = [counter(f"pre_ready{k}") for k in range(SLOTS)]
        batch_done = [counter(f"batch_done{k}") for k in range(2)]
        batch_out = [counter(f"batch_out{k}") for k in range(2)]
        chain = counter("chain")
        pe_step = counter("pe_step")
        act_step = counter("act_step")
        pool_step = counter("pool_step")
        ready = counter("ready")
        cleared = counter("cleared")
        own_step = counter("own_step")
        deviation = counter("deviation")

        def link(eng, ins):
            chain.close(1)
            ins.then_inc(chain.sem, 1)
            eng.wait_ge(chain.sem, chain.base)

        with ExitStack() as tmp:
            w_raw = sb("w_raw", [P, 2, C2, D], F32, tmp)
            att_col = sb("att_col", [P, 2, C2], F32, tmp)
            att_bc = sb("att_bc", [P, 2, C2, P], F32, tmp)
            w2t = sb("w2t", [P, C2, D], F32, tmp)
            rel_raw = sb("rel_raw", [96, 2, 1024], F32, tmp)
            rel_hi = sb("rel_hi", [96, 2, 1024], BF16, tmp)
            rel_mid = sb("rel_mid", [96, 2, 1024], BF16, tmp)
            rel_lo = sb("rel_lo", [96, 2, 1024], BF16, tmp)
            b_raw = sb("b_raw", [3, 4, D], F32, tmp)
            b_part = sb("b_part", [3, 3, 4, D], BF16, tmp)
            sel = sb("sel", [P, 6], F32, tmp)
            tp = tmp.enter_context(nc.psum_tensor("tp", [P, 4, 512], F32))
            bc = tmp.enter_context(nc.psum_tensor("bc", [P, 2, 512], F32))

            names = ("bl", "bias1", "bias2", "b2")
            b_dram = (A["L0_gnn_b_l"], A["L1_gnn_bias1"], A["L1_gnn_bias2"], A["L3_gnn_b2"])
            plain = {"root1": "L1_gnn_root1", "root2": "L1_gnn_root2", "l2": "L2_gnn_W",
                     "g1": "L3_gnn_W1", "g2": "L3_gnn_W2"}
            block = tmp.enter_context(nc.Block())

            @block.sync
            def _(sp):
                loads = 0
                for i, n in enumerate(("L0_gnn_W_l", "L0_gnn_W_r")):
                    sp.dma_start(w_raw[:, i], A[n].rearrange("(c p) n -> p c n", p=P)).then_inc(load[0].sem, 16)
                    loads += 1
                for n, src in plain.items():
                    sp.dma_start(mats[n][:, :, :], A[src].rearrange("(c p) n -> p c n", p=P)).then_inc(load[0].sem, 16)
                    loads += 1
                for i, n in enumerate(("L3_gnn_att_src", "L3_gnn_att_dst")):
                    for c in range(C2):
                        sp.dma_start(att_col[:, i, c:c + 1], A[n][c * P:(c + 1) * P].rearrange("(p a) -> p a", a=1)).then_inc(load[0].sem, 16)
                        loads += 1
                sp.dma_start(b_l2[:, :], A["L2_gnn_b"].rearrange("(a d) -> a d", a=1).broadcast_to([P, D])).then_inc(load[0].sem, 16)
                sp.dma_start(b_g1[:, :], A["L3_gnn_b1"].rearrange("(a d) -> a d", a=1).broadcast_to([P, D])).then_inc(load[0].sem, 16)
                loads += 2
                for i in range(4):
                    for k in range(3):
                        sp.dma_start(b_raw[k:k + 1, i, :], b_dram[i].rearrange("(a d) -> a d", a=1)).then_inc(load[0].sem, 16)
                        loads += 1
                sp.wait_ge(pool_step.sem, 1)
                for i, n in enumerate(("L1_gnn_W1", "L1_gnn_W2")):
                    for k in range(3):
                        for j in range(4):
                            sp.dma_start(rel_raw[32 * k:32 * k + RELS, i, j * D:(j + 1) * D].rearrange("r (b o) -> r b o", o=4),
                                         A[n].rearrange("r b i o -> i r b o")[j]).then_inc(load[1].sem, 16)
                load[0].close(16 * loads)
                load[1].close(16 * 24)

            @block.gpsimd
            def _(pool):
                pool.memset(rel_raw[:, :, :], 0.0).then_inc(pool_step.sem, 1)
                pool.memset(ones[:, :], 1.0)
                pool.memset(onesb[:, :], 1.0)
                pool.memset(eps_col[:, 0:1], EPS / 4)
                pool.memset(eps_col[:, 1:2], EPS)
                pool.memset(zero_b[:, :], 0.0)
                pool.iota(iota[:, :], [[1, D]], base=0, channel_multiplier=0, allow_small_or_imprecise_dtypes=True)
                pool.iota(rel_iota[:, :], [[0, 3], [1, 32]], base=0, channel_multiplier=0, allow_small_or_imprecise_dtypes=True)
                pool.iota(part[:, :], [[0, 1]], base=0, channel_multiplier=1, allow_small_or_imprecise_dtypes=True).then_inc(pool_step.sem, 1)
                pool.wait_ge(pool_step.sem, 2)
                pool.affine_select(ident[:, :], ones[:, :], [[-1, P]], ALU.is_equal, 0.0, base=0, channel_multiplier=1)
                pool.affine_select(identb[:, :], onesb[:, :], [[-1, P]], ALU.is_equal, 0.0, base=0, channel_multiplier=1)
                pool.affine_select(lower[:, :], ones[:, :], [[1, P]], ALU.is_gt, 0.0, base=0, channel_multiplier=-1)
                pool.affine_select(lowerb[:, :], onesb[:, :], [[1, P]], ALU.is_gt, 0.0, base=0, channel_multiplier=-1)
                pool.affine_select(upper[:, :], ones[:, :], [[-1, P]], ALU.is_gt, 0.0, base=0, channel_multiplier=1).then_inc(pool_step.sem, 1)
            pool_step.close(3)

            @block.vector
            def _(dve):
                dve.wait_ge(pool_step.sem, 3)
                for k in range(3):
                    link(dve, dve.tensor_scalar(sel[:, k:k + 1], part[:, :], float(k), None, ALU.is_equal))
                    link(dve, dve.tensor_scalar(sel[:, 3 + k:4 + k], part[:, :], 32.0 * k, None, ALU.is_ge))
                for k in range(2):
                    link(dve, dve.tensor_tensor(sel[:, 3 + k:4 + k], sel[:, 3 + k:4 + k], sel[:, 4 + k:5 + k], ALU.subtract))
                dve.wait_ge(load[0].sem, load[0].base)
                link(dve, dve.tensor_scalar(w_raw[:, :, :, :], w_raw[:, :, :, :], 0.5, None, ALU.mult))
                link(dve, dve.tensor_scalar(b_raw[:, 0, :], b_raw[:, 0, :], 0.5, None, ALU.mult))
                for i in range(2):
                    for c in range(C2):
                        link(dve, dve.tensor_scalar(att_bc[:, i, c, :], ones[:, :], att_col[:, i, c:c + 1], None, ALU.mult))
                ready.close(1)
                dve.nop().then_inc(ready.sem, 1)
                link(dve, dve.tensor_copy(b_part[:, 0], b_raw[:, :, :]))
                link(dve, dve.tensor_tensor(b_raw[:, :, :], b_raw[:, :, :], b_part[:, 0], ALU.subtract))
                link(dve, dve.tensor_copy(b_part[:, 1], b_raw[:, :, :]))
                link(dve, dve.tensor_tensor(b_raw[:, :, :], b_raw[:, :, :], b_part[:, 1], ALU.subtract))
                link(dve, dve.tensor_copy(b_part[:, 2], b_raw[:, :, :]))
                for i, n in enumerate(names):
                    o = bias3[n][:, :]
                    link(dve, dve.tensor_scalar(o, b_part[:, 0, i, :], sel[0:3, 0:1], None, ALU.mult))
                    for k in (1, 2):
                        link(dve, dve.scalar_tensor_tensor(o, b_part[:, k, i, :], sel[0:3, k:k + 1], o, ALU.mult, ALU.add))
                dve.wait_ge(load[1].sem, load[1].base)
                link(dve, dve.tensor_copy(rel_hi[:, :, :], rel_raw[:, :, :]))
                link(dve, dve.tensor_tensor(rel_raw[:, :, :], rel_raw[:, :, :], rel_hi[:, :, :], ALU.subtract))
                link(dve, dve.tensor_copy(rel_mid[:, :, :], rel_raw[:, :, :]))
                link(dve, dve.tensor_tensor(rel_raw[:, :, :], rel_raw[:, :, :], rel_mid[:, :, :], ALU.subtract))
                link(dve, dve.tensor_copy(rel_lo[:, :, :], rel_raw[:, :, :]))
                for i in range(2):
                    o = rel_w[i][:, :]
                    link(dve, dve.tensor_scalar(o, rel_hi[:, i, :], sel[0:96, 3:4], None, ALU.mult))
                    for k, part_k in ((1, rel_mid), (2, rel_lo)):
                        link(dve, dve.scalar_tensor_tensor(o, part_k[:, i, :], sel[0:96, 3 + k:4 + k], o, ALU.mult, ALU.add))
                for i, o in enumerate((mats["wl"], mats["wr"], w2t)):
                    dve.wait_ge(pe_step.sem, 1 + i)
                    for c in range(C2):
                        link(dve, dve.tensor_copy(o[:, c, :], tp[:, c, 0:D]))
                dve.wait_ge(pe_step.sem, 4)
                link(dve, dve.tensor_copy(va[:, :], bc[:, 0, 0:D]))
                link(dve, dve.tensor_copy(vb[:, :], bc[:, 1, 0:D]))

            @block.tensor
            def _(pe):
                pe.wait_ge(ready.sem, ready.base)
                done = chain.base - 2 - 6
                srcs = (lambda j, c: w_raw[:, 0, j, c * P:(c + 1) * P],
                        lambda j, c: w_raw[:, 1, j, c * P:(c + 1) * P],
                        lambda j, c: mats["g2"][:, j, c * P:(c + 1) * P])
                for i, s in enumerate(srcs):
                    if i:
                        pe.wait_ge(chain.sem, done + 2 * i)
                    for j in range(C2):
                        for c in range(C2):
                            ins = pe.transpose(tp[:, c, j * P:(j + 1) * P], s(j, c), ident[:, :])
                    ins.then_inc(pe_step.sem, 1)
                pe.wait_ge(chain.sem, done + 6)
                for i in range(2):
                    for c in range(C2):
                        ins = pe.matmul(bc[:, i, 0:D], att_bc[:, i, c, :], w2t[:, c, :], start=(c == 0), stop=(c == C2 - 1))
                ins.then_inc(pe_step.sem, 1)
                pe_step.close(4)

        def sort_pass(name, columns, digit, target):
            with ExitStack() as tmp:
                rec = sb(f"rec_{name}", [P, T, 4], F32, tmp)
                raw = sb(f"raw_{name}", [P, 3, T], I32, tmp)
                key = sb(f"key_{name}", [P, T], I32, tmp)
                dig_i = sb(f"digi_{name}", [P, T], I32, tmp)
                dig = sb(f"dig_{name}", [P, T], F32, tmp)
                hot = sb(f"hot_{name}", [P, SLOTS, D], BF16, tmp)
                hist = sb(f"hist_{name}", [P, D], BF16, tmp)
                total = sb(f"total_{name}", [P, D], F32, tmp)
                place = sb(f"place_{name}", [P, D], F32, tmp)
                junk = sb(f"junk_{name}", [P, D], F32, tmp)
                rank = sb(f"rank_{name}", [P, SLOTS], F32, tmp)
                to = sb(f"to_{name}", [P, SLOTS], I32, tmp)
                out_rec = sb(f"outrec_{name}", [P, SLOTS, 4], F32, tmp)
                ph = tmp.enter_context(nc.psum_tensor(f"ph_{name}", [P, 3, 512], F32))
                n_load = 1 if columns is None else 2 * len(columns)
                chain0 = {}
                block = tmp.enter_context(nc.Block())

                @block.sync
                def _(sp):
                    if columns is None:
                        sp.dma_start(rec[:, :, :].rearrange("p t f -> p (t f)"),
                                     sorted_lo[1:EP + 1, :].rearrange("(p t) f -> p (t f)", p=P)).then_inc(load[0].sem, 16)
                    else:
                        sp.wait_ge(ready.sem, ready.at(1))
                        for i, src in enumerate(columns):
                            sp.dma_start(raw[0:FULLP, i, :], src[0:FULLP * T].rearrange("(p t) -> p t", t=T)).then_inc(load[0].sem, 16)
                            sp.dma_start(raw[FULLP:FULLP + 1, i, 0:RESTE], src[FULLP * T:E].rearrange("(a t) -> a t", a=1)).then_inc(load[0].sem, 16)
                load[0].close(16 * n_load)
                

                @block.vector
                def _(dve):
                    if columns is not None:
                        dve.memset(raw[:, 1:3, :], 0)
                        dve.memset(rec[:, :, 3:4], 0.0)
                        dve.memset(raw[:, 0, :], N).then_inc(ready.sem, 1)
                    dve.wait_ge(load[0].sem, load[0].base)
                    for i in range(3 if columns is not None else 0):
                        link(dve, dve.tensor_copy(rec[:, :, i], raw[:, i, :]))
                    link(dve, dve.tensor_copy(key[:, :], rec[:, :, 0]))
                    op, by = (ALU.bitwise_and, 255) if digit == 0 else (ALU.logical_shift_right, 8)
                    link(dve, dve.tensor_scalar(dig_i[:, :], key[:, :], by, None, op))
                    link(dve, dve.tensor_copy(dig[:, :], dig_i[:, :]))
                    with dve.Fori(0, ITERS) as i:
                        for k in range(SLOTS):
                            dve.wait_ge(product[k].sem, product[k].at(i))
                            dve.tensor_scalar(hot[:, k, :], iota[:, :], dig[:, bass.ds(i * SLOTS + k, 1)], None, ALU.is_equal).then_inc(msg_ready[k].sem, 1)
                    dve.wait_ge(pe_step.sem, pe_step.at(1))
                    link(dve, dve.tensor_copy(hist[:, :], ph[:, 0, 0:D]))
                    chain0["hist"] = chain.base
                    dve.wait_ge(pe_step.sem, pe_step.at(2))
                    link(dve, dve.tensor_copy(total[:, :], ph[:, 2, 0:D]))
                    link(dve, dve.tensor_tensor_scan(place[:, :], ones[:, 0:1].broadcast_to([P, D]), total[:, :], 0.0, ALU.mult, ALU.add))
                    link(dve, dve.tensor_tensor(place[:, :], place[:, :], total[:, :], ALU.subtract))
                    link(dve, dve.tensor_tensor(place[:, :], place[:, :], ph[:, 1, 0:D], ALU.add))
                    with dve.Fori(0, ITERS) as i:
                        for k in range(SLOTS):
                            before_k = acc_ready[(k - 1) % SLOTS]
                            dve.tensor_scalar(hot[:, k, :], iota[:, :], dig[:, bass.ds(i * SLOTS + k, 1)], None, ALU.is_equal).then_inc(turned[k].sem, 1)
                            dve.wait_ge(turned[k].sem, turned[k].at(i + 1))
                            dve.wait_ge(before_k.sem, before_k.at(i + (k > 0)))
                            dve.scalar_tensor_tensor(junk[:, :], place[:, :], 1.0, hot[:, k, :], ALU.mult, ALU.mult, accum_out=rank[:, k:k + 1]).then_inc(turned_sb[k].sem, 1)
                            dve.wait_ge(turned_sb[k].sem, turned_sb[k].at(i + 1))
                            dve.tensor_tensor(place[:, :], place[:, :], hot[:, k, :], ALU.add).then_inc(acc_ready[k].sem, 1)
                            dve.wait_ge(scattered[k].sem, scattered[k].at(i * 16))
                            dve.tensor_copy(out_rec[:, k, :], rec[:, bass.ds(i * SLOTS + k, 1), :].rearrange("p a f -> p (a f)"))
                            dve.tensor_scalar(to[:, k:k + 1], rank[:, k:k + 1], 1.0, None, ALU.add).then_inc(row_ready[k].sem, 1)

                if columns is not None:
                    ready.close(1)

                @block.tensor
                def _(pe):
                    pe.matmul(ph[:, 0, 0:D], identb[:, :], zero_b[:, :], start=True, stop=False)
                    with pe.Fori(0, ITERS) as i:
                        for k in range(SLOTS):
                            pe.wait_ge(msg_ready[k].sem, msg_ready[k].at(i + 1))
                            pe.matmul(ph[:, 0, 0:D], identb[:, :], hot[:, k, :], start=False, stop=False).then_inc(product[k].sem, 1)
                    pe.matmul(ph[:, 0, 0:D], identb[:, :], zero_b[:, :], start=False, stop=True).then_inc(pe_step.sem, 1)
                    pe.wait_ge(chain.sem, chain0["hist"])
                    pe.matmul(ph[:, 1, 0:D], lowerb[:, :], hist[:, :], start=True, stop=True)
                    pe.matmul(ph[:, 2, 0:D], onesb[:, :], hist[:, :], start=True, stop=True).then_inc(pe_step.sem, 1)

                @block.gpsimd
                def _(pool):
                    with pool.Fori(0, ITERS) as i:
                        for k in range(SLOTS):
                            pool.wait_ge(row_ready[k].sem, row_ready[k].at(i + 1))
                            pool.nop(nofuse=True)
                            pool.indirect_dma_start(
                                out=target[:, :], out_offset=bass.IndirectOffsetOnAxis(ap=to[:, k:k + 1], axis=0),
                                in_=out_rec[:, k, :], in_offset=None, bounds_check=EP, oob_is_err=False).then_inc(scattered[k].sem, 16)
                    for k in range(SLOTS):
                        pool.wait_ge(scattered[k].sem, scattered[k].at(16 * ITERS))
                for k in range(SLOTS):
                    product[k].close(ITERS); msg_ready[k].close(ITERS); acc_ready[k].close(ITERS)
                    turned[k].close(ITERS); turned_sb[k].close(ITERS); row_ready[k].close(ITERS)
                    scattered[k].close(16 * ITERS)
                pe_step.close(2)

        primed_dma = [*scattered, *stored[0:2]]
        primed = [c for group in (idx_ready, msg_ready, acc_ready, row_ready, turned, turned_sb, product,
                                  pre_ready, relw_ready, prod_ready, batch_done, batch_out) for c in group]

        with ExitStack() as tmp:
            zeros = sb("zeros", [P, 28 * DW], F32, tmp)
            edge_key = sb("edge_key", [1, 4], F32, tmp)
            block = tmp.enter_context(nc.Block())
            Q = AGGR // P
            assert Q % 28 == 0

            @block.vector
            def _(dve):
                dve.memset(edge_key[:, :], -1.0)
                dve.memset(zeros[:, :], 0.0).then_inc(ready.sem, 1)

            @block.gpsimd
            def _(pool):
                pool.wait_ge(ready.sem, ready.at(1))
                for c in primed_dma:
                    pool.dma_start(sorted_lo[0:1, :], edge_key[:, :]).then_inc(c.sem, 16)
                    pool.wait_ge(c.sem, 16)
                    c.close(16)

            @block.scalar
            def _(act):
                for c in primed:
                    act.sem_inc(c.sem, 1)
                    c.close(1)

            @block.sync
            def _(sp):
                sp.wait_ge(ready.sem, ready.at(1))
                for a, w in ((agg_d, DW), (agg_s, D)):
                    v = a.rearrange("(p q r) d -> q p (r d)", p=P, r=28)
                    for q in range(Q // 28):
                        sp.dma_start(v[q], zeros[:, 0:28 * w]).then_inc(cleared.sem, 16)
                for a in (by_dst, by_src):
                    for r in (0, EP + 1):
                        sp.dma_start(a[r:r + 1, :], edge_key[:, :]).then_inc(cleared.sem, 16)
                sp.wait_ge(cleared.sem, cleared.at(16 * (2 * (Q // 28) + 4)))
            cleared.close(16 * (2 * (Q // 28) + 4))
            ready.close(1)

        sort_pass("d0", (A["dst"], A["src"], A["edge_type_16"]), 0, sorted_lo)
        sort_pass("d1", None, 1, by_dst)
        sort_pass("s0", (A["src"], A["dst"]), 0, sorted_lo)
        sort_pass("s1", None, 1, by_src)

        def prepare(o, src_dram, name, with_rel):
            C = RELS + 1 if with_rel else 1
            with ExitStack() as tmp:
                prv = sb("prv_" + name, [P, T, 4], F32, tmp)
                rec = sb("cur_" + name, [P, T, 4], F32, tmp)
                nxt = sb("nxt_" + name, [P, T, 4], F32, tmp)
                diag = sb("diag_" + name, [P, 2, P], F32, tmp)
                f1 = sb("f1_" + name, [P, T], F32, tmp)
                f2 = sb("f2_" + name, [P, T], F32, tmp)
                samen = sb("samen_" + name, [P, T], F32, tmp)
                end = sb("end_" + name, [P, T], F32, tmp)
                inhead = sb("inhead_" + name, [P, T], F32, tmp)
                intail = sb("intail_" + name, [P, T], F32, tmp)
                back = sb("back_" + name, [P, P], F32, tmp)
                sameC = sb("sameC_" + name, [P, C, T], F32, tmp)
                samenC = sb("samenC_" + name, [P, C, T], F32, tmp)
                V = sb("V_" + name, [P, C, T], F32, tmp)
                fwd = sb("fwd_" + name, [P, C * T], F32, tmp)
                bwd = sb("bwd_" + name, [P, C * T], F32, tmp)
                runs = sb("runs_" + name, [P, 2, C], F32, tmp)
                ph = tmp.enter_context(nc.psum_tensor("ph_" + name, [P, 2, 512], F32))
                pc = tmp.enter_context(nc.psum_tensor("pc_" + name, [P, 2, 512], F32))
                marks = {}
                block = tmp.enter_context(nc.Block())

                @block.sync
                def _(sp):
                    for t_, r0 in ((prv, 0), (rec, 1), (nxt, 2)):
                        sp.dma_start(t_[:, :, :].rearrange("p t f -> p (t f)"),
                                     src_dram[r0:r0 + EP, :].rearrange("(p t) f -> p (t f)", p=P)).then_inc(load[0].sem, 16)
                load[0].close(48)

                @block.vector
                def _(dve):
                    dve.wait_ge(load[0].sem, load[0].base)
                    key, first, last = rec[:, :, 0], rec[:, 0, 0:1], rec[:, T - 1, 0:1]
                    link(dve, dve.tensor_tensor(o.same[:, :], key, prv[:, :, 0], ALU.is_equal))
                    link(dve, dve.memset(o.same[:, 0:1], 0.0))
                    link(dve, dve.tensor_tensor(samen[:, :], key, nxt[:, :, 0], ALU.is_equal))
                    link(dve, dve.tensor_scalar(end[:, :], samen[:, :], -1.0, 1.0, ALU.mult, ALU.add))
                    link(dve, dve.memset(samen[:, T - 1:T], 0.0))
                    link(dve, dve.tensor_scalar(inhead[:, :], key, first, None, ALU.is_equal))
                    link(dve, dve.tensor_scalar(intail[:, :], key, last, None, ALU.is_equal))
                    link(dve, dve.tensor_copy(o.gather[:, :], rec[:, :, 1]))
                    link(dve, dve.tensor_scalar(f1[:, :], part[:, :].broadcast_to([P, T]), float(HEAD), None, ALU.add))
                    link(dve, dve.tensor_tensor(f1[:, :], f1[:, :], key, ALU.subtract))
                    link(dve, dve.tensor_tensor(f1[:, :], f1[:, :], inhead[:, :], ALU.mult))
                    link(dve, dve.tensor_tensor(f1[:, :], f1[:, :], key, ALU.add))
                    link(dve, dve.tensor_scalar(f2[:, :], end[:, :], -FAR, FAR, ALU.mult, ALU.add))
                    link(dve, dve.tensor_tensor(o.scatter[:, :], f1[:, :], f2[:, :], ALU.add))
                    link(dve, dve.tensor_tensor(f1[:, 0:1], first, nxt[:, T - 1, 0:1], ALU.is_equal))
                    link(dve, dve.scalar_tensor_tensor(o.head[:, :], f1[:, 0:1], FAR, first, ALU.mult, ALU.add))
                    link(dve, dve.tensor_scalar(diag[:, 0, :], ident[:, :], first, None, ALU.mult))
                    link(dve, dve.tensor_scalar(diag[:, 1, :], ident[:, :], last, None, ALU.mult))
                    marks["diag"] = chain.base
                    dve.wait_ge(pe_step.sem, pe_step.at(1))
                    link(dve, dve.scalar_tensor_tensor(o.carry[:, :], ph[:, 0, 0:P], last, lower[:, :], ALU.is_equal, ALU.mult))
                    link(dve, dve.scalar_tensor_tensor(back[:, :], ph[:, 1, 0:P], first, upper[:, :], ALU.is_equal, ALU.mult))
                    link(dve, dve.memset(V[:, C - 1, :], 1.0))
                    for r in range(C - 1):
                        link(dve, dve.tensor_scalar(V[:, r, :], rec[:, :, 2], float(r), None, ALU.is_equal))
                    link(dve, dve.tensor_copy(sameC[:, :, :], o.same[:, :].rearrange("p (a t) -> p a t", a=1).broadcast_to([P, C, T])))
                    link(dve, dve.tensor_copy(samenC[:, :, :], samen[:, :].rearrange("p (a t) -> p a t", a=1).broadcast_to([P, C, T])))
                    flat = lambda a: a[:, :, :].rearrange("p c t -> p (c t)")
                    link(dve, dve.tensor_tensor_scan(fwd[:, :], flat(sameC), flat(V), 0.0, ALU.mult, ALU.add))
                    link(dve, dve.tensor_tensor_scan(bwd[:, ::-1], flat(samenC)[:, ::-1], flat(V)[:, ::-1], 0.0, ALU.mult, ALU.add))
                    fw, bw = (a[:, :].rearrange("p (c t) -> p c t", t=T) for a in (fwd, bwd))
                    link(dve, dve.tensor_copy(runs[:, 0, :], fw[:, :, T - 1]))
                    link(dve, dve.tensor_copy(runs[:, 1, :], bw[:, :, 0]))
                    marks["runs"] = chain.base
                    link(dve, dve.tensor_tensor(fwd[:, :], fwd[:, :], bwd[:, :], ALU.add))
                    link(dve, dve.tensor_tensor(fwd[:, :], fwd[:, :], flat(V), ALU.subtract))
                    dve.wait_ge(pe_step.sem, pe_step.at(2))
                    for j, inside in ((0, inhead), (1, intail)):
                        link(dve, dve.tensor_copy(runs[:, j, :], pc[:, j, 0:C]))
                        link(dve, dve.tensor_tensor(sameC[:, :, :], inside[:, :].rearrange("p (a t) -> p a t", a=1).broadcast_to([P, C, T]),
                                                    runs[:, j, :].rearrange("p (c a) -> p c a", a=1).broadcast_to([P, C, T]), ALU.mult))
                        link(dve, dve.tensor_tensor(fwd[:, :], fwd[:, :], flat(sameC), ALU.add))
                    link(dve, dve.tensor_scalar(f1[:, :], fw[:, C - 1, :], 1.0, None, ALU.max))
                    link(dve, dve.reciprocal(o.weight[:, :], f1[:, :]))
                    if with_rel:
                        link(dve, dve.tensor_tensor(V[:, :, :], V[:, :, :], fw, ALU.mult))
                        link(dve, dve.tensor_reduce(f2[:, :], V[:, 0:RELS, :].rearrange("p c t -> p t c"), AX.X, ALU.add))
                        link(dve, dve.tensor_scalar(f2[:, :], f2[:, :], 1.0, None, ALU.max))
                        link(dve, dve.reciprocal(w_rel[:, :], f2[:, :]))
                        link(dve, dve.memset(aux[:, :, :], 0.0))
                        link(dve, dve.tensor_tensor(aux[:, :, 0], f1[:, :], end[:, :], ALU.mult))
                        link(dve, dve.tensor_copy(ed.samen[:, :], samen[:, :]))
                        link(dve, dve.tensor_copy(ed.end[:, :], end[:, :]))
                        link(dve, dve.tensor_copy(ed.inhead[:, :], inhead[:, :]))
                        link(dve, dve.tensor_copy(ed.intail[:, :], intail[:, :]))
                        link(dve, dve.tensor_copy(ed.back[:, :], back[:, :]))
                        link(dve, dve.tensor_scalar(ed.dst[:, :], key, float(N - 1), None, ALU.min))
                        link(dve, dve.tensor_copy(ed.rel[:, :], rec[:, :, 2]))

                @block.tensor
                def _(pe):
                    pe.wait_ge(chain.sem, marks["diag"])
                    pe.matmul(ph[:, 0, 0:P], ones[:, :], diag[:, 0, :], start=True, stop=True)
                    pe.matmul(ph[:, 1, 0:P], ones[:, :], diag[:, 1, :], start=True, stop=True).then_inc(pe_step.sem, 1)
                    pe.wait_ge(chain.sem, marks["runs"])
                    pe.matmul(pc[:, 0, 0:C], o.carry[:, :], runs[:, 0, :], start=True, stop=True)
                    pe.matmul(pc[:, 1, 0:C], back[:, :], runs[:, 1, :], start=True, stop=True).then_inc(pe_step.sem, 1)
                pe_step.close(2)

        prepare(ed, by_dst, "pd", True)
        prepare(es, by_src, "ps", False)

        def before_slot(c, k, i):
            q = c[(k - 2) % SLOTS]
            return q.sem, q.at(i + (k >= 2))

        def next_tile(i, k):
            return (i, k + 1) if k + 1 < SLOTS else (i + 1, 0)

        def all_tiles(eng, ahead, behind):
            ahead(0, 0)
            with eng.Fori(0, ITERS - 1) as i:
                for k in range(SLOTS):
                    ahead(*next_tile(i, k))
                    behind(i, k)
            for k in range(SLOTS):
                if k + 1 < SLOTS:
                    ahead(ITERS - 1, k + 1)
                behind(ITERS - 1, k)

        def edge_pass(name, o, table, tw, agg, aw, weight, matrix=None, bias=None, rel=None, with_aux=False):
            n_pe = 3 if matrix is not None else 1
            with ExitStack() as tmp:
                rows = sb("rows_" + name, [P, SLOTS, tw], F32, tmp)
                gidx = sb("gidx_" + name, [P, SLOTS], I32, tmp)
                sidx = sb("sidx_" + name, [P, SLOTS], I32, tmp)
                msg = sb("msg_" + name, [P, SLOTS, D], F32, tmp)
                acc = sb("acc_" + name, [P, SLOTS, aw], F32, tmp)
                headrow = sb("headrow_" + name, [P, aw], F32, tmp)
                ps = tmp.enter_context(nc.psum_tensor("ps_" + name, [P, 8, 512], F32))
                res, res_ready = acc, acc_ready
                if matrix is not None:
                    res, res_ready = sb("res_" + name, [P, SLOTS, aw], F32, tmp), row_ready
                    accT = sb("accT_" + name, [P, 2, D], F32, tmp)
                    carried = sb("carried_" + name, [P, aw], F32, tmp)
                if rel is not None:
                    prod = sb("prod_" + name, [P, 2, 1024], F32, tmp)
                turn_ps, out_ps, rel_ps = ps[:, 0:2, 0:D], ps[:, 2:4, 0:D], ps[:, 4:8, :]
                msg_used = prod_ready if rel is not None else acc_ready
                marks = {}
                block = tmp.enter_context(nc.Block())

                @block.gpsimd
                def _(pool):
                    def gather(k, n):
                        pool.wait_ge(idx_ready[k].sem, n)
                        pool.nop(nofuse=True)
                        pool.indirect_dma_start(
                            out=rows[:, k, :], out_offset=None, in_=table[:, :],
                            in_offset=bass.IndirectOffsetOnAxis(ap=gidx[:, k:k + 1], axis=0),
                            bounds_check=N - 1, oob_is_err=False).then_inc(gathered[k].sem, 16)

                    def scatter(k, n):
                        pool.wait_ge(res_ready[k].sem, n)
                        pool.nop(nofuse=True)
                        pool.indirect_dma_start(
                            out=agg[:, :], out_offset=bass.IndirectOffsetOnAxis(ap=sidx[:, k:k + 1], axis=0),
                            in_=res[:, k, :], in_offset=None,
                            bounds_check=HEAD + P - 1, oob_is_err=False).then_inc(scattered[k].sem, 16)

                    for k in range(SLOTS):
                        gather(k, idx_ready[k].at(1))
                    with pool.Fori(0, ITERS - 1) as i:
                        for k in range(SLOTS):
                            scatter(k, res_ready[k].at(i + 1))
                            gather(k, idx_ready[k].at(i + 2))
                    for k in range(SLOTS):
                        scatter(k, res_ready[k].at(ITERS))
                    pool.wait_ge(ready.sem, ready.at(1))
                    pool.indirect_dma_start(
                        out=agg[:, :], out_offset=bass.IndirectOffsetOnAxis(ap=o.head[:, 0:1], axis=0),
                        in_=headrow[:, :], in_offset=None, bounds_check=N - 1, oob_is_err=False).then_inc(stored[2].sem, 16)
                    pool.wait_ge(stored[2].sem, stored[2].at(16))

                @block.sync
                def _(sp):
                    for k in range(SLOTS):
                        sp.wait_ge(scattered[k].sem, scattered[k].at(16 * ITERS))
                    sp.dma_start(headrow[:, :], agg[HEAD:HEAD + P, :]).then_inc(load[0].sem, 16)

                @block.scalar
                def _(act):
                    for k in range(SLOTS):
                        act.copy(gidx[:, k:k + 1], o.gather[:, k:k + 1]).then_inc(idx_ready[k].sem, 1)

                    def weigh(i, k, more=True):
                        act.wait_ge(gathered[k].sem, gathered[k].at(i * 16 + 16))
                        act.wait_ge(msg_used[k].sem, msg_used[k].at(i))
                        w = rows[:, k, D:D + 1] if weight is None else weight[:, bass.ds(i * SLOTS + k, 1)]
                        act.activation(msg[:, k, :], rows[:, k, 0:D], ACT.Copy, scale=w).then_inc(msg_ready[k].sem, 1)
                        if more:
                            act.wait_ge(msg_ready[k].sem, msg_ready[k].at(i + 1))
                            act.copy(gidx[:, k:k + 1], o.gather[:, bass.ds(i * SLOTS + SLOTS + k, 1)]).then_inc(idx_ready[k].sem, 1)

                    def turn_out(i, k):
                        act.wait_ge(turned[k].sem, turned[k].at(i + 1))
                        act.wait_ge(*before_slot(product, k, i))
                        act.copy(accT[:, k % 2, :], turn_ps[:, k % 2, :]).then_inc(turned_sb[k].sem, 1)

                    if matrix is None:
                        with act.Fori(0, ITERS - 1) as i:
                            for k in range(SLOTS):
                                weigh(i, k)
                        for k in range(SLOTS):
                            weigh(ITERS - 1, k, more=False)
                    else:
                        weigh(0, 0)
                        with act.Fori(0, ITERS - 2) as i:
                            for k in range(SLOTS):
                                weigh(*next_tile(i, k))
                                turn_out(i, k)
                        for i in (ITERS - 2, ITERS - 1):
                            for k in range(SLOTS):
                                if (i, k) != (ITERS - 1, SLOTS - 1):
                                    j, m = next_tile(i, k)
                                    weigh(j, m, more=j < ITERS - 1)
                                turn_out(i, k)
                        act.wait_ge(pe_step.sem, pe_step.at(2))
                        act.copy(accT[:, 0, :], turn_ps[:, 0, :]).then_inc(act_step.sem, 1)

                @block.vector
                def _(dve):
                    link(dve, dve.memset(acc[:, :, :], 0.0))

                    def multiply(i, k):
                        dve.wait_ge(relw_ready[k].sem, relw_ready[k].at(i + 1))
                        dve.wait_ge(*before_slot(product, k, i))
                        dve.wait_ge(msg_ready[k].sem, msg_ready[k].at(i + 1))
                        for h in range(2):
                            ins = dve.tensor_tensor(
                                prod[:, k % 2, h * 512:(h + 1) * 512].rearrange("p (i b o) -> p i b o", i=2, o=4),
                                rel_ps[:, 2 * (k % 2) + h, :].rearrange("p (i b o) -> p i b o", i=2, o=4),
                                msg[:, k, :].rearrange("p (b i a) -> p i b a", i=4, a=1)[:, 2 * h:2 * h + 2].broadcast_to([P, 2, D // 4, 4]),
                                ALU.mult)
                        ins.then_inc(prod_ready[k].sem, 1)

                    def add(i, k):
                        t = bass.ds(i * SLOTS + k, 1)
                        last = acc_ready[(k - 1) % SLOTS]
                        if matrix is not None:
                            dve.wait_ge(turned[k].sem, turned[k].at(i))
                        if res is acc:
                            dve.wait_ge(scattered[k].sem, scattered[k].at(i * 16))
                            dve.tensor_copy(sidx[:, k:k + 1], o.scatter[:, t])
                        if rel is not None:
                            dve.wait_ge(product[k].sem, product[k].at(i + 1))
                        else:
                            dve.wait_ge(msg_ready[k].sem, msg_ready[k].at(i + 1))
                        dve.wait_ge(last.sem, last.at(i + (k > 0)))
                        new = out_ps[:, k % 2, :] if rel is not None else msg[:, k, :]
                        ins = dve.scalar_tensor_tensor(acc[:, k, 0:D], acc[:, (k - 1) % SLOTS, 0:D], o.same[:, t], new, ALU.mult, ALU.add)
                        if with_aux:
                            ins = dve.scalar_tensor_tensor(acc[:, k, D:aw], acc[:, (k - 1) % SLOTS, D:aw], o.same[:, t],
                                                           aux[:, t, :].rearrange("p a f -> p (a f)"), ALU.mult, ALU.add)
                        ins.then_inc(acc_ready[k].sem, 1)

                    def finish(i, k):
                        dve.wait_ge(scattered[k].sem, scattered[k].at(i * 16))
                        dve.tensor_copy(sidx[:, k:k + 1], o.scatter[:, bass.ds(i * SLOTS + k, 1)])
                        dve.wait_ge(product[k].sem, product[k].at(i + 1))
                        if with_aux:
                            dve.tensor_copy(res[:, k, D:aw], acc[:, k, D:aw])
                        if bias is not None:
                            ins = dve.tensor_tensor(res[:, k, 0:D], out_ps[:, k % 2, :], bias[:, :], ALU.add)
                        else:
                            ins = dve.tensor_copy(res[:, k, 0:D], out_ps[:, k % 2, :])
                        ins.then_inc(row_ready[k].sem, 1)

                    if matrix is not None:
                        all_tiles(dve, add, finish)
                    elif rel is not None:
                        all_tiles(dve, multiply, add)
                    else:
                        with dve.Fori(0, ITERS) as i:
                            for k in range(SLOTS):
                                add(i, k)
                    dve.wait_ge(load[0].sem, load[0].at(16))
                    dve.wait_ge(pe_step.sem, pe_step.at(1))
                    if matrix is not None:
                        link(dve, dve.tensor_copy(carried[:, :], ps[:, 2, 0:aw]))
                        marks["carried"] = chain.base
                        dve.wait_ge(pe_step.sem, pe_step.at(3))
                        link(dve, dve.tensor_tensor(headrow[:, 0:D], headrow[:, 0:D], ps[:, 3, 0:D], ALU.add))
                        if with_aux:
                            link(dve, dve.tensor_tensor(headrow[:, D:aw], headrow[:, D:aw], carried[:, D:aw], ALU.add))
                    else:
                        link(dve, dve.tensor_tensor(headrow[:, :], headrow[:, :], ps[:, 2, 0:aw], ALU.add))
                    dve.sem_inc(ready.sem, 1)

                @block.tensor
                def _(pe):
                    def turn(i, k):
                        pe.wait_ge(*before_slot(turned_sb, k, i))
                        pe.wait_ge(acc_ready[k].sem, acc_ready[k].at(i + 1))
                        for c in range(C2):
                            ins = pe.transpose(turn_ps[:, k % 2, c * P:(c + 1) * P], acc[:, k, c * P:(c + 1) * P], ident[:, :])
                        ins.then_inc(turned[k].sem, 1)

                    def multiply(i, k):
                        pe.wait_ge(*before_slot(row_ready, k, i))
                        pe.wait_ge(turned_sb[k].sem, turned_sb[k].at(i + 1))
                        for c in range(C2):
                            ins = pe.matmul(out_ps[:, k % 2, :], accT[:, k % 2, c * P:(c + 1) * P], matrix[:, c, :],
                                            start=(c == 0), stop=(c == C2 - 1))
                        ins.then_inc(product[k].sem, 1)

                    def spread(i, k):
                        pe.wait_ge(*before_slot(prod_ready, k, i))
                        for h in range(2):
                            ins = pe.matmul(rel_ps[:, 2 * (k % 2) + h, :], rel_hot[:, bass.ds((i * SLOTS + k) * P, P)],
                                            rel[:, h * 512:(h + 1) * 512], start=True, stop=True)
                        ins.then_inc(relw_ready[k].sem, 1)

                    def block_sum(i, k):
                        pe.wait_ge(*before_slot(acc_ready, k, i))
                        pe.wait_ge(prod_ready[k].sem, prod_ready[k].at(i + 1))
                        for j in range(4):
                            ins = pe.matmul(out_ps[:, k % 2, :], ident[:, :], prod[:, k % 2, j * D:(j + 1) * D], start=(j == 0), stop=(j == 3))
                        ins.then_inc(product[k].sem, 1)

                    if matrix is not None:
                        all_tiles(pe, turn, multiply)
                    elif rel is not None:
                        all_tiles(pe, spread, block_sum)
                    pe.wait_ge(acc_ready[SLOTS - 1].sem, acc_ready[SLOTS - 1].at(ITERS))
                    if matrix is not None:
                        pe.wait_ge(row_ready[SLOTS - 2].sem, row_ready[SLOTS - 2].at(ITERS))
                    pe.matmul(ps[:, 2, 0:aw], o.carry[:, :], acc[:, SLOTS - 1, :], start=True, stop=True).then_inc(pe_step.sem, 1)
                    if matrix is not None:
                        pe.wait_ge(turned_sb[SLOTS - 2].sem, turned_sb[SLOTS - 2].at(ITERS))
                        pe.wait_ge(chain.sem, marks["carried"])
                        for c in range(C2):
                            ins = pe.transpose(ps[:, 0, c * P:(c + 1) * P], carried[:, c * P:(c + 1) * P], ident[:, :])
                        ins.then_inc(pe_step.sem, 1)
                        pe.wait_ge(row_ready[SLOTS - 1].sem, row_ready[SLOTS - 1].at(ITERS))
                        pe.wait_ge(act_step.sem, act_step.at(1))
                        for c in range(C2):
                            ins = pe.matmul(ps[:, 3, 0:D], accT[:, 0, c * P:(c + 1) * P], matrix[:, c, :], start=(c == 0), stop=(c == C2 - 1))
                        ins.then_inc(pe_step.sem, 1)

                for k in range(SLOTS):
                    for c in (idx_ready, acc_ready, msg_ready):
                        c[k].close(ITERS)
                    gathered[k].close(16 * ITERS)
                    scattered[k].close(16 * ITERS)
                    if matrix is not None:
                        for c in (turned, turned_sb, product, row_ready):
                            c[k].close(ITERS)
                    if rel is not None:
                        for c in (relw_ready, prod_ready, product):
                            c[k].close(ITERS)
                stored[2].close(16)
                load[0].close(16)
                ready.close(1)
                pe_step.close(n_pe)
                if matrix is not None:
                    act_step.close(1)

        def node_pass(name, ins, outs, kind, matrix=None, bias=None):
            ninp = len(ins)
            n_store = 2 if kind == "gcn" else 1
            after_norm = kind in ("sage", "rgcn2", "conv", "gat")
            with ExitStack() as tmp:
                inp = [[sb(f"in{j}{s}_{name}", [P, R, w], F32, tmp) for j, (_, w) in enumerate(ins)] for s in range(2)]
                outb = [sb(f"out{s}_{name}", [P, R, outs[0][1]], F32, tmp) for s in range(2)]
                pre = [sb(f"pre{s}_{name}", [P, R, D], F32, tmp) for s in range(2)] if kind in ("gcn", "gat") else None
                u = [sb(f"u{s}_{name}", [P, R, D], F32, tmp) for s in range(2)]
                stats = sb(f"stats_{name}", [P, 2, R, 6], F32, tmp)
                mv = sb(f"mv_{name}", [P, 2, R, 2], F32, tmp)
                scale = sb(f"scale_{name}", [P, 2, R, 2], F32, tmp)
                attb = sb(f"attb_{name}", [P, 2, R, 2], F32, tmp)
                own = sb(f"own_{name}", [P, 2, R], F32, tmp)
                dev = sb(f"dev_{name}", [P, 2, R], F32, tmp)
                junk = sb(f"junk_{name}", [P, 2, R, 2, D], BF16, tmp) if kind == "gcn" else None
                xT = sb(f"xT_{name}", [P, PAIRS, 512], F32, tmp)
                ps = tmp.enter_context(nc.psum_tensor("ps_" + name, [P, 8, 512], F32))
                turn_ps, out_ps = ps[:, 0:PAIRS, :], ps[:, PAIRS:2 * PAIRS, :]
                eps = eps_col[:, 0:1] if kind == "sage" else eps_col[:, 1:2]
                block = tmp.enter_context(nc.Block())

                def view(a, n, pp, r):
                    if pp == P:
                        return a[0:NBATCH * BATCH, :].rearrange("(n p r) d -> n p (r d)", p=P, r=R)[n]
                    return a[NBATCH * BATCH:N, :]

                def batches(eng, body):
                    with eng.Fori(0, LOOPS) as i:
                        for s in range(2):
                            body(i, s, i * 2 + s, P, R)
                    if PEEL:
                        body(LOOPS, 0, NBATCH - 1, P, R)
                    body(LOOPS, 1 if PEEL else 0, NBATCH, REST, 1)

                total = [LOOPS + PEEL + (0 if PEEL else 1), LOOPS + (1 if PEEL else 0)]
                assert PEEL

                @block.sync
                def _(sp):
                    def body(i, s, n, pp, r):
                        sp.wait_ge(batch_done[s].sem, batch_done[s].at(i))
                        sp.nop(nofuse=True)
                        for j, (a, w) in enumerate(ins):
                            sp.dma_start(inp[s][j][0:pp, 0:r, :].rearrange("p r d -> p (r d)"), view(a, n, pp, r)).then_inc(load[s].sem, 16)
                    batches(sp, body)

                @block.gpsimd
                def _(pool):
                    def body(i, s, n, pp, r):
                        pool.wait_ge(batch_out[s].sem, batch_out[s].at(i + 1))
                        pool.nop(nofuse=True)
                        pool.dma_start(view(outs[0][0], n, pp, r), outb[s][0:pp, 0:r, :].rearrange("p r d -> p (r d)")).then_inc(stored[s].sem, 16)
                        if kind == "gcn":
                            pool.dma_start(view(att, n, pp, r), attb[0:pp, s, 0:r, :].rearrange("p r d -> p (r d)")).then_inc(stored[s].sem, 16)
                    batches(pool, body)
                    for s in range(2):
                        pool.wait_ge(stored[s].sem, stored[s].at(16 * n_store * total[s]))

                def pairs(r):
                    return [(g, min(2, r - 2 * g)) for g in range(-(-r // 2))]

                if matrix is not None:
                    @block.tensor
                    def _(pe):
                        def body(i, s, n, pp, r):
                            if pre is None:
                                pe.wait_ge(load[s].sem, load[s].at((i + 1) * (16 * ninp)))
                            src = inp[s][1] if pre is None else pre[s]
                            for g, m in pairs(r):
                                if pre is not None:
                                    pe.wait_ge(pre_ready[g].sem, pre_ready[g].at(n + 1))
                                pe.wait_ge(turned_sb[g].sem, turned_sb[g].at(n))
                                for q in range(m):
                                    for c in range(C2):
                                        z = (2 * q + c) * P
                                        ins_ = pe.transpose(turn_ps[:, g, z:z + pp], src[0:pp, 2 * g + q, c * P:(c + 1) * P], ident[0:pp, 0:pp])
                                ins_.then_inc(turned[g].sem, 1)
                            for g, m in pairs(r):
                                pe.wait_ge(row_ready[g].sem, row_ready[g].at(n))
                                pe.wait_ge(turned_sb[g].sem, turned_sb[g].at(n + 1))
                                for q in range(m):
                                    if bias is not None:
                                        pe.matmul(out_ps[0:pp, g, q * D:(q + 1) * D], onesb[0:3, 0:pp], bias[:, :], start=True, stop=False)
                                    for c in range(C2):
                                        z = (2 * q + c) * P
                                        ins_ = pe.matmul(out_ps[0:pp, g, q * D:(q + 1) * D], xT[:, g, z:z + pp], matrix[:, c, :],
                                                         start=(bias is None and c == 0), stop=(c == C2 - 1))
                                ins_.then_inc(product[g].sem, 1)
                        batches(pe, body)

                @block.scalar
                def _(act):
                    def body(i, s, n, pp, r):
                        if matrix is not None:
                            for g, m in pairs(r):
                                act.wait_ge(turned[g].sem, turned[g].at(n + 1))
                                act.wait_ge(product[g].sem, product[g].at(n))
                                if pp == P:
                                    ins_ = act.copy(xT[:, g, 0:m * D], turn_ps[:, g, 0:m * D])
                                else:
                                    ins_ = act.copy(xT[:, g, 0:m * D].rearrange("p (z q) -> p z q", q=P)[:, :, 0:pp],
                                                    turn_ps[:, g, 0:m * D].rearrange("p (z q) -> p z q", q=P)[:, :, 0:pp])
                                ins_.then_inc(turned_sb[g].sem, 1)
                        if after_norm:
                            act.wait_ge(relw_ready[1].sem, relw_ready[1].at(n + 1))
                            act.activation(dev[0:pp, s, 0:r], mv[0:pp, s, 0:r, 1], ACT.Sqrt, bias=eps[0:pp, :]).then_inc(deviation.sem, 1)
                        act.wait_ge(stored[s].sem, stored[s].at(i * (16 * n_store)))
                        act.wait_ge(acc_ready[s].sem, acc_ready[s].at(i + 1))
                        if after_norm:
                            for q in range(r):
                                ins_ = act.activation(outb[s][0:pp, q, 0:D], u[s][0:pp, q, :], ACT.Identity,
                                                      bias=scale[0:pp, s, q, 1:2], scale=scale[0:pp, s, q, 0:1])
                        else:
                            ins_ = act.activation(outb[s][0:pp, 0:r, :], u[s][0:pp, 0:r, :], ACT.Relu)
                        ins_.then_inc(batch_out[s].sem, 1)
                    batches(act, body)
                    if kind == "sage":
                        act.wait_ge(acc_ready[1].sem, acc_ready[1].at(total[1]))
                        act.activation(cnt_nodes[:, :], cnt_nodes[:, :], ACT.Sqrt, bias=ones[:, 0:1]).then_inc(act_step.sem, 1)
                        act_step.close(1)

                @block.vector
                def _(dve):
                    def body(i, s, n, pp, r):
                        ag, us = inp[s][0], u[s]
                        dve.wait_ge(load[s].sem, load[s].at((i + 1) * (16 * ninp)))
                        dve.wait_ge(batch_out[s].sem, batch_out[s].at(i))
                        if kind in ("gcn", "conv"):
                            dve.wait_ge(stored[s].sem, stored[s].at(i * (16 * n_store)))
                        if kind == "gat":
                            dve.tensor_scalar(own[0:pp, s, 0:r], ag[0:pp, 0:r, D + 1], -1.0, 1.0, ALU.mult, ALU.add).then_inc(own_step.sem, 1)
                            dve.wait_ge(own_step.sem, own_step.at(n * 2 + 1))
                            dve.tensor_tensor(own[0:pp, s, 0:r], own[0:pp, s, 0:r], ag[0:pp, 0:r, D], ALU.add).then_inc(own_step.sem, 1)
                            dve.wait_ge(own_step.sem, own_step.at(n * 2 + 2))
                        if kind == "sage":
                            dve.tensor_copy(cnt_nodes[0:pp, bass.ds(n * R, r)], ag[0:pp, 0:r, D])
                        if kind in ("gcn", "gat"):
                            for g, m in pairs(r):
                                for q in range(2 * g, 2 * g + m):
                                    w = dinv[0:pp, bass.ds(n * R + q, 1)] if kind == "gcn" else own[0:pp, s, q:q + 1]
                                    ins_ = dve.scalar_tensor_tensor(pre[s][0:pp, q, :], inp[s][1][0:pp, q, 0:D], w, ag[0:pp, q, 0:D], ALU.mult, ALU.add)
                                ins_.then_inc(pre_ready[g].sem, 1)
                        for g, m in pairs(r):
                            a, b = 2 * g, 2 * g + m
                            o_ps = out_ps[0:pp, g, 0:m * D].rearrange("p (r d) -> p r d", d=D)
                            if matrix is not None:
                                dve.wait_ge(product[g].sem, product[g].at(n + 1))
                            if kind == "sage":
                                dve.tensor_tensor(us[0:pp, a:b, :], o_ps, ag[0:pp, a:b, 0:D], ALU.add).then_inc(row_ready[g].sem, 1)
                                dve.wait_ge(row_ready[g].sem, row_ready[g].at(n + 1))
                                ins_ = dve.scalar_tensor_tensor(us[0:pp, a:b, :], us[0:pp, a:b, :], 0.0, inp[s][1][0:pp, a:b, 0:D], ALU.max, ALU.add)
                            elif kind == "rgcn1":
                                ins_ = dve.tensor_tensor(us[0:pp, a:b, :], o_ps, ag[0:pp, a:b, 0:D], ALU.add)
                                ins_.then_inc(row_ready[g].sem, 1)
                                continue
                            elif kind == "rgcn2":
                                dve.tensor_tensor(us[0:pp, a:b, :], o_ps, ag[0:pp, a:b, 0:D], ALU.add).then_inc(row_ready[g].sem, 1)
                                dve.wait_ge(row_ready[g].sem, row_ready[g].at(n + 1))
                                ins_ = dve.tensor_tensor(us[0:pp, a:b, :], us[0:pp, a:b, :], inp[s][2][0:pp, a:b, 0:D], ALU.add)
                            elif kind == "conv":
                                ins_ = dve.tensor_tensor(us[0:pp, a:b, :], inp[s][1][0:pp, a:b, 0:D], ag[0:pp, a:b, 0:D], ALU.add)
                            elif kind == "gcn":
                                for q in range(a, b):
                                    ins_ = dve.scalar_tensor_tensor(us[0:pp, q, :], o_ps[:, q - a, :], dinv[0:pp, bass.ds(n * R + q, 1)],
                                                                    b_g1[0:pp, :], ALU.mult, ALU.add)
                                ins_.then_inc(row_ready[g].sem, 1)
                                dve.wait_ge(row_ready[g].sem, row_ready[g].at(n + 1))
                                for q in range(a, b):
                                    for j, v in ((0, va), (1, vb)):
                                        ins_ = dve.scalar_tensor_tensor(junk[0:pp, s, q, j, :], us[0:pp, q, :], 0.0, v[0:pp, :], ALU.max, ALU.mult,
                                                                        accum_out=attb[0:pp, s, q, j:j + 1])
                                continue
                            elif kind == "gat":
                                ins_ = dve.scalar_tensor_tensor(us[0:pp, a:b, :], o_ps, 0.0, inp[s][2][0:pp, a:b, 0:D], ALU.max, ALU.add)
                                ins_.then_inc(row_ready[g].sem, 1)
                            ins_.then_inc(msg_ready[g].sem, 1) if kind != "gat" else None
                            c = msg_ready[g] if kind != "gat" else row_ready[g]
                            dve.wait_ge(c.sem, c.at(n + 1))
                            for q in range(a, b):
                                ins_ = dve.bn_stats(stats[0:pp, s, q, :], us[0:pp, q, :])
                            if b == r:
                                ins_.then_inc(relw_ready[0].sem, 1)
                        if after_norm:
                            dve.wait_ge(relw_ready[0].sem, relw_ready[0].at(n + 1))
                            dve.nop(nofuse=True)
                            for q in range(r):
                                ins_ = dve.bn_aggr(mv[0:pp, s, q, :], stats[0:pp, s, q, :])
                            ins_.then_inc(relw_ready[1].sem, 1)
                            dve.wait_ge(relw_ready[1].sem, relw_ready[1].at(n + 1))
                            dve.wait_ge(deviation.sem, deviation.at(n + 1))
                            dve.nop(nofuse=True)
                            dve.reciprocal(scale[0:pp, s, 0:r, 0], dev[0:pp, s, 0:r]).then_inc(relw_ready[2].sem, 1)
                            dve.wait_ge(relw_ready[2].sem, relw_ready[2].at(n + 1))
                            if kind == "conv":
                                dve.tensor_copy(outb[s][0:pp, 0:r, D], dinv[0:pp, bass.ds(n * R, r)])
                            ins_ = dve.scalar_tensor_tensor(scale[0:pp, s, 0:r, 1], mv[0:pp, s, 0:r, 0], -1.0, scale[0:pp, s, 0:r, 0], ALU.mult, ALU.mult)
                        if kind == "rgcn1":
                            last = row_ready[pairs(r)[-1][0]]
                            dve.wait_ge(last.sem, last.at(n + 1))
                            dve.sem_inc(acc_ready[s].sem, 1)
                        else:
                            ins_.then_inc(acc_ready[s].sem, 1)
                        dve.wait_ge(acc_ready[s].sem, acc_ready[s].at(i + 1))
                        dve.sem_inc(batch_done[s].sem, 1)
                    if kind == "sage":
                        link(dve, dve.memset(cnt_nodes[:, :], 0.0))
                    if kind == "conv":
                        dve.memset(outb[0][:, :, D:DW], 0.0)
                        link(dve, dve.memset(outb[1][:, :, D:DW], 0.0))
                    batches(dve, body)
                    if kind == "sage":
                        dve.wait_ge(act_step.sem, act_step.base)
                        link(dve, dve.reciprocal(dinv[:, :], cnt_nodes[:, :]))

                for s in range(2):
                    load[s].close(16 * ninp * total[s])
                    stored[s].close(16 * n_store * total[s])
                    batch_done[s].close(total[s]); batch_out[s].close(total[s]); acc_ready[s].close(total[s])
                raise_to = NBATCH + 1
                for g in range(PAIRS):
                    n_g = raise_to if g == 0 else NBATCH
                    if matrix is not None:
                        for c in (turned, turned_sb, product, row_ready):
                            c[g].close(n_g)
                    if pre is not None:
                        pre_ready[g].close(n_g)
                    if kind in ("sage", "rgcn2", "conv"):
                        msg_ready[g].close(n_g)
                if after_norm:
                    deviation.close(raise_to)
                    for j in range(3):
                        relw_ready[j].close(raise_to)
                if kind == "gat":
                    own_step.close(2 * raise_to)

        def one_hot_relations():
            with ExitStack() as tmp:
                hot = sb("hot_rel", [P, SLOTS, 96], BF16, tmp)
                ps = tmp.enter_context(nc.psum_tensor("ps_rel", [P, SLOTS, 1024], BF16))
                block = tmp.enter_context(nc.Block())

                @block.vector
                def _(dve):
                    with dve.Fori(0, ITERS) as i:
                        for k in range(SLOTS):
                            dve.wait_ge(turned[k].sem, turned[k].at(i))
                            dve.tensor_scalar(hot[:, k, :], rel_iota[:, :], ed.rel[:, bass.ds(i * SLOTS + k, 1)], None, ALU.is_equal).then_inc(msg_ready[k].sem, 1)

                @block.tensor
                def _(pe):
                    with pe.Fori(0, ITERS) as i:
                        for k in range(SLOTS):
                            pe.wait_ge(turned_sb[k].sem, turned_sb[k].at(i))
                            pe.wait_ge(msg_ready[k].sem, msg_ready[k].at(i + 1))
                            pe.transpose(ps[0:96, k, 0:P], hot[:, k, :], identb[:, :]).then_inc(turned[k].sem, 1)

                @block.scalar
                def _(act):
                    with act.Fori(0, ITERS) as i:
                        for k in range(SLOTS):
                            act.wait_ge(turned[k].sem, turned[k].at(i + 1))
                            act.copy(rel_hot[:, bass.ds((i * SLOTS + k) * P, P)], ps[0:96, k, 0:P]).then_inc(turned_sb[k].sem, 1)
                for k in range(SLOTS):
                    for c in (turned, turned_sb, msg_ready):
                        c[k].close(ITERS)

        def attention():
            BIG = 1e30
            with ExitStack() as tmp:
                rowa = sb("rowa", [P, SLOTS, 2, 2], F32, tmp)
                gidx = sb("gidx_att", [P, SLOTS, 2], I32, tmp)
                score = sb("score", [P, 2, T, 2], F32, tmp)
                e, es_, m, f, b, t1, pen, penn = (sb("att_" + n, [P, T], F32, tmp) for n in ("e", "es", "m", "f", "b", "t1", "pen", "penn"))
                diag = sb("att_diag", [P, 2, P], F32, tmp)
                col = sb("att_c", [P, 4], F32, tmp)
                msk = sb("att_msk", [P, P], F32, tmp)
                ps = tmp.enter_context(nc.psum_tensor("ps_att", [P, 4, 512], F32))
                marks = {}
                block = tmp.enter_context(nc.Block())

                @block.gpsimd
                def _(pool):
                    with pool.Fori(0, ITERS) as i:
                        for k in range(SLOTS):
                            pool.wait_ge(idx_ready[k].sem, idx_ready[k].at(i + 1))
                            pool.nop(nofuse=True)
                            for j in range(2):
                                pool.indirect_dma_start(
                                    out=rowa[:, k, j, :], out_offset=None, in_=att[:, :],
                                    in_offset=bass.IndirectOffsetOnAxis(ap=gidx[:, k, j:j + 1], axis=0),
                                    bounds_check=N - 1, oob_is_err=False).then_inc(gathered[k].sem, 16)

                @block.vector
                def _(dve):
                    for k in range(SLOTS):
                        dve.tensor_copy(gidx[:, k, 0:1], ed.gather[:, k:k + 1])
                        dve.tensor_copy(gidx[:, k, 1:2], ed.dst[:, k:k + 1]).then_inc(idx_ready[k].sem, 1)

                    def tile(i, k, more=True):
                        dve.wait_ge(gathered[k].sem, gathered[k].at(i * 32 + 32))
                        for j in range(2):
                            ins = dve.tensor_copy(score[:, j, bass.ds(i * SLOTS + k, 1), :].rearrange("p a f -> p (a f)"), rowa[:, k, j, :])
                        if more:
                            dve.tensor_copy(gidx[:, k, 0:1], ed.gather[:, bass.ds(i * SLOTS + SLOTS + k, 1)])
                            ins = dve.tensor_copy(gidx[:, k, 1:2], ed.dst[:, bass.ds(i * SLOTS + SLOTS + k, 1)])
                            ins.then_inc(idx_ready[k].sem, 1)
                    with dve.Fori(0, ITERS - 1) as i:
                        for k in range(SLOTS):
                            tile(i, k)
                    for k in range(SLOTS):
                        tile(ITERS - 1, k, more=False)
                    link(dve, dve.tensor_copy(col[:, :], part[:, :].broadcast_to([P, 4])))
                    for o_, j in ((e, 0), (es_, 1)):
                        link(dve, dve.tensor_tensor(t1[:, :], score[:, j, :, 0], score[:, 1, :, 1], ALU.add))
                        link(dve, dve.scalar_tensor_tensor(o_[:, :], t1[:, :], 0.2, t1[:, :], ALU.mult, ALU.max))
                    link(dve, dve.tensor_scalar(pen[:, :], ed.same[:, :], -1.0, BIG, ALU.add, ALU.mult))
                    link(dve, dve.tensor_scalar(penn[:, :], ed.samen[:, :], -1.0, BIG, ALU.add, ALU.mult))
                    link(dve, dve.tensor_tensor_scan(f[:, :], pen[:, :], e[:, :], -BIG, ALU.add, ALU.max))
                    link(dve, dve.tensor_tensor_scan(b[:, ::-1], penn[:, ::-1], e[:, ::-1], -BIG, ALU.add, ALU.max))
                    link(dve, dve.tensor_scalar(diag[:, 0, :], ident[:, :], f[:, T - 1:T], None, ALU.mult))
                    link(dve, dve.tensor_scalar(diag[:, 1, :], ident[:, :], b[:, 0:1], None, ALU.mult))
                    marks["diag"] = chain.base
                    link(dve, dve.tensor_tensor(m[:, :], f[:, :], b[:, :], ALU.max))
                    link(dve, dve.tensor_tensor(m[:, :], m[:, :], es_[:, :], ALU.max))
                    dve.wait_ge(pe_step.sem, pe_step.at(1))
                    for j, (mask, inside) in enumerate(((ed.back, ed.inhead), (ed.carry, ed.intail))):
                        link(dve, dve.tensor_scalar(msk[:, :], mask[:, :], -1.0, BIG, ALU.add, ALU.mult))
                        link(dve, dve.tensor_tensor(msk[:, :], msk[:, :], ps[:, j, 0:P], ALU.add))
                        link(dve, dve.tensor_reduce(col[:, j:j + 1], msk[:, :], AX.X, ALU.max))
                        link(dve, dve.tensor_scalar(t1[:, :], inside[:, :], -1.0, BIG, ALU.add, ALU.mult))
                        link(dve, dve.scalar_tensor_tensor(m[:, :], t1[:, :], col[:, j:j + 1], m[:, :], ALU.add, ALU.max))
                    link(dve, dve.tensor_tensor(e[:, :], e[:, :], m[:, :], ALU.subtract))
                    link(dve, dve.tensor_tensor(es_[:, :], es_[:, :], m[:, :], ALU.subtract))
                    marks["sub"] = chain.base
                    dve.wait_ge(act_step.sem, act_step.at(2))
                    link(dve, dve.tensor_tensor_scan(f[:, :], ed.same[:, :], e[:, :], 0.0, ALU.mult, ALU.add))
                    link(dve, dve.tensor_tensor_scan(b[:, ::-1], ed.samen[:, ::-1], e[:, ::-1], 0.0, ALU.mult, ALU.add))
                    marks["sums"] = chain.base
                    link(dve, dve.tensor_tensor(m[:, :], b[:, :], e[:, :], ALU.subtract))
                    link(dve, dve.tensor_tensor(m[:, :], m[:, :], f[:, :], ALU.add))
                    link(dve, dve.tensor_tensor(m[:, :], m[:, :], es_[:, :], ALU.add))
                    dve.wait_ge(pe_step.sem, pe_step.at(2))
                    link(dve, dve.tensor_copy(col[:, 2:4], ps[:, 2, 0:2]))
                    link(dve, dve.scalar_tensor_tensor(m[:, :], ed.inhead[:, :], col[:, 2:3], m[:, :], ALU.mult, ALU.add))
                    link(dve, dve.scalar_tensor_tensor(m[:, :], ed.intail[:, :], col[:, 3:4], m[:, :], ALU.mult, ALU.add))
                    link(dve, dve.tensor_scalar(m[:, :], m[:, :], 1e-16, None, ALU.add))
                    link(dve, dve.reciprocal(t1[:, :], m[:, :]))
                    link(dve, dve.tensor_tensor(w_rel[:, :], e[:, :], t1[:, :], ALU.mult))
                    link(dve, dve.tensor_tensor(t1[:, :], es_[:, :], t1[:, :], ALU.mult))
                    link(dve, dve.tensor_tensor(aux[:, :, 0], t1[:, :], ed.end[:, :], ALU.mult))
                    link(dve, dve.tensor_copy(aux[:, :, 1], ed.end[:, :]))

                @block.scalar
                def _(act):
                    act.wait_ge(chain.sem, marks["sub"])
                    act.activation(e[:, :], e[:, :], ACT.Exp).then_inc(act_step.sem, 1)
                    act.activation(es_[:, :], es_[:, :], ACT.Exp).then_inc(act_step.sem, 1)

                @block.tensor
                def _(pe):
                    pe.wait_ge(chain.sem, marks["diag"])
                    for j in range(2):
                        ins = pe.matmul(ps[:, j, 0:P], ones[:, :], diag[:, j, :], start=True, stop=True)
                    ins.then_inc(pe_step.sem, 1)
                    pe.wait_ge(chain.sem, marks["sums"])
                    pe.matmul(ps[:, 2, 0:1], ed.carry[:, :], f[:, T - 1:T], start=True, stop=True, skip_group_check=True)
                    pe.matmul(ps[:, 2, 1:2], ed.back[:, :], b[:, 0:1], start=True, stop=True, skip_group_check=True).then_inc(pe_step.sem, 1)
                for k in range(SLOTS):
                    idx_ready[k].close(ITERS)
                    gathered[k].close(32 * ITERS)
                pe_step.close(2)
                act_step.close(2)

        one_hot_relations()
        edge_pass("e0", ed, x_in, D, agg_d, DW, ed.weight, matrix=mats["wl"], with_aux=True)
        node_pass("n0", ((agg_d, DW), (x_in, D)), ((x1, D),), "sage", matrix=mats["wr"], bias=bias3["bl"])
        edge_pass("e1", ed, x1, D, agg_d, DW, w_rel, rel=rel_w[0])
        node_pass("n1", ((agg_d, DW), (x1, D)), ((y1, D),), "rgcn1", matrix=mats["root1"], bias=bias3["bias1"])
        edge_pass("e2", ed, y1, D, agg_d, DW, w_rel, rel=rel_w[1])
        node_pass("n2", ((agg_d, DW), (y1, D), (x1, D)), ((x2, D),), "rgcn2", matrix=mats["root2"], bias=bias3["bias2"])
        edge_pass("e3", es, x2, D, agg_s, D, es.weight, matrix=mats["l2"], bias=b_l2)
        node_pass("n3", ((agg_s, D), (x2, D)), ((x3, DW),), "conv")
        edge_pass("e4", ed, x3, DW, agg_d, DW, None)
        node_pass("n4", ((agg_d, DW), (x3, DW)), ((y3, D),), "gcn", matrix=mats["g1"])
        attention()
        edge_pass("e5", ed, y3, D, agg_d, DW, w_rel, with_aux=True)
        node_pass("n5", ((agg_d, DW), (y3, D), (x3, DW)), ((out, D),), "gat", matrix=mats["g2"], bias=bias3["b2"])


_INS = ["x", "src", "dst", "edge_type_16", "L0_gnn_W_l", "L0_gnn_b_l", "L0_gnn_W_r", "L1_gnn_W1", "L1_gnn_root1",
        "L1_gnn_bias1", "L1_gnn_W2", "L1_gnn_root2", "L1_gnn_bias2", "L2_gnn_W", "L2_gnn_b", "L3_gnn_W1",
        "L3_gnn_b1", "L3_gnn_W2", "L3_gnn_att_src", "L3_gnn_att_dst", "L3_gnn_b2"]


def kernel(**inputs):
    import numpy as _np
    import concourse.bacc as _bacc
    from concourse import mybir as _mybir
    from concourse.bass_utils import run_bass_kernel_spmd as _run

    nc = _bacc.Bacc("TRN2", target_bir_lowering=False, num_devices=1)
    arrays, aps = {}, {}
    for name in _INS:
        a = _np.ascontiguousarray(inputs[name])
        arrays[f"in_{name}_dram"] = a
        aps[name] = nc.dram_tensor(f"in_{name}_dram", a.shape, _mybir.dt.from_np(a.dtype), kind="ExternalInput").ap()
    out = nc.dram_tensor("out_0_dram", inputs["x"].shape, _mybir.dt.float32, kind="ExternalOutput").ap()
    gnn_kernel(nc, aps, out)
    r = _run(nc, [arrays], core_ids=[0])
    return r.results[0]["out_0_dram"]
```

```python
from contextlib import ExitStack

import concourse.bass as bass
from concourse import mybir

F32 = mybir.dt.float32
BF16 = mybir.dt.bfloat16
I32 = mybir.dt.int32
ALU = mybir.AluOpType
ACT = mybir.ActivationFunctionType
AX = mybir.AxisListType

P = 128
SLOTS = 4
BSLOTS = 4
R = 6
PAIRS = R // 2
EPS = 1e-5
FAR = 1000000.0
RELS = 16


class Counter:

    def __init__(self, sem):
        self.sem = sem
        self.base = 0

    def at(self, n):
        return n + self.base

    def close(self, steps):
        self.base += steps


def gnn_kernel(nc, A, out):
    x_in = A["x"]
    N, D = x_in.shape
    E = A["src"].shape[0]
    T = -(-E // P)
    EP = P * T
    FULLP = E // T
    RESTE = E - FULLP * T
    assert D == 256 and T % SLOTS == 0 and N < 256 * 256
    ITERS = T // SLOTS
    AUX = 4
    DW = D + AUX
    HEAD = N + 1
    AGGR = -(-(HEAD + P) // P) * P
    BATCH = P * R
    NBATCH = N // BATCH
    REST = N - NBATCH * BATCH
    assert 0 < REST <= P
    NT = NBATCH * R + 1
    C2 = D // P

    ctx = ExitStack()
    with ctx:
        def sb(name, shape, dt=F32, stack=ctx):
            return stack.enter_context(nc.sbuf_tensor(name, shape, dt))

        def counter(name):
            return Counter(ctx.enter_context(nc.semaphore(name)))

        def dram(name, shape, dt=F32):
            return nc.dram_tensor(name, shape, dt, kind="Internal").ap()

        sorted_lo = dram("sorted_lo", [EP + 2, 4])
        by_dst = dram("by_dst", [EP + 2, 4])
        by_src = dram("by_src", [EP + 2, 4])
        agg_d = dram("agg_d", [AGGR, DW])
        agg_s = dram("agg_s", [AGGR, D])
        x1 = dram("x1", [N, D])
        y1 = dram("y1", [N, D])
        x2 = dram("x2", [N, D])
        x3 = dram("x3", [N, DW])
        y3 = dram("y3", [N, D])
        att = dram("att", [N, 2])

        ident = sb("ident", [P, P])
        identb = sb("identb", [P, P], BF16)
        lower = sb("lower", [P, P])
        lowerb = sb("lowerb", [P, P], BF16)
        upper = sb("upper", [P, P])
        ones = sb("ones", [P, P])
        onesb = sb("onesb", [P, P], BF16)
        iota = sb("iota", [P, D], BF16)
        rel_iota = sb("rel_iota", [P, 96], BF16)
        part = sb("part", [P, 1])
        zero_b = sb("zero_b", [P, D], BF16)
        mats = {n: sb("w_" + n, [P, C2, D]) for n in ("wl", "wr", "root1", "root2", "l2", "g1", "g2")}
        rel_w = [sb(f"rel_w{i}", [96, 1024], BF16) for i in range(2)]
        bias3 = {n: sb("b_" + n, [3, D], BF16) for n in ("bl", "bias1", "bias2", "b2")}
        b_l2 = sb("b_l2", [P, D])
        b_g1 = sb("b_g1", [P, D])
        va = sb("va", [P, D])
        vb = sb("vb", [P, D])
        eps_col = sb("eps_col", [P, 2])
        cnt_nodes = sb("cnt_nodes", [P, NT])
        dinv = sb("dinv", [P, NT])

        class Edges:
            pass
        ed, es = Edges(), Edges()
        for o, s in ((ed, "d"), (es, "s")):
            o.same = sb("same_" + s, [P, T])
            o.gather = sb("gather_" + s, [P, T], I32)
            o.scatter = sb("scatter_" + s, [P, T], I32)
            o.head = sb("head_" + s, [P, 1], I32)
            o.carry = sb("carry_" + s, [P, P])
            o.weight = sb("weight_" + s, [P, T])
        ed.samen = sb("samen", [P, T])
        ed.end = sb("end", [P, T])
        ed.inhead = sb("inhead", [P, T])
        ed.intail = sb("intail", [P, T])
        ed.back = sb("back", [P, P])
        ed.dst = sb("dst_idx", [P, T], I32)
        ed.rel = sb("rel", [P, T])
        w_rel = sb("w_rel", [P, T])
        aux = sb("aux", [P, T, AUX])

        load = [counter(f"load{i}") for i in range(4)]
        put_head = counter("put_head")
        stored = [counter(f"stored{i}") for i in range(BSLOTS)]
        idx_ready = [counter(f"idx_ready{k}") for k in range(SLOTS)]
        gathered = [counter(f"gathered{k}") for k in range(SLOTS)]
        scattered = [counter(f"scattered{k}") for k in range(SLOTS)]
        msg_ready = [counter(f"msg_ready{k}") for k in range(SLOTS)]
        acc_ready = [counter(f"acc_ready{k}") for k in range(SLOTS)]
        row_ready = [counter(f"row_ready{k}") for k in range(SLOTS)]
        relw_ready = [counter(f"relw_ready{k}") for k in range(SLOTS)]
        prod_ready = [counter(f"prod_ready{k}") for k in range(SLOTS)]
        turned = [counter(f"turned{k}") for k in range(SLOTS)]
        turned_sb = [counter(f"turned_sb{k}") for k in range(SLOTS)]
        product = [counter(f"product{k}") for k in range(SLOTS)]
        pre_ready = [counter(f"pre_ready{k}") for k in range(SLOTS)]
        batch_done = [counter(f"batch_done{k}") for k in range(BSLOTS)]
        batch_out = [counter(f"batch_out{k}") for k in range(BSLOTS)]
        sum_ready = [counter(f"sum_ready{k}") for k in range(PAIRS)]
        stats_ready = counter("stats_ready")
        var_ready = counter("var_ready")
        rstd_ready = counter("rstd_ready")
        chain = counter("chain")
        pe_step = counter("pe_step")
        act_step = counter("act_step")
        pool_step = counter("pool_step")
        ready = counter("ready")
        cleared = counter("cleared")
        own_step = counter("own_step")
        deviation = counter("deviation")

        def link(eng, ins):
            chain.close(1)
            ins.then_inc(chain.sem, 1)
            eng.wait_ge(chain.sem, chain.base)

        with ExitStack() as tmp:
            w_raw = sb("w_raw", [P, 2, C2, D], F32, tmp)
            att_col = sb("att_col", [P, 2, C2], F32, tmp)
            att_bc = sb("att_bc", [P, 2, C2, P], F32, tmp)
            w2t = sb("w2t", [P, C2, D], F32, tmp)
            rel_raw = sb("rel_raw", [96, 2, 1024], F32, tmp)
            rel_hi = sb("rel_hi", [96, 2, 1024], BF16, tmp)
            rel_mid = sb("rel_mid", [96, 2, 1024], BF16, tmp)
            rel_lo = sb("rel_lo", [96, 2, 1024], BF16, tmp)
            b_raw = sb("b_raw", [3, 4, D], F32, tmp)
            b_part = sb("b_part", [3, 3, 4, D], BF16, tmp)
            sel = sb("sel", [P, 6], F32, tmp)
            tp = tmp.enter_context(nc.psum_tensor("tp", [P, 4, 512], F32))
            bc = tmp.enter_context(nc.psum_tensor("bc", [P, 2, 512], F32))

            names = ("bl", "bias1", "bias2", "b2")
            b_dram = (A["L0_gnn_b_l"], A["L1_gnn_bias1"], A["L1_gnn_bias2"], A["L3_gnn_b2"])
            plain = {"root1": "L1_gnn_root1", "root2": "L1_gnn_root2", "l2": "L2_gnn_W",
                     "g1": "L3_gnn_W1", "g2": "L3_gnn_W2"}
            block = tmp.enter_context(nc.Block())

            @block.sync
            def _(sp):
                loads = 0
                for i, n in enumerate(("L0_gnn_W_l", "L0_gnn_W_r")):
                    sp.dma_start(w_raw[:, i], A[n].rearrange("(c p) n -> p c n", p=P)).then_inc(load[0].sem, 16)
                    loads += 1
                for n, src in plain.items():
                    sp.dma_start(mats[n][:, :, :], A[src].rearrange("(c p) n -> p c n", p=P)).then_inc(load[0].sem, 16)
                    loads += 1
                for i, n in enumerate(("L3_gnn_att_src", "L3_gnn_att_dst")):
                    for c in range(C2):
                        sp.dma_start(att_col[:, i, c:c + 1], A[n][c * P:(c + 1) * P].rearrange("(p a) -> p a", a=1)).then_inc(load[0].sem, 16)
                        loads += 1
                sp.dma_start(b_l2[:, :], A["L2_gnn_b"].rearrange("(a d) -> a d", a=1).broadcast_to([P, D])).then_inc(load[0].sem, 16)
                sp.dma_start(b_g1[:, :], A["L3_gnn_b1"].rearrange("(a d) -> a d", a=1).broadcast_to([P, D])).then_inc(load[0].sem, 16)
                loads += 2
                for i in range(4):
                    for k in range(3):
                        sp.dma_start(b_raw[k:k + 1, i, :], b_dram[i].rearrange("(a d) -> a d", a=1)).then_inc(load[0].sem, 16)
                        loads += 1
                sp.wait_ge(pool_step.sem, 1)
                for i, n in enumerate(("L1_gnn_W1", "L1_gnn_W2")):
                    for k in range(3):
                        for j in range(4):
                            sp.dma_start(rel_raw[32 * k:32 * k + RELS, i, j * D:(j + 1) * D].rearrange("r (b o) -> r b o", o=4),
                                         A[n].rearrange("r b i o -> i r b o")[j]).then_inc(load[1].sem, 16)
                load[0].close(16 * loads)
                load[1].close(16 * 24)

            @block.gpsimd
            def _(pool):
                pool.memset(rel_raw[:, :, :], 0.0).then_inc(pool_step.sem, 1)
                pool.memset(ones[:, :], 1.0)
                pool.memset(onesb[:, :], 1.0)
                pool.memset(eps_col[:, 0:1], EPS / 4)
                pool.memset(eps_col[:, 1:2], EPS)
                pool.memset(zero_b[:, :], 0.0)
                pool.iota(iota[:, :], [[1, D]], base=0, channel_multiplier=0, allow_small_or_imprecise_dtypes=True)
                pool.iota(rel_iota[:, :], [[0, 3], [1, 32]], base=0, channel_multiplier=0, allow_small_or_imprecise_dtypes=True)
                pool.iota(part[:, :], [[0, 1]], base=0, channel_multiplier=1, allow_small_or_imprecise_dtypes=True).then_inc(pool_step.sem, 1)
                pool.wait_ge(pool_step.sem, 2)
                pool.affine_select(ident[:, :], ones[:, :], [[-1, P]], ALU.is_equal, 0.0, base=0, channel_multiplier=1)
                pool.affine_select(identb[:, :], onesb[:, :], [[-1, P]], ALU.is_equal, 0.0, base=0, channel_multiplier=1)
                pool.affine_select(lower[:, :], ones[:, :], [[1, P]], ALU.is_gt, 0.0, base=0, channel_multiplier=-1)
                pool.affine_select(lowerb[:, :], onesb[:, :], [[1, P]], ALU.is_gt, 0.0, base=0, channel_multiplier=-1)
                pool.affine_select(upper[:, :], ones[:, :], [[-1, P]], ALU.is_gt, 0.0, base=0, channel_multiplier=1).then_inc(pool_step.sem, 1)
            pool_step.close(3)

            @block.vector
            def _(dve):
                dve.wait_ge(pool_step.sem, 3)
                for k in range(3):
                    link(dve, dve.tensor_scalar(sel[:, k:k + 1], part[:, :], float(k), None, ALU.is_equal))
                    link(dve, dve.tensor_scalar(sel[:, 3 + k:4 + k], part[:, :], 32.0 * k, None, ALU.is_ge))
                for k in range(2):
                    link(dve, dve.tensor_tensor(sel[:, 3 + k:4 + k], sel[:, 3 + k:4 + k], sel[:, 4 + k:5 + k], ALU.subtract))
                dve.wait_ge(load[0].sem, load[0].base)
                link(dve, dve.tensor_scalar(w_raw[:, :, :, :], w_raw[:, :, :, :], 0.5, None, ALU.mult))
                link(dve, dve.tensor_scalar(b_raw[:, 0, :], b_raw[:, 0, :], 0.5, None, ALU.mult))
                for i in range(2):
                    for c in range(C2):
                        link(dve, dve.tensor_scalar(att_bc[:, i, c, :], ones[:, :], att_col[:, i, c:c + 1], None, ALU.mult))
                ready.close(1)
                dve.nop().then_inc(ready.sem, 1)
                link(dve, dve.tensor_copy(b_part[:, 0], b_raw[:, :, :]))
                link(dve, dve.tensor_tensor(b_raw[:, :, :], b_raw[:, :, :], b_part[:, 0], ALU.subtract))
                link(dve, dve.tensor_copy(b_part[:, 1], b_raw[:, :, :]))
                link(dve, dve.tensor_tensor(b_raw[:, :, :], b_raw[:, :, :], b_part[:, 1], ALU.subtract))
                link(dve, dve.tensor_copy(b_part[:, 2], b_raw[:, :, :]))
                for i, n in enumerate(names):
                    o = bias3[n][:, :]
                    link(dve, dve.tensor_scalar(o, b_part[:, 0, i, :], sel[0:3, 0:1], None, ALU.mult))
                    for k in (1, 2):
                        link(dve, dve.scalar_tensor_tensor(o, b_part[:, k, i, :], sel[0:3, k:k + 1], o, ALU.mult, ALU.add))
                dve.wait_ge(load[1].sem, load[1].base)
                link(dve, dve.tensor_copy(rel_hi[:, :, :], rel_raw[:, :, :]))
                link(dve, dve.tensor_tensor(rel_raw[:, :, :], rel_raw[:, :, :], rel_hi[:, :, :], ALU.subtract))
                link(dve, dve.tensor_copy(rel_mid[:, :, :], rel_raw[:, :, :]))
                link(dve, dve.tensor_tensor(rel_raw[:, :, :], rel_raw[:, :, :], rel_mid[:, :, :], ALU.subtract))
                link(dve, dve.tensor_copy(rel_lo[:, :, :], rel_raw[:, :, :]))
                for i in range(2):
                    o = rel_w[i][:, :]
                    link(dve, dve.tensor_scalar(o, rel_hi[:, i, :], sel[0:96, 3:4], None, ALU.mult))
                    for k, part_k in ((1, rel_mid), (2, rel_lo)):
                        link(dve, dve.scalar_tensor_tensor(o, part_k[:, i, :], sel[0:96, 3 + k:4 + k], o, ALU.mult, ALU.add))
                for i, o in enumerate((mats["wl"], mats["wr"], w2t)):
                    dve.wait_ge(pe_step.sem, 1 + i)
                    for c in range(C2):
                        link(dve, dve.tensor_copy(o[:, c, :], tp[:, c, 0:D]))
                dve.wait_ge(pe_step.sem, 4)
                link(dve, dve.tensor_copy(va[:, :], bc[:, 0, 0:D]))
                link(dve, dve.tensor_copy(vb[:, :], bc[:, 1, 0:D]))

            @block.tensor
            def _(pe):
                pe.wait_ge(ready.sem, ready.base)
                done = chain.base - 2 - 6
                srcs = (lambda j, c: w_raw[:, 0, j, c * P:(c + 1) * P],
                        lambda j, c: w_raw[:, 1, j, c * P:(c + 1) * P],
                        lambda j, c: mats["g2"][:, j, c * P:(c + 1) * P])
                for i, s in enumerate(srcs):
                    if i:
                        pe.wait_ge(chain.sem, done + 2 * i)
                    for j in range(C2):
                        for c in range(C2):
                            ins = pe.transpose(tp[:, c, j * P:(j + 1) * P], s(j, c), ident[:, :])
                    ins.then_inc(pe_step.sem, 1)
                pe.wait_ge(chain.sem, done + 6)
                for i in range(2):
                    for c in range(C2):
                        ins = pe.matmul(bc[:, i, 0:D], att_bc[:, i, c, :], w2t[:, c, :], start=(c == 0), stop=(c == C2 - 1))
                ins.then_inc(pe_step.sem, 1)
                pe_step.close(4)

        def sort_pass(name, columns, digit, target):
            with ExitStack() as tmp:
                rec = sb(f"rec_{name}", [P, T, 4], F32, tmp)
                raw = sb(f"raw_{name}", [P, 3, T], I32, tmp)
                key = sb(f"key_{name}", [P, T], I32, tmp)
                dig_i = sb(f"digi_{name}", [P, T], I32, tmp)
                dig = sb(f"dig_{name}", [P, T], F32, tmp)
                hot = sb(f"hot_{name}", [P, SLOTS, D], BF16, tmp)
                hist = sb(f"hist_{name}", [P, D], BF16, tmp)
                total = sb(f"total_{name}", [P, D], F32, tmp)
                place = sb(f"place_{name}", [P, D], F32, tmp)
                junk = sb(f"junk_{name}", [P, D], F32, tmp)
                rank = sb(f"rank_{name}", [P, SLOTS], F32, tmp)
                to = sb(f"to_{name}", [P, SLOTS], I32, tmp)
                out_rec = sb(f"outrec_{name}", [P, SLOTS, 4], F32, tmp)
                ph = tmp.enter_context(nc.psum_tensor(f"ph_{name}", [P, 3, 512], F32))
                n_load = 1 if columns is None else 2 * len(columns)
                chain0 = {}
                block = tmp.enter_context(nc.Block())

                @block.sync
                def _(sp):
                    if columns is None:
                        sp.dma_start(rec[:, :, :].rearrange("p t f -> p (t f)"),
                                     sorted_lo[1:EP + 1, :].rearrange("(p t) f -> p (t f)", p=P)).then_inc(load[0].sem, 16)
                    else:
                        sp.wait_ge(ready.sem, ready.at(1))
                        for i, src in enumerate(columns):
                            sp.dma_start(raw[0:FULLP, i, :], src[0:FULLP * T].rearrange("(p t) -> p t", t=T)).then_inc(load[0].sem, 16)
                            sp.dma_start(raw[FULLP:FULLP + 1, i, 0:RESTE], src[FULLP * T:E].rearrange("(a t) -> a t", a=1)).then_inc(load[0].sem, 16)
                load[0].close(16 * n_load)
                

                @block.vector
                def _(dve):
                    if columns is not None:
                        dve.memset(raw[:, 1:3, :], 0)
                        dve.memset(rec[:, :, 3:4], 0.0)
                        dve.memset(raw[:, 0, :], N).then_inc(ready.sem, 1)
                    dve.wait_ge(load[0].sem, load[0].base)
                    for i in range(3 if columns is not None else 0):
                        link(dve, dve.tensor_copy(rec[:, :, i], raw[:, i, :]))
                    link(dve, dve.tensor_copy(key[:, :], rec[:, :, 0]))
                    op, by = (ALU.bitwise_and, 255) if digit == 0 else (ALU.logical_shift_right, 8)
                    link(dve, dve.tensor_scalar(dig_i[:, :], key[:, :], by, None, op))
                    link(dve, dve.tensor_copy(dig[:, :], dig_i[:, :]))
                    with dve.Fori(0, ITERS) as i:
                        for k in range(SLOTS):
                            dve.wait_ge(product[k].sem, product[k].at(i))
                            dve.tensor_scalar(hot[:, k, :], iota[:, :], dig[:, bass.ds(i * SLOTS + k, 1)], None, ALU.is_equal).then_inc(msg_ready[k].sem, 1)
                    dve.wait_ge(pe_step.sem, pe_step.at(1))
                    link(dve, dve.tensor_copy(hist[:, :], ph[:, 0, 0:D]))
                    chain0["hist"] = chain.base
                    dve.wait_ge(pe_step.sem, pe_step.at(2))
                    link(dve, dve.tensor_copy(total[:, :], ph[:, 2, 0:D]))
                    link(dve, dve.tensor_tensor_scan(place[:, :], ones[:, 0:1].broadcast_to([P, D]), total[:, :], 0.0, ALU.mult, ALU.add))
                    link(dve, dve.tensor_tensor(place[:, :], place[:, :], total[:, :], ALU.subtract))
                    link(dve, dve.tensor_tensor(place[:, :], place[:, :], ph[:, 1, 0:D], ALU.add))
                    with dve.Fori(0, ITERS) as i:
                        for k in range(SLOTS):
                            before_k = acc_ready[(k - 1) % SLOTS]
                            dve.tensor_scalar(hot[:, k, :], iota[:, :], dig[:, bass.ds(i * SLOTS + k, 1)], None, ALU.is_equal).then_inc(turned[k].sem, 1)
                            dve.wait_ge(turned[k].sem, turned[k].at(i + 1))
                            dve.wait_ge(before_k.sem, before_k.at(i + (k > 0)))
                            dve.scalar_tensor_tensor(junk[:, :], place[:, :], 1.0, hot[:, k, :], ALU.mult, ALU.mult, accum_out=rank[:, k:k + 1]).then_inc(turned_sb[k].sem, 1)
                            dve.wait_ge(turned_sb[k].sem, turned_sb[k].at(i + 1))
                            dve.tensor_tensor(place[:, :], place[:, :], hot[:, k, :], ALU.add).then_inc(acc_ready[k].sem, 1)
                            dve.wait_ge(scattered[k].sem, scattered[k].at(i * 16))
                            dve.tensor_copy(out_rec[:, k, :], rec[:, bass.ds(i * SLOTS + k, 1), :].rearrange("p a f -> p (a f)"))
                            dve.tensor_scalar(to[:, k:k + 1], rank[:, k:k + 1], 1.0, None, ALU.add).then_inc(row_ready[k].sem, 1)

                if columns is not None:
                    ready.close(1)

                @block.tensor
                def _(pe):
                    pe.matmul(ph[:, 0, 0:D], identb[:, :], zero_b[:, :], start=True, stop=False)
                    with pe.Fori(0, ITERS) as i:
                        for k in range(SLOTS):
                            pe.wait_ge(msg_ready[k].sem, msg_ready[k].at(i + 1))
                            pe.matmul(ph[:, 0, 0:D], identb[:, :], hot[:, k, :], start=False, stop=False).then_inc(product[k].sem, 1)
                    pe.matmul(ph[:, 0, 0:D], identb[:, :], zero_b[:, :], start=False, stop=True).then_inc(pe_step.sem, 1)
                    pe.wait_ge(chain.sem, chain0["hist"])
                    pe.matmul(ph[:, 1, 0:D], lowerb[:, :], hist[:, :], start=True, stop=True)
                    pe.matmul(ph[:, 2, 0:D], onesb[:, :], hist[:, :], start=True, stop=True).then_inc(pe_step.sem, 1)

                @block.gpsimd
                def _(pool):
                    with pool.Fori(0, ITERS) as i:
                        for k in range(SLOTS):
                            pool.wait_ge(row_ready[k].sem, row_ready[k].at(i + 1))
                            pool.nop(nofuse=True)
                            pool.indirect_dma_start(
                                out=target[:, :], out_offset=bass.IndirectOffsetOnAxis(ap=to[:, k:k + 1], axis=0),
                                in_=out_rec[:, k, :], in_offset=None, bounds_check=EP, oob_is_err=False).then_inc(scattered[k].sem, 16)
                    for k in range(SLOTS):
                        pool.wait_ge(scattered[k].sem, scattered[k].at(16 * ITERS))
                for k in range(SLOTS):
                    product[k].close(ITERS); msg_ready[k].close(ITERS); acc_ready[k].close(ITERS)
                    turned[k].close(ITERS); turned_sb[k].close(ITERS); row_ready[k].close(ITERS)
                    scattered[k].close(16 * ITERS)
                pe_step.close(2)

        primed_dma = scattered
        primed = [c for group in (idx_ready, msg_ready, acc_ready, row_ready, turned, turned_sb, product,
                                  pre_ready, relw_ready, prod_ready, batch_done, batch_out) for c in group]

        with ExitStack() as tmp:
            zeros = sb("zeros", [P, 28 * DW], F32, tmp)
            edge_key = sb("edge_key", [1, 4], F32, tmp)
            block = tmp.enter_context(nc.Block())
            Q = AGGR // P
            assert Q % 28 == 0

            @block.vector
            def _(dve):
                dve.memset(edge_key[:, :], -1.0)
                dve.memset(zeros[:, :], 0.0).then_inc(ready.sem, 1)

            @block.gpsimd
            def _(pool):
                pool.wait_ge(ready.sem, ready.at(1))
                for c in primed_dma:
                    pool.dma_start(sorted_lo[0:1, :], edge_key[:, :]).then_inc(c.sem, 16)
                    pool.wait_ge(c.sem, 16)
                    c.close(16)

            @block.scalar
            def _(act):
                for c in primed:
                    act.sem_inc(c.sem, 1)
                    c.close(1)

            @block.sync
            def _(sp):
                sp.wait_ge(ready.sem, ready.at(1))
                for a, w in ((agg_d, DW), (agg_s, D)):
                    v = a.rearrange("(p q r) d -> q p (r d)", p=P, r=28)
                    for q in range(Q // 28):
                        sp.dma_start(v[q], zeros[:, 0:28 * w]).then_inc(cleared.sem, 16)
                for c in stored:
                    sp.dma_start(sorted_lo[EP + 1:EP + 2, :], edge_key[:, :]).then_inc(c.sem, 16)
                    sp.wait_ge(c.sem, 16)
                    c.close(16)
                for a in (by_dst, by_src):
                    for r in (0, EP + 1):
                        sp.dma_start(a[r:r + 1, :], edge_key[:, :]).then_inc(cleared.sem, 16)
                sp.wait_ge(cleared.sem, cleared.at(16 * (2 * (Q // 28) + 4)))
            cleared.close(16 * (2 * (Q // 28) + 4))
            ready.close(1)

        sort_pass("d0", (A["dst"], A["src"], A["edge_type_16"]), 0, sorted_lo)
        sort_pass("d1", None, 1, by_dst)
        sort_pass("s0", (A["src"], A["dst"]), 0, sorted_lo)
        sort_pass("s1", None, 1, by_src)

        def prepare(o, src_dram, name, with_rel):
            C = RELS + 1 if with_rel else 1
            with ExitStack() as tmp:
                prv = sb("prv_" + name, [P, T, 4], F32, tmp)
                rec = sb("cur_" + name, [P, T, 4], F32, tmp)
                nxt = sb("nxt_" + name, [P, T, 4], F32, tmp)
                diag = sb("diag_" + name, [P, 2, P], F32, tmp)
                f1 = sb("f1_" + name, [P, T], F32, tmp)
                f2 = sb("f2_" + name, [P, T], F32, tmp)
                samen = sb("samen_" + name, [P, T], F32, tmp)
                end = sb("end_" + name, [P, T], F32, tmp)
                inhead = sb("inhead_" + name, [P, T], F32, tmp)
                intail = sb("intail_" + name, [P, T], F32, tmp)
                back = sb("back_" + name, [P, P], F32, tmp)
                sameC = sb("sameC_" + name, [P, C, T], F32, tmp)
                samenC = sb("samenC_" + name, [P, C, T], F32, tmp)
                V = sb("V_" + name, [P, C, T], F32, tmp)
                fwd = sb("fwd_" + name, [P, C * T], F32, tmp)
                bwd = sb("bwd_" + name, [P, C * T], F32, tmp)
                runs = sb("runs_" + name, [P, 2, C], F32, tmp)
                ph = tmp.enter_context(nc.psum_tensor("ph_" + name, [P, 2, 512], F32))
                pc = tmp.enter_context(nc.psum_tensor("pc_" + name, [P, 2, 512], F32))
                marks = {}
                block = tmp.enter_context(nc.Block())

                @block.sync
                def _(sp):
                    for t_, r0 in ((prv, 0), (rec, 1), (nxt, 2)):
                        sp.dma_start(t_[:, :, :].rearrange("p t f -> p (t f)"),
                                     src_dram[r0:r0 + EP, :].rearrange("(p t) f -> p (t f)", p=P)).then_inc(load[0].sem, 16)
                load[0].close(48)

                @block.vector
                def _(dve):
                    dve.wait_ge(load[0].sem, load[0].base)
                    key, first, last = rec[:, :, 0], rec[:, 0, 0:1], rec[:, T - 1, 0:1]
                    link(dve, dve.tensor_tensor(o.same[:, :], key, prv[:, :, 0], ALU.is_equal))
                    link(dve, dve.memset(o.same[:, 0:1], 0.0))
                    link(dve, dve.tensor_tensor(samen[:, :], key, nxt[:, :, 0], ALU.is_equal))
                    link(dve, dve.tensor_scalar(end[:, :], samen[:, :], -1.0, 1.0, ALU.mult, ALU.add))
                    link(dve, dve.memset(samen[:, T - 1:T], 0.0))
                    link(dve, dve.tensor_scalar(inhead[:, :], key, first, None, ALU.is_equal))
                    link(dve, dve.tensor_scalar(intail[:, :], key, last, None, ALU.is_equal))
                    link(dve, dve.tensor_copy(o.gather[:, :], rec[:, :, 1]))
                    link(dve, dve.tensor_scalar(f1[:, :], part[:, :].broadcast_to([P, T]), float(HEAD), None, ALU.add))
                    link(dve, dve.tensor_tensor(f1[:, :], f1[:, :], key, ALU.subtract))
                    link(dve, dve.tensor_tensor(f1[:, :], f1[:, :], inhead[:, :], ALU.mult))
                    link(dve, dve.tensor_tensor(f1[:, :], f1[:, :], key, ALU.add))
                    link(dve, dve.tensor_scalar(f2[:, :], end[:, :], -FAR, FAR, ALU.mult, ALU.add))
                    link(dve, dve.tensor_tensor(o.scatter[:, :], f1[:, :], f2[:, :], ALU.add))
                    link(dve, dve.tensor_tensor(f1[:, 0:1], first, nxt[:, T - 1, 0:1], ALU.is_equal))
                    link(dve, dve.scalar_tensor_tensor(o.head[:, :], f1[:, 0:1], FAR, first, ALU.mult, ALU.add))
                    link(dve, dve.tensor_scalar(diag[:, 0, :], ident[:, :], first, None, ALU.mult))
                    link(dve, dve.tensor_scalar(diag[:, 1, :], ident[:, :], last, None, ALU.mult))
                    marks["diag"] = chain.base
                    dve.wait_ge(pe_step.sem, pe_step.at(1))
                    link(dve, dve.scalar_tensor_tensor(o.carry[:, :], ph[:, 0, 0:P], last, lower[:, :], ALU.is_equal, ALU.mult))
                    link(dve, dve.scalar_tensor_tensor(back[:, :], ph[:, 1, 0:P], first, upper[:, :], ALU.is_equal, ALU.mult))
                    link(dve, dve.memset(V[:, C - 1, :], 1.0))
                    for r in range(C - 1):
                        link(dve, dve.tensor_scalar(V[:, r, :], rec[:, :, 2], float(r), None, ALU.is_equal))
                    link(dve, dve.tensor_copy(sameC[:, :, :], o.same[:, :].rearrange("p (a t) -> p a t", a=1).broadcast_to([P, C, T])))
                    link(dve, dve.tensor_copy(samenC[:, :, :], samen[:, :].rearrange("p (a t) -> p a t", a=1).broadcast_to([P, C, T])))
                    flat = lambda a: a[:, :, :].rearrange("p c t -> p (c t)")
                    link(dve, dve.tensor_tensor_scan(fwd[:, :], flat(sameC), flat(V), 0.0, ALU.mult, ALU.add))
                    link(dve, dve.tensor_tensor_scan(bwd[:, ::-1], flat(samenC)[:, ::-1], flat(V)[:, ::-1], 0.0, ALU.mult, ALU.add))
                    fw, bw = (a[:, :].rearrange("p (c t) -> p c t", t=T) for a in (fwd, bwd))
                    link(dve, dve.tensor_copy(runs[:, 0, :], fw[:, :, T - 1]))
                    link(dve, dve.tensor_copy(runs[:, 1, :], bw[:, :, 0]))
                    marks["runs"] = chain.base
                    link(dve, dve.tensor_tensor(fwd[:, :], fwd[:, :], bwd[:, :], ALU.add))
                    link(dve, dve.tensor_tensor(fwd[:, :], fwd[:, :], flat(V), ALU.subtract))
                    dve.wait_ge(pe_step.sem, pe_step.at(2))
                    for j, inside in ((0, inhead), (1, intail)):
                        link(dve, dve.tensor_copy(runs[:, j, :], pc[:, j, 0:C]))
                        link(dve, dve.tensor_tensor(sameC[:, :, :], inside[:, :].rearrange("p (a t) -> p a t", a=1).broadcast_to([P, C, T]),
                                                    runs[:, j, :].rearrange("p (c a) -> p c a", a=1).broadcast_to([P, C, T]), ALU.mult))
                        link(dve, dve.tensor_tensor(fwd[:, :], fwd[:, :], flat(sameC), ALU.add))
                    link(dve, dve.tensor_scalar(f1[:, :], fw[:, C - 1, :], 1.0, None, ALU.max))
                    link(dve, dve.reciprocal(o.weight[:, :], f1[:, :]))
                    if with_rel:
                        link(dve, dve.tensor_tensor(V[:, :, :], V[:, :, :], fw, ALU.mult))
                        link(dve, dve.tensor_reduce(f2[:, :], V[:, 0:RELS, :].rearrange("p c t -> p t c"), AX.X, ALU.add))
                        link(dve, dve.tensor_scalar(f2[:, :], f2[:, :], 1.0, None, ALU.max))
                        link(dve, dve.reciprocal(w_rel[:, :], f2[:, :]))
                        link(dve, dve.memset(aux[:, :, :], 0.0))
                        link(dve, dve.tensor_tensor(aux[:, :, 0], f1[:, :], end[:, :], ALU.mult))
                        link(dve, dve.tensor_copy(ed.samen[:, :], samen[:, :]))
                        link(dve, dve.tensor_copy(ed.end[:, :], end[:, :]))
                        link(dve, dve.tensor_copy(ed.inhead[:, :], inhead[:, :]))
                        link(dve, dve.tensor_copy(ed.intail[:, :], intail[:, :]))
                        link(dve, dve.tensor_copy(ed.back[:, :], back[:, :]))
                        link(dve, dve.tensor_scalar(ed.dst[:, :], key, float(N - 1), None, ALU.min))
                        link(dve, dve.tensor_copy(ed.rel[:, :], rec[:, :, 2]))

                @block.tensor
                def _(pe):
                    pe.wait_ge(chain.sem, marks["diag"])
                    pe.matmul(ph[:, 0, 0:P], ones[:, :], diag[:, 0, :], start=True, stop=True)
                    pe.matmul(ph[:, 1, 0:P], ones[:, :], diag[:, 1, :], start=True, stop=True).then_inc(pe_step.sem, 1)
                    pe.wait_ge(chain.sem, marks["runs"])
                    pe.matmul(pc[:, 0, 0:C], o.carry[:, :], runs[:, 0, :], start=True, stop=True)
                    pe.matmul(pc[:, 1, 0:C], back[:, :], runs[:, 1, :], start=True, stop=True).then_inc(pe_step.sem, 1)
                pe_step.close(2)

        prepare(ed, by_dst, "pd", True)
        prepare(es, by_src, "ps", False)

        def before_slot(c, k, i):
            q = c[(k - 2) % SLOTS]
            return q.sem, q.at(i + (k >= 2))

        def all_tiles(eng, *stages):
            most = max(lead for lead, _ in stages)
            loops = (T - most) // SLOTS

            def one(n):
                for lead, work in stages:
                    if 0 <= n + lead < T:
                        work(*divmod(n + lead, SLOTS))
            for n in range(-most, 0):
                one(n)
            with eng.Fori(0, loops) as i:
                for k in range(SLOTS):
                    for lead, work in stages:
                        rounds_on, slot = divmod(k + lead, SLOTS)
                        work(i + rounds_on if rounds_on else i, slot)
            for n in range(loops * SLOTS, T):
                one(n)

        def edge_pass(name, o, table, tw, agg, aw, weight, matrix=None, bias=None, rel=None, with_aux=False):
            n_pe = 3 if matrix is not None else 1
            GATHER_LEAD = SLOTS + 2 if matrix is not None else SLOTS
            with ExitStack() as tmp:
                rows = sb("rows_" + name, [P, SLOTS, tw], F32, tmp)
                gidx = sb("gidx_" + name, [P, SLOTS], I32, tmp)
                sidx = sb("sidx_" + name, [P, SLOTS], I32, tmp)
                msg = sb("msg_" + name, [P, SLOTS, D], F32, tmp)
                acc = sb("acc_" + name, [P, SLOTS, aw], F32, tmp)
                headrow = sb("headrow_" + name, [P, aw], F32, tmp)
                ps = tmp.enter_context(nc.psum_tensor("ps_" + name, [P, 8, 512], F32))
                res, res_ready = acc, acc_ready
                if matrix is not None:
                    res, res_ready = sb("res_" + name, [P, SLOTS, aw], F32, tmp), row_ready
                    accT = sb("accT_" + name, [P, 2, D], F32, tmp)
                    carried = sb("carried_" + name, [P, aw], F32, tmp)
                if rel is not None:
                    prod = sb("prod_" + name, [P, 2, 1024], F32, tmp)
                turn_ps, out_ps, rel_ps = ps[:, 0:2, 0:D], ps[:, 2:4, 0:D], ps[:, 4:8, :]
                msg_used = prod_ready if rel is not None else acc_ready
                marks = {}
                block = tmp.enter_context(nc.Block())

                @block.gpsimd
                def _(pool):
                    def gather(i, k):
                        pool.wait_ge(idx_ready[k].sem, idx_ready[k].at(i + 1))
                        pool.nop(nofuse=True)
                        pool.indirect_dma_start(
                            out=rows[:, k, :], out_offset=None, in_=table[:, :],
                            in_offset=bass.IndirectOffsetOnAxis(ap=gidx[:, k:k + 1], axis=0),
                            bounds_check=N - 1, oob_is_err=False).then_inc(gathered[k].sem, 16)

                    def scatter(i, k):
                        pool.wait_ge(res_ready[k].sem, res_ready[k].at(i + 1))
                        pool.nop(nofuse=True)
                        pool.indirect_dma_start(
                            out=agg[:, :], out_offset=bass.IndirectOffsetOnAxis(ap=sidx[:, k:k + 1], axis=0),
                            in_=res[:, k, :], in_offset=None,
                            bounds_check=HEAD + P - 1, oob_is_err=False).then_inc(scattered[k].sem, 16)

                    all_tiles(pool, (GATHER_LEAD, gather), (0, scatter))
                    pool.wait_ge(ready.sem, ready.at(1))
                    pool.indirect_dma_start(
                        out=agg[:, :], out_offset=bass.IndirectOffsetOnAxis(ap=o.head[:, 0:1], axis=0),
                        in_=headrow[:, :], in_offset=None, bounds_check=N - 1, oob_is_err=False).then_inc(put_head.sem, 16)
                    pool.wait_ge(put_head.sem, put_head.at(16))

                @block.sync
                def _(sp):
                    for k in range(SLOTS):
                        sp.wait_ge(scattered[k].sem, scattered[k].at(16 * ITERS))
                    sp.dma_start(headrow[:, :], agg[HEAD:HEAD + P, :]).then_inc(load[0].sem, 16)

                @block.scalar
                def _(act):
                    def weigh(i, k):
                        act.wait_ge(gathered[k].sem, gathered[k].at(i * 16 + 16))
                        act.wait_ge(msg_used[k].sem, msg_used[k].at(i))
                        w = rows[:, k, D:D + 1] if weight is None else weight[:, bass.ds(i * SLOTS + k, 1)]
                        act.activation(msg[:, k, :], rows[:, k, 0:D], ACT.Copy, scale=w).then_inc(msg_ready[k].sem, 1)

                    def next_index(i, k):
                        act.wait_ge(msg_ready[k].sem, msg_ready[k].at(i))
                        act.copy(gidx[:, k:k + 1], o.gather[:, bass.ds(i * SLOTS + k, 1)]).then_inc(idx_ready[k].sem, 1)

                    def turn_out(i, k):
                        act.wait_ge(turned[k].sem, turned[k].at(i + 1))
                        act.wait_ge(*before_slot(product, k, i))
                        act.copy(accT[:, k % 2, :], turn_ps[:, k % 2, :]).then_inc(turned_sb[k].sem, 1)

                    if matrix is None:
                        all_tiles(act, (0, weigh), (SLOTS, next_index))
                    else:
                        all_tiles(act, (3, weigh), (SLOTS + 3, next_index), (0, turn_out))
                        act.wait_ge(pe_step.sem, pe_step.at(2))
                        act.copy(accT[:, 0, :], turn_ps[:, 0, :]).then_inc(act_step.sem, 1)

                @block.vector
                def _(dve):
                    link(dve, dve.memset(acc[:, :, :], 0.0))

                    def multiply(i, k):
                        dve.wait_ge(relw_ready[k].sem, relw_ready[k].at(i + 1))
                        dve.wait_ge(*before_slot(product, k, i))
                        dve.wait_ge(msg_ready[k].sem, msg_ready[k].at(i + 1))
                        for h in range(2):
                            ins = dve.tensor_tensor(
                                prod[:, k % 2, h * 512:(h + 1) * 512].rearrange("p (i b o) -> p i b o", i=2, o=4),
                                rel_ps[:, 2 * (k % 2) + h, :].rearrange("p (i b o) -> p i b o", i=2, o=4),
                                msg[:, k, :].rearrange("p (b i a) -> p i b a", i=4, a=1)[:, 2 * h:2 * h + 2].broadcast_to([P, 2, D // 4, 4]),
                                ALU.mult)
                        ins.then_inc(prod_ready[k].sem, 1)

                    def add(i, k):
                        t = bass.ds(i * SLOTS + k, 1)
                        last = acc_ready[(k - 1) % SLOTS]
                        if matrix is not None:
                            dve.wait_ge(turned[k].sem, turned[k].at(i))
                        if res is acc:
                            dve.wait_ge(scattered[k].sem, scattered[k].at(i * 16))
                            dve.tensor_copy(sidx[:, k:k + 1], o.scatter[:, t])
                        if rel is not None:
                            dve.wait_ge(product[k].sem, product[k].at(i + 1))
                        else:
                            dve.wait_ge(msg_ready[k].sem, msg_ready[k].at(i + 1))
                        dve.wait_ge(last.sem, last.at(i + (k > 0)))
                        new = out_ps[:, k % 2, :] if rel is not None else msg[:, k, :]
                        ins = dve.scalar_tensor_tensor(acc[:, k, 0:D], acc[:, (k - 1) % SLOTS, 0:D], o.same[:, t], new, ALU.mult, ALU.add)
                        if with_aux:
                            ins = dve.scalar_tensor_tensor(acc[:, k, D:aw], acc[:, (k - 1) % SLOTS, D:aw], o.same[:, t],
                                                           aux[:, t, :].rearrange("p a f -> p (a f)"), ALU.mult, ALU.add)
                        ins.then_inc(acc_ready[k].sem, 1)

                    def finish(i, k):
                        dve.wait_ge(scattered[k].sem, scattered[k].at(i * 16))
                        dve.tensor_copy(sidx[:, k:k + 1], o.scatter[:, bass.ds(i * SLOTS + k, 1)])
                        dve.wait_ge(product[k].sem, product[k].at(i + 1))
                        if with_aux:
                            dve.tensor_copy(res[:, k, D:aw], acc[:, k, D:aw])
                        if bias is not None:
                            ins = dve.tensor_tensor(res[:, k, 0:D], out_ps[:, k % 2, :], bias[:, :], ALU.add)
                        else:
                            ins = dve.tensor_copy(res[:, k, 0:D], out_ps[:, k % 2, :])
                        ins.then_inc(row_ready[k].sem, 1)

                    if matrix is not None:
                        all_tiles(dve, (2, add), (0, finish))
                    elif rel is not None:
                        all_tiles(dve, (1, multiply), (0, add))
                    else:
                        all_tiles(dve, (0, add))
                    dve.wait_ge(load[0].sem, load[0].at(16))
                    dve.wait_ge(pe_step.sem, pe_step.at(1))
                    if matrix is not None:
                        link(dve, dve.tensor_copy(carried[:, :], ps[:, 2, 0:aw]))
                        marks["carried"] = chain.base
                        dve.wait_ge(pe_step.sem, pe_step.at(3))
                        link(dve, dve.tensor_tensor(headrow[:, 0:D], headrow[:, 0:D], ps[:, 3, 0:D], ALU.add))
                        if with_aux:
                            link(dve, dve.tensor_tensor(headrow[:, D:aw], headrow[:, D:aw], carried[:, D:aw], ALU.add))
                    else:
                        link(dve, dve.tensor_tensor(headrow[:, :], headrow[:, :], ps[:, 2, 0:aw], ALU.add))
                    dve.sem_inc(ready.sem, 1)

                @block.tensor
                def _(pe):
                    def turn(i, k):
                        pe.wait_ge(*before_slot(turned_sb, k, i))
                        pe.wait_ge(acc_ready[k].sem, acc_ready[k].at(i + 1))
                        for c in range(C2):
                            ins = pe.transpose(turn_ps[:, k % 2, c * P:(c + 1) * P], acc[:, k, c * P:(c + 1) * P], ident[:, :])
                        ins.then_inc(turned[k].sem, 1)

                    def multiply(i, k):
                        pe.wait_ge(*before_slot(row_ready, k, i))
                        pe.wait_ge(turned_sb[k].sem, turned_sb[k].at(i + 1))
                        for c in range(C2):
                            ins = pe.matmul(out_ps[:, k % 2, :], accT[:, k % 2, c * P:(c + 1) * P], matrix[:, c, :],
                                            start=(c == 0), stop=(c == C2 - 1))
                        ins.then_inc(product[k].sem, 1)

                    def spread(i, k):
                        pe.wait_ge(*before_slot(prod_ready, k, i))
                        for h in range(2):
                            ins = pe.matmul(rel_ps[:, 2 * (k % 2) + h, :], rel_hot[:, bass.ds((i * SLOTS + k) * P, P)],
                                            rel[:, h * 512:(h + 1) * 512], start=True, stop=True)
                        ins.then_inc(relw_ready[k].sem, 1)

                    def block_sum(i, k):
                        pe.wait_ge(*before_slot(acc_ready, k, i))
                        pe.wait_ge(prod_ready[k].sem, prod_ready[k].at(i + 1))
                        for j in range(4):
                            ins = pe.matmul(out_ps[:, k % 2, :], ident[:, :], prod[:, k % 2, j * D:(j + 1) * D], start=(j == 0), stop=(j == 3))
                        ins.then_inc(product[k].sem, 1)

                    if matrix is not None:
                        all_tiles(pe, (1, turn), (0, multiply))
                    elif rel is not None:
                        all_tiles(pe, (1, spread), (0, block_sum))
                    pe.wait_ge(acc_ready[SLOTS - 1].sem, acc_ready[SLOTS - 1].at(ITERS))
                    if matrix is not None:
                        pe.wait_ge(row_ready[SLOTS - 2].sem, row_ready[SLOTS - 2].at(ITERS))
                    pe.matmul(ps[:, 2, 0:aw], o.carry[:, :], acc[:, SLOTS - 1, :], start=True, stop=True).then_inc(pe_step.sem, 1)
                    if matrix is not None:
                        pe.wait_ge(turned_sb[SLOTS - 2].sem, turned_sb[SLOTS - 2].at(ITERS))
                        pe.wait_ge(chain.sem, marks["carried"])
                        for c in range(C2):
                            ins = pe.transpose(ps[:, 0, c * P:(c + 1) * P], carried[:, c * P:(c + 1) * P], ident[:, :])
                        ins.then_inc(pe_step.sem, 1)
                        pe.wait_ge(row_ready[SLOTS - 1].sem, row_ready[SLOTS - 1].at(ITERS))
                        pe.wait_ge(act_step.sem, act_step.at(1))
                        for c in range(C2):
                            ins = pe.matmul(ps[:, 3, 0:D], accT[:, 0, c * P:(c + 1) * P], matrix[:, c, :], start=(c == 0), stop=(c == C2 - 1))
                        ins.then_inc(pe_step.sem, 1)

                for k in range(SLOTS):
                    for c in (idx_ready, acc_ready, msg_ready):
                        c[k].close(ITERS)
                    gathered[k].close(16 * ITERS)
                    scattered[k].close(16 * ITERS)
                    if matrix is not None:
                        for c in (turned, turned_sb, product, row_ready):
                            c[k].close(ITERS)
                    if rel is not None:
                        for c in (relw_ready, prod_ready, product):
                            c[k].close(ITERS)
                put_head.close(16)
                load[0].close(16)
                ready.close(1)
                pe_step.close(n_pe)
                if matrix is not None:
                    act_step.close(1)

        def batches(eng, *stages):
            most = max(lead for lead, _ in stages)
            least = min(lead for lead, _ in stages)
            assert least >= 0

            def do(work, i, s, n):
                if isinstance(n, int) and n >= NBATCH:
                    work(i, s, n, REST, 1)
                else:
                    work(i, s, n, P, R)

            def one(n):
                for lead, work in stages:
                    if 0 <= n + lead <= NBATCH:
                        do(work, (n + lead) // BSLOTS, (n + lead) % BSLOTS, n + lead)
            for n in range(-most, 0):
                one(n)
            loops = (NBATCH - most) // BSLOTS
            with eng.Fori(0, loops) as i:
                for s in range(BSLOTS):
                    for lead, work in stages:
                        do(work, i + (s + lead) // BSLOTS if s + lead >= BSLOTS else i, (s + lead) % BSLOTS, i * BSLOTS + (s + lead))
            for n in range(loops * BSLOTS, NBATCH + 1):
                one(n)

        def rounds(s):
            return NBATCH // BSLOTS + (s <= NBATCH % BSLOTS)

        def node_pass(name, ins, target, kind, matrix=None, bias=None):
            ninp = len(ins)
            norm = kind != "rgcn1" and kind != "gcn"
            own_row = kind in ("gcn", "gat")
            wide = DW if kind == "conv" else D
            n_store = 2 if kind == "gcn" else 1
            with ExitStack() as tmp:
                inp = [[sb(f"in{j}{s}_{name}", [P, R, w], F32, tmp) for j, (_, w) in enumerate(ins)] for s in range(BSLOTS)]
                u = [sb(f"u{s}_{name}", [P, R, wide], F32, tmp) for s in range(BSLOTS)]
                stats = sb(f"stats_{name}", [P, 2, R, 6], F32, tmp)
                mv = sb(f"mv_{name}", [P, BSLOTS, R, 2], F32, tmp)
                dev = sb(f"dev_{name}", [P, BSLOTS, R], F32, tmp)
                scale = sb(f"scale_{name}", [P, BSLOTS, R, 2], F32, tmp)
                own = sb(f"own_{name}", [P, BSLOTS, R], F32, tmp)
                attb = sb(f"attb_{name}", [P, BSLOTS, R, 2], F32, tmp)
                junk = sb(f"junk_{name}", [P, 2, R, 2, D], BF16, tmp) if kind == "gcn" else None
                xT = sb(f"xT_{name}", [P, 2, PAIRS, 512], F32, tmp)
                ps = tmp.enter_context(nc.psum_tensor("ps_" + name, [P, 8, 512], F32))
                turn_ps, out_ps = ps[:, 0:PAIRS, :], ps[:, PAIRS:2 * PAIRS, :]
                eps = eps_col[:, 0:1] if kind == "sage" else eps_col[:, 1:2]
                block = tmp.enter_context(nc.Block())

                def view(a, n, pp, r):
                    if pp == P:
                        return a[0:NBATCH * BATCH, :].rearrange("(n p r) d -> n p (r d)", p=P, r=R)[n]
                    return a[NBATCH * BATCH:N, :]

                def pairs(r):
                    return [(g, min(2, r - 2 * g)) for g in range(-(-r // 2))]

                @block.sync
                def _(sp):
                    def fetch(i, s, n, pp, r):
                        sp.wait_ge(batch_done[s].sem, batch_done[s].at(i))
                        sp.nop(nofuse=True)
                        for j, (a, w) in enumerate(ins):
                            sp.dma_start(inp[s][j][0:pp, 0:r, :].rearrange("p r d -> p (r d)"), view(a, n, pp, r)).then_inc(load[s].sem, 16)
                    batches(sp, (0, fetch))

                if matrix is not None:
                    @block.tensor
                    def _(pe):
                        def turn(i, s, n, pp, r):
                            if not own_row:
                                pe.wait_ge(load[s].sem, load[s].at((i + 1) * (16 * ninp)))
                            for g, m in pairs(r):
                                if own_row:
                                    pe.wait_ge(pre_ready[g].sem, pre_ready[g].at(n + 1))
                                pe.wait_ge(turned_sb[g].sem, turned_sb[g].at(n))
                                for q in range(m):
                                    for c in range(C2):
                                        z = (2 * q + c) * P
                                        last = pe.transpose(turn_ps[:, g, z:z + pp], inp[s][1][0:pp, 2 * g + q, c * P:(c + 1) * P], ident[0:pp, 0:pp])
                                last.then_inc(turned[g].sem, 1)

                        def multiply(i, s, n, pp, r):
                            for g, m in pairs(r):
                                pe.wait_ge(row_ready[g].sem, row_ready[g].at(n))
                                pe.wait_ge(turned_sb[g].sem, turned_sb[g].at(n + 1))
                                for q in range(m):
                                    if bias is not None:
                                        pe.matmul(out_ps[0:pp, g, q * D:(q + 1) * D], onesb[0:3, 0:pp], bias[:, :], start=True, stop=False)
                                    for c in range(C2):
                                        z = (2 * q + c) * P
                                        last = pe.matmul(out_ps[0:pp, g, q * D:(q + 1) * D], xT[:, s % 2, g, z:z + pp], matrix[:, c, :],
                                                         start=(bias is None and c == 0), stop=(c == C2 - 1))
                                last.then_inc(product[g].sem, 1)
                        batches(pe, (1, turn), (0, multiply))

                @block.scalar
                def _(act):
                    def copy_out(i, s, n, pp, r):
                        for g, m in pairs(r):
                            act.wait_ge(turned[g].sem, turned[g].at(n + 1))
                            if not isinstance(n, int) or n > 0:
                                act.wait_ge(product[g].sem, product[g].at(n - 1))
                            if pp == P:
                                last = act.copy(xT[:, s % 2, g, 0:m * D], turn_ps[:, g, 0:m * D])
                            else:
                                last = act.copy(xT[:, s % 2, g, 0:m * D].rearrange("p (z q) -> p z q", q=P)[:, :, 0:pp],
                                                turn_ps[:, g, 0:m * D].rearrange("p (z q) -> p z q", q=P)[:, :, 0:pp])
                            last.then_inc(turned_sb[g].sem, 1)

                    def deviate(i, s, n, pp, r):
                        act.wait_ge(var_ready.sem, var_ready.at(n + 1))
                        act.activation(dev[0:pp, s, 0:r], mv[0:pp, s, 0:r, 1], ACT.Sqrt, bias=eps[0:pp, :]).then_inc(deviation.sem, 1)

                    def normalise(i, s, n, pp, r):
                        act.wait_ge(acc_ready[s].sem, acc_ready[s].at(i + 1))
                        for q in range(r):
                            last = act.activation(u[s][0:pp, q, 0:D], u[s][0:pp, q, 0:D], ACT.Identity,
                                                  bias=scale[0:pp, s, q, 1:2], scale=scale[0:pp, s, q, 0:1])
                        last.then_inc(batch_out[s].sem, 1)

                    def relu(i, s, n, pp, r):
                        act.wait_ge(acc_ready[s].sem, acc_ready[s].at(i + 1))
                        act.activation(u[s][0:pp, 0:r, :], u[s][0:pp, 0:r, :], ACT.Relu).then_inc(batch_out[s].sem, 1)

                    def store(i, s, n, pp, r):
                        act.wait_ge(batch_out[s].sem, batch_out[s].at(i + 1))
                        act.nop(nofuse=True)
                        act.dma_start(view(target, n, pp, r), u[s][0:pp, 0:r, :].rearrange("p r d -> p (r d)")).then_inc(stored[s].sem, 16)
                        if kind == "gcn":
                            act.dma_start(view(att, n, pp, r), attb[0:pp, s, 0:r, :].rearrange("p r d -> p (r d)")).then_inc(stored[s].sem, 16)

                    if not norm:
                        batches(act, (2, copy_out), (0, relu), (0, store))
                    elif matrix is None:
                        batches(act, (1, deviate), (0, normalise), (0, store))
                    else:
                        batches(act, (3, copy_out), (1, deviate), (0, normalise), (0, store))
                    for s in range(BSLOTS):
                        act.wait_ge(stored[s].sem, stored[s].at(16 * n_store * rounds(s)))
                    if kind == "sage":
                        s = NBATCH % BSLOTS
                        act.wait_ge(acc_ready[s].sem, acc_ready[s].at(rounds(s)))
                        act.activation(cnt_nodes[:, :], cnt_nodes[:, :], ACT.Sqrt, bias=ones[:, 0:1]).then_inc(act_step.sem, 1)
                        act_step.close(1)

                @block.vector
                def _(dve):
                    def join(i, s, n, pp, r):
                        ag, own_in = inp[s][0], inp[s][1]
                        dve.wait_ge(load[s].sem, load[s].at((i + 1) * (16 * ninp)))
                        if kind == "gat":
                            dve.tensor_scalar(own[0:pp, s, 0:r], ag[0:pp, 0:r, D + 1], -1.0, 1.0, ALU.mult, ALU.add).then_inc(own_step.sem, 1)
                            dve.wait_ge(own_step.sem, own_step.at(n * 2 + 1))
                            dve.tensor_tensor(own[0:pp, s, 0:r], own[0:pp, s, 0:r], ag[0:pp, 0:r, D], ALU.add).then_inc(own_step.sem, 1)
                            dve.wait_ge(own_step.sem, own_step.at(n * 2 + 2))
                        for g, m in pairs(r):
                            for q in range(2 * g, 2 * g + m):
                                w = dinv[0:pp, bass.ds(n * R + q, 1)] if kind == "gcn" else own[0:pp, s, q:q + 1]
                                last = dve.scalar_tensor_tensor(own_in[0:pp, q, 0:D], own_in[0:pp, q, 0:D], w, ag[0:pp, q, 0:D], ALU.mult, ALU.add)
                            last.then_inc(pre_ready[g].sem, 1)

                    def combine(i, s, n, pp, r):
                        ag, us = inp[s][0], u[s]
                        if not own_row:
                            dve.wait_ge(load[s].sem, load[s].at((i + 1) * (16 * ninp)))
                        dve.wait_ge(stored[s].sem, stored[s].at(i * (16 * n_store)))
                        if kind == "sage":
                            dve.tensor_copy(cnt_nodes[0:pp, bass.ds(n * R, r)], ag[0:pp, 0:r, D])
                        if kind == "conv":
                            dve.nop(nofuse=True)
                            dve.tensor_copy(us[0:pp, 0:r, D], dinv[0:pp, bass.ds(n * R, r)])
                        for g, m in pairs(r):
                            a, b = 2 * g, 2 * g + m
                            o_ps = out_ps[0:pp, g, 0:m * D].rearrange("p (r d) -> p r d", d=D)
                            if matrix is not None:
                                dve.wait_ge(product[g].sem, product[g].at(n + 1))
                            if kind in ("sage", "rgcn1", "rgcn2"):
                                dve.tensor_tensor(us[0:pp, a:b, :], o_ps, ag[0:pp, a:b, 0:D], ALU.add).then_inc(row_ready[g].sem, 1)
                            if kind == "gcn":
                                for q in range(a, b):
                                    last = dve.scalar_tensor_tensor(us[0:pp, q, :], o_ps[:, q - a, :], dinv[0:pp, bass.ds(n * R + q, 1)],
                                                                    b_g1[0:pp, :], ALU.mult, ALU.add)
                                last.then_inc(row_ready[g].sem, 1)
                            if kind == "gat":
                                dve.scalar_tensor_tensor(us[0:pp, a:b, :], o_ps, 0.0, inp[s][2][0:pp, a:b, 0:D], ALU.max, ALU.add).then_inc(row_ready[g].sem, 1)
                            if kind == "conv":
                                dve.tensor_tensor(us[0:pp, a:b, 0:D], inp[s][1][0:pp, a:b, 0:D], ag[0:pp, a:b, 0:D], ALU.add).then_inc(row_ready[g].sem, 1)
                            if kind in ("sage", "rgcn2"):
                                dve.wait_ge(row_ready[g].sem, row_ready[g].at(n + 1))
                            if kind == "sage":
                                dve.scalar_tensor_tensor(us[0:pp, a:b, :], us[0:pp, a:b, :], 0.0, inp[s][1][0:pp, a:b, 0:D], ALU.max, ALU.add).then_inc(sum_ready[g].sem, 1)
                            if kind == "rgcn2":
                                dve.tensor_tensor(us[0:pp, a:b, :], us[0:pp, a:b, :], inp[s][2][0:pp, a:b, 0:D], ALU.add).then_inc(sum_ready[g].sem, 1)
                        c = sum_ready if kind in ("sage", "rgcn2") else row_ready
                        for g, m in pairs(r):
                            dve.wait_ge(c[g].sem, c[g].at(n + 1))
                            if kind == "rgcn1":
                                continue
                            for q in range(2 * g, 2 * g + m):
                                if norm:
                                    last = dve.bn_stats(stats[0:pp, s % 2, q, :], us[0:pp, q, 0:D])
                                    continue
                                for j, v in ((0, va), (1, vb)):
                                    last = dve.scalar_tensor_tensor(junk[0:pp, s % 2, q, j, :], us[0:pp, q, :], 0.0, v[0:pp, :], ALU.max, ALU.mult,
                                                                    accum_out=attb[0:pp, s, q, j:j + 1])
                        if kind == "rgcn1":
                            dve.sem_inc(acc_ready[s].sem, 1)
                        elif kind == "gcn":
                            last.then_inc(acc_ready[s].sem, 1)
                        else:
                            last.then_inc(stats_ready.sem, 1)
                            dve.wait_ge(stats_ready.sem, stats_ready.at(n + 1))
                            dve.nop(nofuse=True)
                            for q in range(r):
                                last = dve.bn_aggr(mv[0:pp, s, q, :], stats[0:pp, s % 2, q, :])
                            last.then_inc(var_ready.sem, 1)
                        dve.sem_inc(batch_done[s].sem, 1)

                    def means(i, s, n, pp, r):
                        dve.wait_ge(deviation.sem, deviation.at(n + 1))
                        dve.nop(nofuse=True)
                        dve.reciprocal(scale[0:pp, s, 0:r, 0], dev[0:pp, s, 0:r]).then_inc(rstd_ready.sem, 1)
                        dve.wait_ge(rstd_ready.sem, rstd_ready.at(n + 1))
                        dve.scalar_tensor_tensor(scale[0:pp, s, 0:r, 1], mv[0:pp, s, 0:r, 0], -1.0, scale[0:pp, s, 0:r, 0],
                                                 ALU.mult, ALU.mult).then_inc(acc_ready[s].sem, 1)

                    if kind == "sage":
                        link(dve, dve.memset(cnt_nodes[:, :], 0.0))
                    if kind == "conv":
                        for s in range(BSLOTS):
                            link(dve, dve.memset(u[s][:, :, D:DW], 0.0))
                    work = [(1, combine), (0, means)] if norm else [(0, combine)]
                    if own_row:
                        work = [(work[0][0] + 2, join)] + work
                    batches(dve, *work)
                    if kind == "sage":
                        dve.wait_ge(act_step.sem, act_step.base)
                        link(dve, dve.reciprocal(dinv[:, :], cnt_nodes[:, :]))

                for s in range(BSLOTS):
                    load[s].close(16 * ninp * rounds(s))
                    stored[s].close(16 * n_store * rounds(s))
                    for c in (batch_done, batch_out, acc_ready):
                        c[s].close(rounds(s))
                for g in range(PAIRS):
                    steps = NBATCH + (g == 0)
                    row_ready[g].close(steps)
                    if matrix is not None:
                        for c in (turned, turned_sb, product):
                            c[g].close(steps)
                    if own_row:
                        pre_ready[g].close(steps)
                    if kind in ("sage", "rgcn2"):
                        sum_ready[g].close(steps)
                if norm:
                    for c in (deviation, stats_ready, var_ready, rstd_ready):
                        c.close(NBATCH + 1)
                if kind == "gat":
                    own_step.close(2 * (NBATCH + 1))

        def one_hot_relations():
            with ExitStack() as tmp:
                hot = sb("hot_rel", [P, SLOTS, 96], BF16, tmp)
                ps = tmp.enter_context(nc.psum_tensor("ps_rel", [P, SLOTS, 1024], BF16))
                block = tmp.enter_context(nc.Block())

                @block.vector
                def _(dve):
                    with dve.Fori(0, ITERS) as i:
                        for k in range(SLOTS):
                            dve.wait_ge(turned[k].sem, turned[k].at(i))
                            dve.tensor_scalar(hot[:, k, :], rel_iota[:, :], ed.rel[:, bass.ds(i * SLOTS + k, 1)], None, ALU.is_equal).then_inc(msg_ready[k].sem, 1)

                @block.tensor
                def _(pe):
                    with pe.Fori(0, ITERS) as i:
                        for k in range(SLOTS):
                            pe.wait_ge(turned_sb[k].sem, turned_sb[k].at(i))
                            pe.wait_ge(msg_ready[k].sem, msg_ready[k].at(i + 1))
                            pe.transpose(ps[0:96, k, 0:P], hot[:, k, :], identb[:, :]).then_inc(turned[k].sem, 1)

                @block.scalar
                def _(act):
                    with act.Fori(0, ITERS) as i:
                        for k in range(SLOTS):
                            act.wait_ge(turned[k].sem, turned[k].at(i + 1))
                            act.copy(rel_hot[:, bass.ds((i * SLOTS + k) * P, P)], ps[0:96, k, 0:P]).then_inc(turned_sb[k].sem, 1)
                for k in range(SLOTS):
                    for c in (turned, turned_sb, msg_ready):
                        c[k].close(ITERS)

        def attention():
            BIG = 1e30
            with ExitStack() as tmp:
                rowa = sb("rowa", [P, SLOTS, 2, 2], F32, tmp)
                gidx = sb("gidx_att", [P, SLOTS, 2], I32, tmp)
                score = sb("score", [P, 2, T, 2], F32, tmp)
                e, es_, m, f, b, t1, pen, penn = (sb("att_" + n, [P, T], F32, tmp) for n in ("e", "es", "m", "f", "b", "t1", "pen", "penn"))
                diag = sb("att_diag", [P, 2, P], F32, tmp)
                col = sb("att_c", [P, 4], F32, tmp)
                msk = sb("att_msk", [P, P], F32, tmp)
                ps = tmp.enter_context(nc.psum_tensor("ps_att", [P, 4, 512], F32))
                marks = {}
                block = tmp.enter_context(nc.Block())

                @block.gpsimd
                def _(pool):
                    with pool.Fori(0, ITERS) as i:
                        for k in range(SLOTS):
                            pool.wait_ge(idx_ready[k].sem, idx_ready[k].at(i + 1))
                            pool.nop(nofuse=True)
                            for j in range(2):
                                pool.indirect_dma_start(
                                    out=rowa[:, k, j, :], out_offset=None, in_=att[:, :],
                                    in_offset=bass.IndirectOffsetOnAxis(ap=gidx[:, k, j:j + 1], axis=0),
                                    bounds_check=N - 1, oob_is_err=False).then_inc(gathered[k].sem, 16)

                @block.vector
                def _(dve):
                    for k in range(SLOTS):
                        dve.tensor_copy(gidx[:, k, 0:1], ed.gather[:, k:k + 1])
                        dve.tensor_copy(gidx[:, k, 1:2], ed.dst[:, k:k + 1]).then_inc(idx_ready[k].sem, 1)

                    def tile(i, k, more=True):
                        dve.wait_ge(gathered[k].sem, gathered[k].at(i * 32 + 32))
                        for j in range(2):
                            ins = dve.tensor_copy(score[:, j, bass.ds(i * SLOTS + k, 1), :].rearrange("p a f -> p (a f)"), rowa[:, k, j, :])
                        if more:
                            dve.tensor_copy(gidx[:, k, 0:1], ed.gather[:, bass.ds(i * SLOTS + SLOTS + k, 1)])
                            ins = dve.tensor_copy(gidx[:, k, 1:2], ed.dst[:, bass.ds(i * SLOTS + SLOTS + k, 1)])
                            ins.then_inc(idx_ready[k].sem, 1)
                    with dve.Fori(0, ITERS - 1) as i:
                        for k in range(SLOTS):
                            tile(i, k)
                    for k in range(SLOTS):
                        tile(ITERS - 1, k, more=False)
                    link(dve, dve.tensor_copy(col[:, :], part[:, :].broadcast_to([P, 4])))
                    for o_, j in ((e, 0), (es_, 1)):
                        link(dve, dve.tensor_tensor(t1[:, :], score[:, j, :, 0], score[:, 1, :, 1], ALU.add))
                        link(dve, dve.scalar_tensor_tensor(o_[:, :], t1[:, :], 0.2, t1[:, :], ALU.mult, ALU.max))
                    link(dve, dve.tensor_scalar(pen[:, :], ed.same[:, :], -1.0, BIG, ALU.add, ALU.mult))
                    link(dve, dve.tensor_scalar(penn[:, :], ed.samen[:, :], -1.0, BIG, ALU.add, ALU.mult))
                    link(dve, dve.tensor_tensor_scan(f[:, :], pen[:, :], e[:, :], -BIG, ALU.add, ALU.max))
                    link(dve, dve.tensor_tensor_scan(b[:, ::-1], penn[:, ::-1], e[:, ::-1], -BIG, ALU.add, ALU.max))
                    link(dve, dve.tensor_scalar(diag[:, 0, :], ident[:, :], f[:, T - 1:T], None, ALU.mult))
                    link(dve, dve.tensor_scalar(diag[:, 1, :], ident[:, :], b[:, 0:1], None, ALU.mult))
                    marks["diag"] = chain.base
                    link(dve, dve.tensor_tensor(m[:, :], f[:, :], b[:, :], ALU.max))
                    link(dve, dve.tensor_tensor(m[:, :], m[:, :], es_[:, :], ALU.max))
                    dve.wait_ge(pe_step.sem, pe_step.at(1))
                    for j, (mask, inside) in enumerate(((ed.back, ed.inhead), (ed.carry, ed.intail))):
                        link(dve, dve.tensor_scalar(msk[:, :], mask[:, :], -1.0, BIG, ALU.add, ALU.mult))
                        link(dve, dve.tensor_tensor(msk[:, :], msk[:, :], ps[:, j, 0:P], ALU.add))
                        link(dve, dve.tensor_reduce(col[:, j:j + 1], msk[:, :], AX.X, ALU.max))
                        link(dve, dve.tensor_scalar(t1[:, :], inside[:, :], -1.0, BIG, ALU.add, ALU.mult))
                        link(dve, dve.scalar_tensor_tensor(m[:, :], t1[:, :], col[:, j:j + 1], m[:, :], ALU.add, ALU.max))
                    link(dve, dve.tensor_tensor(e[:, :], e[:, :], m[:, :], ALU.subtract))
                    link(dve, dve.tensor_tensor(es_[:, :], es_[:, :], m[:, :], ALU.subtract))
                    marks["sub"] = chain.base
                    dve.wait_ge(act_step.sem, act_step.at(2))
                    link(dve, dve.tensor_tensor_scan(f[:, :], ed.same[:, :], e[:, :], 0.0, ALU.mult, ALU.add))
                    link(dve, dve.tensor_tensor_scan(b[:, ::-1], ed.samen[:, ::-1], e[:, ::-1], 0.0, ALU.mult, ALU.add))
                    marks["sums"] = chain.base
                    link(dve, dve.tensor_tensor(m[:, :], b[:, :], e[:, :], ALU.subtract))
                    link(dve, dve.tensor_tensor(m[:, :], m[:, :], f[:, :], ALU.add))
                    link(dve, dve.tensor_tensor(m[:, :], m[:, :], es_[:, :], ALU.add))
                    dve.wait_ge(pe_step.sem, pe_step.at(2))
                    link(dve, dve.tensor_copy(col[:, 2:4], ps[:, 2, 0:2]))
                    link(dve, dve.scalar_tensor_tensor(m[:, :], ed.inhead[:, :], col[:, 2:3], m[:, :], ALU.mult, ALU.add))
                    link(dve, dve.scalar_tensor_tensor(m[:, :], ed.intail[:, :], col[:, 3:4], m[:, :], ALU.mult, ALU.add))
                    link(dve, dve.tensor_scalar(m[:, :], m[:, :], 1e-16, None, ALU.add))
                    link(dve, dve.reciprocal(t1[:, :], m[:, :]))
                    link(dve, dve.tensor_tensor(w_rel[:, :], e[:, :], t1[:, :], ALU.mult))
                    link(dve, dve.tensor_tensor(t1[:, :], es_[:, :], t1[:, :], ALU.mult))
                    link(dve, dve.tensor_tensor(aux[:, :, 0], t1[:, :], ed.end[:, :], ALU.mult))
                    link(dve, dve.tensor_copy(aux[:, :, 1], ed.end[:, :]))

                @block.scalar
                def _(act):
                    act.wait_ge(chain.sem, marks["sub"])
                    act.activation(e[:, :], e[:, :], ACT.Exp).then_inc(act_step.sem, 1)
                    act.activation(es_[:, :], es_[:, :], ACT.Exp).then_inc(act_step.sem, 1)

                @block.tensor
                def _(pe):
                    pe.wait_ge(chain.sem, marks["diag"])
                    for j in range(2):
                        ins = pe.matmul(ps[:, j, 0:P], ones[:, :], diag[:, j, :], start=True, stop=True)
                    ins.then_inc(pe_step.sem, 1)
                    pe.wait_ge(chain.sem, marks["sums"])
                    pe.matmul(ps[:, 2, 0:1], ed.carry[:, :], f[:, T - 1:T], start=True, stop=True, skip_group_check=True)
                    pe.matmul(ps[:, 2, 1:2], ed.back[:, :], b[:, 0:1], start=True, stop=True, skip_group_check=True).then_inc(pe_step.sem, 1)
                for k in range(SLOTS):
                    idx_ready[k].close(ITERS)
                    gathered[k].close(32 * ITERS)
                pe_step.close(2)
                act_step.close(2)

        rel_scope = ctx.enter_context(ExitStack())
        rel_hot = sb("rel_hot", [96, T * P], BF16, rel_scope)
        one_hot_relations()
        edge_pass("e0", ed, x_in, D, agg_d, DW, ed.weight, matrix=mats["wl"], with_aux=True)
        node_pass("n0", ((agg_d, DW), (x_in, D)), x1, "sage", matrix=mats["wr"], bias=bias3["bl"])
        edge_pass("e1", ed, x1, D, agg_d, DW, w_rel, rel=rel_w[0])
        node_pass("n1", ((agg_d, DW), (x1, D)), y1, "rgcn1", matrix=mats["root1"], bias=bias3["bias1"])
        edge_pass("e2", ed, y1, D, agg_d, DW, w_rel, rel=rel_w[1])
        rel_scope.close()
        node_pass("n2", ((agg_d, DW), (y1, D), (x1, D)), x2, "rgcn2", matrix=mats["root2"], bias=bias3["bias2"])
        edge_pass("e3", es, x2, D, agg_s, D, es.weight, matrix=mats["l2"], bias=b_l2)
        node_pass("n3", ((agg_s, D), (x2, D)), x3, "conv")
        edge_pass("e4", ed, x3, DW, agg_d, DW, None)
        node_pass("n4", ((agg_d, DW), (x3, DW)), y3, "gcn", matrix=mats["g1"])
        attention()
        edge_pass("e5", ed, y3, D, agg_d, DW, w_rel, with_aux=True)
        node_pass("n5", ((agg_d, DW), (y3, D), (x3, DW)), out, "gat", matrix=mats["g2"], bias=bias3["b2"])


_INS = ["x", "src", "dst", "edge_type_16", "L0_gnn_W_l", "L0_gnn_b_l", "L0_gnn_W_r", "L1_gnn_W1", "L1_gnn_root1",
        "L1_gnn_bias1", "L1_gnn_W2", "L1_gnn_root2", "L1_gnn_bias2", "L2_gnn_W", "L2_gnn_b", "L3_gnn_W1",
        "L3_gnn_b1", "L3_gnn_W2", "L3_gnn_att_src", "L3_gnn_att_dst", "L3_gnn_b2"]


def kernel(**inputs):
    import numpy as _np
    import concourse.bacc as _bacc
    from concourse import mybir as _mybir
    from concourse.bass_utils import run_bass_kernel_spmd as _run

    nc = _bacc.Bacc("TRN2", target_bir_lowering=False, num_devices=1)
    arrays, aps = {}, {}
    for name in _INS:
        a = _np.ascontiguousarray(inputs[name])
        arrays[f"in_{name}_dram"] = a
        aps[name] = nc.dram_tensor(f"in_{name}_dram", a.shape, _mybir.dt.from_np(a.dtype), kind="ExternalInput").ap()
    out = nc.dram_tensor("out_0_dram", inputs["x"].shape, _mybir.dt.float32, kind="ExternalOutput").ap()
    gnn_kernel(nc, aps, out)
    r = _run(nc, [arrays], core_ids=[0])
    return r.results[0]["out_0_dram"]
```

```python
from contextlib import ExitStack

import concourse.bass as bass
from concourse import mybir

F32 = mybir.dt.float32
BF16 = mybir.dt.bfloat16
I32 = mybir.dt.int32
ALU = mybir.AluOpType
ACT = mybir.ActivationFunctionType
AX = mybir.AxisListType

P = 128
SLOTS = 8
BSLOTS = 4
R = 6
PAIRS = R // 2
EPS = 1e-5
FAR = 1000000.0
RELS = 16


class Counter:

    def __init__(self, sem):
        self.sem = sem
        self.base = 0

    def at(self, n):
        return n + self.base

    def close(self, steps):
        self.base += steps


def gnn_kernel(nc, A, out):
    x_in = A["x"]
    N, D = x_in.shape
    E = A["src"].shape[0]
    T = -(-E // (P * SLOTS)) * SLOTS
    EP = P * T
    FULLP = E // T
    RESTE = E - FULLP * T
    assert D == 256 and T % SLOTS == 0 and N < 256 * 256
    ITERS = T // SLOTS
    AUX = 4
    DW = D + AUX
    BATCH = P * R
    NBATCH = N // BATCH
    REST = N - NBATCH * BATCH
    assert 0 < REST <= P
    NT = NBATCH * R + 1
    C2 = D // P

    ctx = ExitStack()
    with ctx:
        def sb(name, shape, dt=F32, stack=ctx):
            return stack.enter_context(nc.sbuf_tensor(name, shape, dt))

        def counter(name):
            return Counter(ctx.enter_context(nc.semaphore(name)))

        def dram(name, shape, dt=F32):
            return nc.dram_tensor(name, shape, dt, kind="Internal").ap()

        sorted_lo = [dram(f"sorted_lo{j}", [EP + 2, 4]) for j in range(2)]
        first_round = dram("first_round", [2 * SLOTS, 4])
        by_dst = dram("by_dst", [EP + 2, 4])
        by_src = dram("by_src", [EP + 2, 4])
        seg_d = dram("seg_d", [EP + P, DW])
        seg_s = dram("seg_s", [EP + P, D])
        ends_d = dram("all_ends_d", [2 * P * 256, 1], I32)
        ends_s = dram("all_ends_s", [2 * P * 256, 1], I32)
        x1 = dram("x1", [N, D])
        y1 = dram("y1", [N, D])
        x2 = dram("x2", [N, D])
        x3 = dram("x3", [N, DW])
        y3 = dram("y3", [N, D])

        ident = sb("ident", [P, P])
        identb = sb("identb", [P, P], BF16)
        lower = sb("lower", [P, P])
        lowerb = sb("lowerb", [P, P], BF16)
        upper = sb("upper", [P, P])
        restb = sb("restb", [P, P], BF16)
        ones = sb("ones", [P, P])
        onesb = sb("onesb", [P, P], BF16)
        iota = sb("iota", [P, D], BF16)
        rel_iota = sb("rel_iota", [P, 96], BF16)
        part = sb("part", [P, 1])
        zero_b = sb("zero_b", [P, D], BF16)
        mats = {n: sb("w_" + n, [P, C2, D]) for n in ("wl", "wr", "root1", "root2", "l2", "g1", "g2")}
        rel_w = [sb(f"rel_w{i}", [96, 1024], BF16) for i in range(2)]
        bias3 = {n: sb("b_" + n, [3, D], BF16) for n in ("bias2", "b2")}
        b_l0 = sb("b_l0", [P, DW])
        no_sum = sb("no_sum", [P, DW])
        b_l1 = sb("b_l1", [P, D])
        b_l2 = sb("b_l2", [P, D])
        b_g1 = sb("b_g1", [P, D])
        va = sb("va", [P, D])
        vb = sb("vb", [P, D])
        eps_col = sb("eps_col", [P, 2])
        cnt_nodes = sb("cnt_nodes", [P, NT])
        dinv = sb("dinv", [P, NT])

        class Edges:
            pass
        ed, es = Edges(), Edges()
        for o, s in ((ed, "d"), (es, "s")):
            o.same = sb("same_" + s, [P, T])
            o.gather = sb("gather_" + s, [P, T], I32)
            o.ends = sb("ends_" + s, [P, NT], I32)
            o.head = sb("head_" + s, [P, 1], I32)
            o.carry = sb("carry_" + s, [P, P])
            o.weight = sb("weight_" + s, [P, T])
        ed.samen = sb("samen", [P, T])
        ed.end = sb("end", [P, T])
        ed.inhead = sb("inhead", [P, T])
        ed.intail = sb("intail", [P, T])
        ed.back = sb("back", [P, P])
        ed.dst = sb("dst_idx", [P, T], I32)
        ed.rel = sb("rel", [P, T])
        w_rel = sb("w_rel", [P, T])
        aux = sb("aux", [P, T, AUX])

        load = [counter(f"load{i}") for i in range(4)]
        put_head = counter("put_head")
        stored = [counter(f"stored{i}") for i in range(SLOTS)]
        idx_ready = [counter(f"idx_ready{k}") for k in range(SLOTS)]
        gathered = [counter(f"gathered{k}") for k in range(SLOTS)]
        scattered = [counter(f"scattered{k}") for k in range(SLOTS)]
        msg_ready = [counter(f"msg_ready{k}") for k in range(SLOTS)]
        acc_ready = [counter(f"acc_ready{k}") for k in range(SLOTS)]
        row_ready = [counter(f"row_ready{k}") for k in range(SLOTS)]
        relw_ready = [counter(f"relw_ready{k}") for k in range(SLOTS)]
        prod_ready = [counter(f"prod_ready{k}") for k in range(SLOTS)]
        turned = [counter(f"turned{k}") for k in range(SLOTS)]
        turned_sb = [counter(f"turned_sb{k}") for k in range(SLOTS)]
        product = [counter(f"product{k}") for k in range(SLOTS)]
        pre_ready = [counter(f"pre_ready{k}") for k in range(PAIRS)]
        batch_done = [counter(f"batch_done{k}") for k in range(BSLOTS)]
        batch_out = [counter(f"batch_out{k}") for k in range(BSLOTS)]
        sum_ready = [counter(f"sum_ready{k}") for k in range(PAIRS)]
        stats_ready = counter("stats_ready")
        var_ready = counter("var_ready")
        rstd_ready = counter("rstd_ready")
        chain = counter("chain")
        pe_step = counter("pe_step")
        act_step = counter("act_step")
        pool_step = counter("pool_step")
        ready = counter("ready")
        cleared = counter("cleared")
        own_step = counter("own_step")
        ends_ready = counter("ends_ready")
        deviation = counter("deviation")

        def link(eng, ins):
            chain.close(1)
            ins.then_inc(chain.sem, 1)
            eng.wait_ge(chain.sem, chain.base)

        with ExitStack() as tmp:
            w_raw = sb("w_raw", [P, 2, C2, D], F32, tmp)
            att_col = sb("att_col", [P, 2, C2], F32, tmp)
            att_bc = sb("att_bc", [P, 2, C2, P], F32, tmp)
            w2t = sb("w2t", [P, C2, D], F32, tmp)
            rel_raw = sb("rel_raw", [96, 2, 1024], F32, tmp)
            rel_hi = sb("rel_hi", [96, 2, 1024], BF16, tmp)
            rel_mid = sb("rel_mid", [96, 2, 1024], BF16, tmp)
            rel_lo = sb("rel_lo", [96, 2, 1024], BF16, tmp)
            b_raw = sb("b_raw", [3, 2, D], F32, tmp)
            b_part = sb("b_part", [3, 3, 2, D], BF16, tmp)
            sel = sb("sel", [P, 6], F32, tmp)
            tp = tmp.enter_context(nc.psum_tensor("tp", [P, 4, 512], F32))
            bc = tmp.enter_context(nc.psum_tensor("bc", [P, 2, 512], F32))

            names = ("bias2", "b2")
            b_dram = (A["L1_gnn_bias2"], A["L3_gnn_b2"])
            plain = {"root1": "L1_gnn_root1", "root2": "L1_gnn_root2", "l2": "L2_gnn_W",
                     "g1": "L3_gnn_W1", "g2": "L3_gnn_W2"}
            block = tmp.enter_context(nc.Block())

            @block.sync
            def _(sp):
                loads = 0
                for i, n in enumerate(("L0_gnn_W_l", "L0_gnn_W_r")):
                    sp.dma_start(w_raw[:, i], A[n].rearrange("(c p) n -> p c n", p=P)).then_inc(load[0].sem, 16)
                    loads += 1
                for n, src in plain.items():
                    sp.dma_start(mats[n][:, :, :], A[src].rearrange("(c p) n -> p c n", p=P)).then_inc(load[0].sem, 16)
                    loads += 1
                for i, n in enumerate(("L3_gnn_att_src", "L3_gnn_att_dst")):
                    for c in range(C2):
                        sp.dma_start(att_col[:, i, c:c + 1], A[n][c * P:(c + 1) * P].rearrange("(p a) -> p a", a=1)).then_inc(load[0].sem, 16)
                        loads += 1
                sp.dma_start(b_l0[:, 0:D], A["L0_gnn_b_l"].rearrange("(a d) -> a d", a=1).broadcast_to([P, D])).then_inc(load[0].sem, 16)
                sp.dma_start(b_l1[:, :], A["L1_gnn_bias1"].rearrange("(a d) -> a d", a=1).broadcast_to([P, D])).then_inc(load[0].sem, 16)
                sp.dma_start(b_l2[:, :], A["L2_gnn_b"].rearrange("(a d) -> a d", a=1).broadcast_to([P, D])).then_inc(load[0].sem, 16)
                sp.dma_start(b_g1[:, :], A["L3_gnn_b1"].rearrange("(a d) -> a d", a=1).broadcast_to([P, D])).then_inc(load[0].sem, 16)
                loads += 4
                for i in range(2):
                    for k in range(3):
                        sp.dma_start(b_raw[k:k + 1, i, :], b_dram[i].rearrange("(a d) -> a d", a=1)).then_inc(load[0].sem, 16)
                        loads += 1
                sp.wait_ge(pool_step.sem, 1)
                for i, n in enumerate(("L1_gnn_W1", "L1_gnn_W2")):
                    for k in range(3):
                        for j in range(4):
                            sp.dma_start(rel_raw[32 * k:32 * k + RELS, i, j * D:(j + 1) * D].rearrange("r (b o) -> r b o", o=4),
                                         A[n].rearrange("r b i o -> i r b o")[j]).then_inc(load[1].sem, 16)
                load[0].close(16 * loads)
                load[1].close(16 * 24)

            @block.gpsimd
            def _(pool):
                pool.memset(rel_raw[:, :, :], 0.0).then_inc(pool_step.sem, 1)
                pool.memset(ones[:, :], 1.0)
                pool.memset(onesb[:, :], 1.0)
                pool.memset(eps_col[:, 0:1], EPS / 4)
                pool.memset(eps_col[:, 1:2], EPS)
                pool.memset(zero_b[:, :], 0.0)
                pool.memset(no_sum[:, :], 0.0)
                pool.memset(b_l0[:, D:DW], 0.0)
                pool.iota(iota[:, :], [[1, D]], base=0, channel_multiplier=0, allow_small_or_imprecise_dtypes=True)
                pool.iota(rel_iota[:, :], [[0, 3], [1, 32]], base=0, channel_multiplier=0, allow_small_or_imprecise_dtypes=True)
                pool.iota(part[:, :], [[0, 1]], base=0, channel_multiplier=1, allow_small_or_imprecise_dtypes=True).then_inc(pool_step.sem, 1)
                pool.wait_ge(pool_step.sem, 2)
                pool.affine_select(ident[:, :], ones[:, :], [[-1, P]], ALU.is_equal, 0.0, base=0, channel_multiplier=1)
                pool.affine_select(identb[:, :], onesb[:, :], [[-1, P]], ALU.is_equal, 0.0, base=0, channel_multiplier=1)
                pool.affine_select(lower[:, :], ones[:, :], [[1, P]], ALU.is_gt, 0.0, base=0, channel_multiplier=-1)
                pool.affine_select(lowerb[:, :], onesb[:, :], [[1, P]], ALU.is_gt, 0.0, base=0, channel_multiplier=-1)
                pool.affine_select(restb[:, :], onesb[:, :], [[-1, P]], ALU.is_ge, 0.0, base=0, channel_multiplier=1)
                pool.affine_select(upper[:, :], ones[:, :], [[-1, P]], ALU.is_gt, 0.0, base=0, channel_multiplier=1).then_inc(pool_step.sem, 1)
            pool_step.close(3)

            @block.vector
            def _(dve):
                dve.wait_ge(pool_step.sem, 3)
                for k in range(3):
                    link(dve, dve.tensor_scalar(sel[:, k:k + 1], part[:, :], float(k), None, ALU.is_equal))
                    link(dve, dve.tensor_scalar(sel[:, 3 + k:4 + k], part[:, :], 32.0 * k, None, ALU.is_ge))
                for k in range(2):
                    link(dve, dve.tensor_tensor(sel[:, 3 + k:4 + k], sel[:, 3 + k:4 + k], sel[:, 4 + k:5 + k], ALU.subtract))
                dve.wait_ge(load[0].sem, load[0].base)
                link(dve, dve.tensor_scalar(w_raw[:, :, :, :], w_raw[:, :, :, :], 0.5, None, ALU.mult))
                link(dve, dve.tensor_scalar(b_l0[:, 0:D], b_l0[:, 0:D], 0.5, None, ALU.mult))
                for i in range(2):
                    for c in range(C2):
                        link(dve, dve.tensor_scalar(att_bc[:, i, c, :], ones[:, :], att_col[:, i, c:c + 1], None, ALU.mult))
                ready.close(1)
                dve.nop().then_inc(ready.sem, 1)
                link(dve, dve.tensor_copy(b_part[:, 0], b_raw[:, :, :]))
                link(dve, dve.tensor_tensor(b_raw[:, :, :], b_raw[:, :, :], b_part[:, 0], ALU.subtract))
                link(dve, dve.tensor_copy(b_part[:, 1], b_raw[:, :, :]))
                link(dve, dve.tensor_tensor(b_raw[:, :, :], b_raw[:, :, :], b_part[:, 1], ALU.subtract))
                link(dve, dve.tensor_copy(b_part[:, 2], b_raw[:, :, :]))
                for i, n in enumerate(names):
                    o = bias3[n][:, :]
                    link(dve, dve.tensor_scalar(o, b_part[:, 0, i, :], sel[0:3, 0:1], None, ALU.mult))
                    for k in (1, 2):
                        link(dve, dve.scalar_tensor_tensor(o, b_part[:, k, i, :], sel[0:3, k:k + 1], o, ALU.mult, ALU.add))
                dve.wait_ge(load[1].sem, load[1].base)
                link(dve, dve.tensor_copy(rel_hi[:, :, :], rel_raw[:, :, :]))
                link(dve, dve.tensor_tensor(rel_raw[:, :, :], rel_raw[:, :, :], rel_hi[:, :, :], ALU.subtract))
                link(dve, dve.tensor_copy(rel_mid[:, :, :], rel_raw[:, :, :]))
                link(dve, dve.tensor_tensor(rel_raw[:, :, :], rel_raw[:, :, :], rel_mid[:, :, :], ALU.subtract))
                link(dve, dve.tensor_copy(rel_lo[:, :, :], rel_raw[:, :, :]))
                for i in range(2):
                    o = rel_w[i][:, :]
                    link(dve, dve.tensor_scalar(o, rel_hi[:, i, :], sel[0:96, 3:4], None, ALU.mult))
                    for k, part_k in ((1, rel_mid), (2, rel_lo)):
                        link(dve, dve.scalar_tensor_tensor(o, part_k[:, i, :], sel[0:96, 3 + k:4 + k], o, ALU.mult, ALU.add))
                for i, o in enumerate((mats["wl"], mats["wr"], w2t)):
                    dve.wait_ge(pe_step.sem, 1 + i)
                    for c in range(C2):
                        link(dve, dve.tensor_copy(o[:, c, :], tp[:, c, 0:D]))
                dve.wait_ge(pe_step.sem, 4)
                link(dve, dve.tensor_copy(va[:, :], bc[:, 0, 0:D]))
                link(dve, dve.tensor_copy(vb[:, :], bc[:, 1, 0:D]))

            @block.tensor
            def _(pe):
                pe.wait_ge(ready.sem, ready.base)
                done = chain.base - 2 - 6
                srcs = (lambda j, c: w_raw[:, 0, j, c * P:(c + 1) * P],
                        lambda j, c: w_raw[:, 1, j, c * P:(c + 1) * P],
                        lambda j, c: mats["g2"][:, j, c * P:(c + 1) * P])
                for i, s in enumerate(srcs):
                    if i:
                        pe.wait_ge(chain.sem, done + 2 * i)
                    for j in range(C2):
                        for c in range(C2):
                            ins = pe.transpose(tp[:, c, j * P:(j + 1) * P], s(j, c), ident[:, :])
                    ins.then_inc(pe_step.sem, 1)
                pe.wait_ge(chain.sem, done + 6)
                for i in range(2):
                    for c in range(C2):
                        ins = pe.matmul(bc[:, i, 0:D], att_bc[:, i, c, :], w2t[:, c, :], start=(c == 0), stop=(c == C2 - 1))
                ins.then_inc(pe_step.sem, 1)
                pe_step.close(4)

        primed_dma = scattered
        primed = [c for group in (idx_ready, msg_ready, acc_ready, row_ready, turned, turned_sb, product,
                                  pre_ready, relw_ready, prod_ready, batch_done, batch_out) for c in group]
        with ExitStack() as tmp:
            edge_key = sb("edge_key", [1, 4], F32, tmp)
            block = tmp.enter_context(nc.Block())

            @block.vector
            def _(dve):
                dve.memset(edge_key[:, :], -1.0).then_inc(ready.sem, 1)

            @block.gpsimd
            def _(pool):
                pool.wait_ge(ready.sem, ready.at(1))
                for k, c in enumerate(primed_dma):
                    pool.dma_start(first_round[k:k + 1, :], edge_key[:, :]).then_inc(c.sem, 16)
                for c in primed_dma:
                    pool.wait_ge(c.sem, 16)
                    c.close(16)

            @block.scalar
            def _(act):
                for c in primed:
                    act.sem_inc(c.sem, 1)
                    c.close(1)

            @block.sync
            def _(sp):
                sp.wait_ge(ready.sem, ready.at(1))
                for k, c in enumerate(stored):
                    sp.dma_start(first_round[SLOTS + k:SLOTS + k + 1, :], edge_key[:, :]).then_inc(c.sem, 16)
                for a in (by_dst, by_src):
                    for r in (0, EP + 1):
                        sp.dma_start(a[r:r + 1, :], edge_key[:, :]).then_inc(cleared.sem, 16)
                for c in stored:
                    sp.wait_ge(c.sem, 16)
                    c.close(16)
                sp.dma_start(seg_s[EP:EP + P, :], no_sum[:, 0:D]).then_inc(cleared.sem, 16)
                sp.wait_ge(cleared.sem, cleared.at(80))
            cleared.close(80)
            ready.close(1)

        LISTS = 2
        TURNS = SLOTS // LISTS
        ORDER = [(t, j) for t in range(TURNS) for j in range(LISTS)]
        assert T % TURNS == 0

        TH = T // 2
        assert T % 2 == 0 and TH <= P and T <= 256
        base_hi = sb("base_hi", [P, LISTS, D])

        def sort_pass(name, digit, targets):
            columns = (A["dst"], A["src"], A["edge_type_16"])
            count_hot_ready = msg_ready
            hot_ready = turned
            hot_used = product
            places_ready = acc_ready
            rank_ready = turned_sb
            record_ready = row_ready
            to_ready = relw_ready
            with ExitStack() as tmp:
                rec = sb(f"rec_{name}", [P, LISTS, T, 4], F32, tmp)
                key = sb(f"key_{name}", [P, LISTS, T], I32, tmp)
                dig_i = sb(f"digi_{name}", [P, LISTS, T], I32, tmp)
                dig = sb(f"dig_{name}", [P, LISTS, T], F32, tmp)
                hot = sb(f"hot_{name}", [P, SLOTS, D], BF16, tmp)
                junk = sb(f"junk_{name}", [P, LISTS, D], F32, tmp)
                rank = sb(f"rank_{name}", [P, SLOTS], F32, tmp)
                to = sb(f"to_{name}", [P, SLOTS], I32, tmp)
                out_rec = sb(f"outrec_{name}", [P, SLOTS, 4], F32, tmp)
                ph = tmp.enter_context(nc.psum_tensor(f"ph_{name}", [P, LISTS, 3, 512], F32))
                if digit:
                    stage = sb("stage", [P, LISTS, 2, P * 4], F32, tmp)
                else:
                    raw = sb("raw", [P, 3, T], I32, tmp)
                    dig_upper = sb("dig_upper", [P, LISTS, T], F32, tmp)
                    hot_upper = sb("hot_upper", [P, SLOTS, D], BF16, tmp)
                    total = sb("total", [P, 2, LISTS, D], F32, tmp)
                    base_lo = sb("base_lo", [P, LISTS, D], F32, tmp)
                    diag = sb("total_diag", [P, LISTS * 2, P], F32, tmp)
                    count = sb("count", [P, LISTS * 2, 256], F32, tmp)
                    upto = sb("upto", [P, LISTS * 2, 256], F32, tmp)
                    part_total = sb("part_total", [P, LISTS * 2, 1], F32, tmp)
                    end_row = sb("end_row", [P, LISTS * 2, 256], I32, tmp)
                    pn = tmp.enter_context(nc.psum_tensor("pn", [P, LISTS, 512], F32))
                n_load = 2 * LISTS if digit else 3 * (1 + (RESTE > 0))
                ROUNDS = T // TURNS
                counting = 0 if digit else ROUNDS
                marks = {}
                block = tmp.enter_context(nc.Block())

                @block.sync
                def _(sp):
                    if digit:
                        for j in range(LISTS):
                            for c in range(2):
                                sp.dma_start(stage[0:TH, j, c, :], sorted_lo[j][1:EP + 1, :].rearrange("(c q p) f -> c q (p f)", c=2, p=P)[c]).then_inc(load[0].sem, 16)
                    else:
                        sp.wait_ge(ready.sem, ready.at(1))
                        for i, src in enumerate(columns):
                            sp.dma_start(raw[0:FULLP, i, :], src[0:FULLP * T].rearrange("(p t) -> p t", t=T)).then_inc(load[0].sem, 16)
                            if RESTE:
                                sp.dma_start(raw[FULLP:FULLP + 1, i, 0:RESTE], src[FULLP * T:E].rearrange("(a t) -> a t", a=1)).then_inc(load[0].sem, 16)
                        sp.wait_ge(ends_ready.sem, ends_ready.at(1))
                        for j, e in enumerate((ends_d, ends_s)):
                            for h in range(2):
                                sp.dma_start(e[h * P * 256:(h + 1) * P * 256, :].rearrange("(p c) a -> p (c a)", p=P), end_row[:, 2 * j + h, :]).then_inc(cleared.sem, 16)
                        sp.wait_ge(cleared.sem, cleared.at(64))
                        for o, e in ((ed, ends_d), (es, ends_s)):
                            sp.dma_start(o.ends[:, 0:NBATCH * R].rearrange("p (n r) -> p n r", r=R),
                                         e[0:NBATCH * BATCH, :].rearrange("(n p r) a -> p n (r a)", p=P, r=R)).then_inc(cleared.sem, 16)
                            sp.dma_start(o.ends[0:REST, NT - 1:NT], e[NBATCH * BATCH:N, :]).then_inc(cleared.sem, 16)
                        sp.wait_ge(cleared.sem, cleared.at(64 + 64))
                load[0].close(16 * n_load)
                if not digit:
                    cleared.close(64 + 64)

                @block.vector
                def _(dve):
                    if not digit:
                        dve.memset(raw[:, 2, :], 0)
                        dve.memset(rec[:, :, :, 3:4], 0.0)
                        dve.memset(raw[:, 0:2, :], N).then_inc(ready.sem, 1)
                    else:
                        dve.memset(rec[:, :, :, 3:4], 0.0)
                        dve.wait_ge(pe_step.sem, pe_step.at(1))
                        for f in range(3):
                            link(dve, dve.tensor_copy(rec[:, :, :, f], ph[:, :, f, 256:256 + T]))
                    if not digit:
                        dve.wait_ge(load[0].sem, load[0].base)
                        for j in range(LISTS):
                            for f, i in enumerate((j, 1 - j, 2)):
                                link(dve, dve.tensor_copy(rec[:, j, :, f], raw[:, i, :]))
                            link(dve, dve.tensor_scalar(rec[:, j, :, 1], rec[:, j, :, 1], float(N - 1), None, ALU.min))
                    link(dve, dve.tensor_copy(key[:, :, :], rec[:, :, :, 0]))
                    op, by = (ALU.logical_shift_right, 8) if digit else (ALU.bitwise_and, 255)
                    link(dve, dve.tensor_scalar(dig_i[:, :, :], key[:, :, :], by, None, op))
                    link(dve, dve.tensor_copy(dig[:, :, :], dig_i[:, :, :]))
                    if not digit:
                        link(dve, dve.tensor_scalar(dig_i[:, :, :], key[:, :, :], 8, None, ALU.logical_shift_right))
                        link(dve, dve.tensor_copy(dig_upper[:, :, :], dig_i[:, :, :]))
                    marks["records"] = chain.base

                    def one_hot(i, t, j, c):
                        k = j * TURNS + t
                        dve.tensor_scalar(hot[:, k, :], iota[:, :], dig[:, j, bass.ds(i * TURNS + t, 1)], None, ALU.is_equal).then_inc(c[k].sem, 1)

                    if not digit:
                        with dve.Fori(0, ROUNDS) as i:
                            for t, j in ORDER:
                                k = j * TURNS + t
                                dve.wait_ge(hot_used[k].sem, hot_used[k].at(i))
                                dve.tensor_scalar(hot_upper[:, k, :], iota[:, :], dig_upper[:, j, bass.ds(i * TURNS + t, 1)], None, ALU.is_equal)
                                one_hot(i, t, j, count_hot_ready)
                        dve.wait_ge(pe_step.sem, pe_step.at(1))
                        link(dve, dve.tensor_copy(count[:, :, :].rearrange("p (j h) d -> p j (h d)", h=2), pn[:, :, :]))
                        for b in range(LISTS * 2):
                            link(dve, dve.tensor_tensor_scan(upto[:, b, :], ones[:, 0:1].broadcast_to([P, 256]), count[:, b, :], 0.0, ALU.mult, ALU.add))
                        link(dve, dve.tensor_copy(part_total[:, :, :], upto[:, :, 255:256]))
                        for b in range(LISTS * 2):
                            link(dve, dve.tensor_scalar(diag[:, b, :], ident[:, :], part_total[:, b, :], None, ALU.mult))
                        marks["totals"] = chain.base
                        dve.wait_ge(pe_step.sem, pe_step.at(2))
                        for h, base in ((0, base_lo), (1, base_hi)):
                            link(dve, dve.tensor_copy(total[:, h, :, :], ph[:, :, 1 + h, 0:D]))
                            for j in range(LISTS):
                                link(dve, dve.tensor_tensor_scan(base[:, j, :], ones[:, 0:1].broadcast_to([P, D]), total[:, h, j, :], 1.0, ALU.mult, ALU.add))
                            link(dve, dve.tensor_tensor(base[:, :, :], base[:, :, :], total[:, h, :, :], ALU.subtract))
                        for j in range(LISTS):
                            for h in range(2):
                                b = 2 * j + h
                                link(dve, dve.tensor_scalar(upto[:, b, :], upto[:, b, :], ph[:, j, 0, h:h + 1], -1.0, ALU.add, ALU.add))
                        link(dve, dve.tensor_scalar(part_total[:, 0, :], part[:, :], float(EP), None, ALU.add))
                        link(dve, dve.tensor_scalar(upto[:, :, :], upto[:, :, :], part_total[:, 0, :], None, ALU.subtract))
                        link(dve, dve.tensor_scalar(count[:, :, :], count[:, :, :], 0.0, None, ALU.is_gt))
                        link(dve, dve.tensor_tensor(upto[:, :, :], upto[:, :, :], count[:, :, :], ALU.mult))
                        link(dve, dve.tensor_scalar(end_row[:, :, :], upto[:, :, :], part_total[:, 0, :], None, ALU.add))
                        dve.sem_inc(ends_ready.sem, 1)
                        marks["base"] = chain.base
                    with dve.Fori(0, ROUNDS) as i:
                        for t in range(TURNS):
                            for j in range(LISTS):
                                k = j * TURNS + t
                                dve.wait_ge(hot_used[k].sem, hot_used[k].at(i + counting))
                                one_hot(i, t, j, hot_ready)
                            for j in range(LISTS):
                                k = j * TURNS + t
                                dve.wait_ge(places_ready[k].sem, places_ready[k].at(i + 1))
                                dve.wait_ge(to_ready[k].sem, to_ready[k].at(i))
                                dve.scalar_tensor_tensor(junk[:, j, :], ph[:, j, 0, 0:D], 1.0, hot[:, k, :], ALU.mult, ALU.mult, accum_out=rank[:, k:k + 1]).then_inc(rank_ready[k].sem, 1)

                if not digit:
                    ready.close(1)
                    ends_ready.close(1)

                @block.scalar
                def _(act):
                    act.wait_ge(chain.sem, marks["records"])
                    with act.Fori(0, ROUNDS) as i:
                        for t, j in ORDER:
                            k = j * TURNS + t
                            act.wait_ge(scattered[k].sem, scattered[k].at(i * 16))
                            act.copy(out_rec[:, k, :], rec[:, j, bass.ds(i * TURNS + t, 1), :].rearrange("p a f -> p (a f)")).then_inc(record_ready[k].sem, 1)
                            act.wait_ge(rank_ready[k].sem, rank_ready[k].at(i + 1))
                            act.copy(to[:, k:k + 1], rank[:, k:k + 1]).then_inc(to_ready[k].sem, 1)

                def both(a):
                    return a[:, :].rearrange("p (a d) -> p a d", a=1).broadcast_to([P, 2, D])

                @block.tensor
                def _(pe):
                    if digit:
                        pe.wait_ge(load[0].sem, load[0].base)
                        for j in range(LISTS):
                            for f in range(3):
                                for c in range(2):
                                    ins = pe.transpose(ph[:, j, f, 256 + c * TH:256 + (c + 1) * TH], stage[0:TH, j, c, f:4 * P:4], ident[0:TH, 0:TH])
                        ins.then_inc(pe_step.sem, 1)
                        pe.wait_ge(chain.sem, marks["records"])
                    else:
                        for j in range(LISTS):
                            pe.matmul(pn[:, j, :], identb[:, :], both(zero_b), start=True, stop=False)
                        with pe.Fori(0, ROUNDS) as i:
                            for t, j in ORDER:
                                k = j * TURNS + t
                                pe.wait_ge(count_hot_ready[k].sem, count_hot_ready[k].at(i + 1))
                                for h in range(2):
                                    ins = pe.matmul(pn[:, j, h * 256:(h + 1) * 256], hot_upper[:, k, h * P:(h + 1) * P], hot[:, k, :], start=False, stop=False)
                                ins.then_inc(hot_used[k].sem, 1)
                        for j in range(LISTS):
                            ins = pe.matmul(pn[:, j, :], identb[:, :], both(zero_b), start=False, stop=True)
                        ins.then_inc(pe_step.sem, 1)
                        pe.wait_ge(chain.sem, marks["totals"])
                        for j in range(LISTS):
                            pe.matmul(ph[:, j, 0, 0:1], lower[:, :], part_total[:, 2 * j, :], start=True, stop=True)
                            pe.matmul(ph[:, j, 0, 1:2], lower[:, :], part_total[:, 2 * j + 1, :], start=True, stop=False)
                            pe.matmul(ph[:, j, 0, 1:2], ones[:, :], part_total[:, 2 * j, :], start=False, stop=True)
                            for h in range(2):
                                pe.matmul(ph[:, j, 1, 0:D], ones[:, :], count[:, 2 * j + h, :], start=(h == 0), stop=(h == 1))
                            for h in range(2):
                                ins = pe.matmul(ph[:, j, 2, h * P:(h + 1) * P], ones[:, :], diag[:, 2 * j + h, :], start=True, stop=True)
                        ins.then_inc(pe_step.sem, 1)
                        pe.wait_ge(chain.sem, marks["base"])
                    for j in range(LISTS):
                        pe.matmul(ph[:, j, 0, 0:D], ident[:, :], (base_hi if digit else base_lo)[:, j, :], start=True, stop=True)
                    with pe.Fori(0, ROUNDS) as i:
                        for t in range(TURNS):
                            for j in range(LISTS):
                                k = j * TURNS + t
                                pe.wait_ge(hot_ready[k].sem, hot_ready[k].at(i + 1))
                                pe.matmul(ph[:, j, 0, 0:D], lowerb[:, :], hot[:, k, :], start=False, stop=True, skip_group_check=True).then_inc(places_ready[k].sem, 1)
                            for j in range(LISTS):
                                k = j * TURNS + t
                                pe.wait_ge(rank_ready[k].sem, rank_ready[k].at(i + 1))
                                pe.matmul(ph[:, j, 0, 0:D], restb[:, :], hot[:, k, :], start=False, stop=True, skip_group_check=True).then_inc(hot_used[k].sem, 1)

                @block.gpsimd
                def _(pool):
                    with pool.Fori(0, ROUNDS) as i:
                        for t, j in ORDER:
                            k = j * TURNS + t
                            pool.wait_ge(record_ready[k].sem, record_ready[k].at(i + 1))
                            pool.wait_ge(to_ready[k].sem, to_ready[k].at(i + 1))
                            pool.nop(nofuse=True)
                            pool.indirect_dma_start(
                                out=targets[j][:, :], out_offset=bass.IndirectOffsetOnAxis(ap=to[:, k:k + 1], axis=0),
                                in_=out_rec[:, k, :], in_offset=None, bounds_check=EP, oob_is_err=False).then_inc(scattered[k].sem, 16)
                    for k in range(SLOTS):
                        pool.wait_ge(scattered[k].sem, scattered[k].at(16 * ROUNDS))
                for k in range(SLOTS):
                    for c in (places_ready, hot_ready, rank_ready, record_ready, to_ready):
                        c[k].close(ROUNDS)
                    hot_used[k].close(counting + ROUNDS)
                    count_hot_ready[k].close(counting)
                    scattered[k].close(16 * ROUNDS)
                pe_step.close(1 if digit else 2)

        sort_pass("lo", 0, sorted_lo)
        sort_pass("hi", 1, (by_dst, by_src))

        def prepare(o, src_dram, name, with_rel):
            C = RELS + 1 if with_rel else 1
            with ExitStack() as tmp:
                prv = sb("prv_" + name, [P, T, 4], F32, tmp)
                rec = sb("cur_" + name, [P, T, 4], F32, tmp)
                nxt = sb("nxt_" + name, [P, T, 4], F32, tmp)
                diag = sb("diag_" + name, [P, 2, P], F32, tmp)
                f1 = sb("f1_" + name, [P, T], F32, tmp)
                f2 = sb("f2_" + name, [P, T], F32, tmp)
                samen = sb("samen_" + name, [P, T], F32, tmp)
                end = sb("end_" + name, [P, T], F32, tmp)
                inhead = sb("inhead_" + name, [P, T], F32, tmp)
                intail = sb("intail_" + name, [P, T], F32, tmp)
                back = sb("back_" + name, [P, P], F32, tmp)
                sameC = sb("sameC_" + name, [P, C, T], F32, tmp)
                samenC = sb("samenC_" + name, [P, C, T], F32, tmp)
                V = sb("V_" + name, [P, C, T], F32, tmp)
                fwd = sb("fwd_" + name, [P, C * T], F32, tmp)
                bwd = sb("bwd_" + name, [P, C * T], F32, tmp)
                runs = sb("runs_" + name, [P, 2, C], F32, tmp)
                ph = tmp.enter_context(nc.psum_tensor("ph_" + name, [P, 2, 512], F32))
                pc = tmp.enter_context(nc.psum_tensor("pc_" + name, [P, 2, 512], F32))
                marks = {}
                block = tmp.enter_context(nc.Block())

                @block.sync
                def _(sp):
                    for t_, r0 in ((prv, 0), (rec, 1), (nxt, 2)):
                        sp.dma_start(t_[:, :, :].rearrange("p t f -> p (t f)"),
                                     src_dram[r0:r0 + EP, :].rearrange("(p t) f -> p (t f)", p=P)).then_inc(load[0].sem, 16)
                load[0].close(48)

                @block.vector
                def _(dve):
                    dve.wait_ge(load[0].sem, load[0].base)
                    key, first, last = rec[:, :, 0], rec[:, 0, 0:1], rec[:, T - 1, 0:1]
                    link(dve, dve.tensor_tensor(o.same[:, :], key, prv[:, :, 0], ALU.is_equal))
                    link(dve, dve.memset(o.same[:, 0:1], 0.0))
                    link(dve, dve.tensor_tensor(samen[:, :], key, nxt[:, :, 0], ALU.is_equal))
                    link(dve, dve.tensor_scalar(end[:, :], samen[:, :], -1.0, 1.0, ALU.mult, ALU.add))
                    link(dve, dve.memset(samen[:, T - 1:T], 0.0))
                    link(dve, dve.tensor_scalar(inhead[:, :], key, first, None, ALU.is_equal))
                    link(dve, dve.tensor_scalar(intail[:, :], key, last, None, ALU.is_equal))
                    link(dve, dve.tensor_copy(o.gather[:, :], rec[:, :, 1]))
                    link(dve, dve.tensor_reduce(f1[:, 0:1], inhead[:, :], AX.X, ALU.add))
                    link(dve, dve.scalar_tensor_tensor(f1[:, 0:1], part[:, :], float(T), f1[:, 0:1], ALU.mult, ALU.add))
                    link(dve, dve.tensor_tensor(f2[:, 0:1], first, nxt[:, T - 1, 0:1], ALU.is_equal))
                    link(dve, dve.tensor_scalar(f2[:, 0:1], f2[:, 0:1], FAR, -1.0, ALU.mult, ALU.add))
                    link(dve, dve.tensor_tensor(o.head[:, :], f1[:, 0:1], f2[:, 0:1], ALU.add))
                    link(dve, dve.tensor_scalar(diag[:, 0, :], ident[:, :], first, None, ALU.mult))
                    link(dve, dve.tensor_scalar(diag[:, 1, :], ident[:, :], last, None, ALU.mult))
                    marks["diag"] = chain.base
                    dve.wait_ge(pe_step.sem, pe_step.at(1))
                    link(dve, dve.scalar_tensor_tensor(o.carry[:, :], ph[:, 0, 0:P], last, lower[:, :], ALU.is_equal, ALU.mult))
                    link(dve, dve.scalar_tensor_tensor(back[:, :], ph[:, 1, 0:P], first, upper[:, :], ALU.is_equal, ALU.mult))
                    link(dve, dve.memset(V[:, C - 1, :], 1.0))
                    for r in range(C - 1):
                        link(dve, dve.tensor_scalar(V[:, r, :], rec[:, :, 2], float(r), None, ALU.is_equal))
                    link(dve, dve.tensor_copy(sameC[:, :, :], o.same[:, :].rearrange("p (a t) -> p a t", a=1).broadcast_to([P, C, T])))
                    link(dve, dve.tensor_copy(samenC[:, :, :], samen[:, :].rearrange("p (a t) -> p a t", a=1).broadcast_to([P, C, T])))
                    flat = lambda a: a[:, :, :].rearrange("p c t -> p (c t)")
                    link(dve, dve.tensor_tensor_scan(fwd[:, :], flat(sameC), flat(V), 0.0, ALU.mult, ALU.add))
                    link(dve, dve.tensor_tensor_scan(bwd[:, ::-1], flat(samenC)[:, ::-1], flat(V)[:, ::-1], 0.0, ALU.mult, ALU.add))
                    fw, bw = (a[:, :].rearrange("p (c t) -> p c t", t=T) for a in (fwd, bwd))
                    link(dve, dve.tensor_copy(runs[:, 0, :], fw[:, :, T - 1]))
                    link(dve, dve.tensor_copy(runs[:, 1, :], bw[:, :, 0]))
                    marks["runs"] = chain.base
                    link(dve, dve.tensor_tensor(fwd[:, :], fwd[:, :], bwd[:, :], ALU.add))
                    link(dve, dve.tensor_tensor(fwd[:, :], fwd[:, :], flat(V), ALU.subtract))
                    dve.wait_ge(pe_step.sem, pe_step.at(2))
                    for j, inside in ((0, inhead), (1, intail)):
                        link(dve, dve.tensor_copy(runs[:, j, :], pc[:, j, 0:C]))
                        link(dve, dve.tensor_tensor(sameC[:, :, :], inside[:, :].rearrange("p (a t) -> p a t", a=1).broadcast_to([P, C, T]),
                                                    runs[:, j, :].rearrange("p (c a) -> p c a", a=1).broadcast_to([P, C, T]), ALU.mult))
                        link(dve, dve.tensor_tensor(fwd[:, :], fwd[:, :], flat(sameC), ALU.add))
                    link(dve, dve.tensor_scalar(f1[:, :], fw[:, C - 1, :], 1.0, None, ALU.max))
                    link(dve, dve.reciprocal(o.weight[:, :], f1[:, :]))
                    if with_rel:
                        link(dve, dve.tensor_tensor(V[:, :, :], V[:, :, :], fw, ALU.mult))
                        link(dve, dve.tensor_reduce(f2[:, :], V[:, 0:RELS, :].rearrange("p c t -> p t c"), AX.X, ALU.add))
                        link(dve, dve.tensor_scalar(f2[:, :], f2[:, :], 1.0, None, ALU.max))
                        link(dve, dve.reciprocal(w_rel[:, :], f2[:, :]))
                        link(dve, dve.memset(aux[:, :, :], 0.0))
                        link(dve, dve.tensor_tensor(aux[:, :, 0], f1[:, :], end[:, :], ALU.mult))
                        link(dve, dve.tensor_copy(ed.samen[:, :], samen[:, :]))
                        link(dve, dve.tensor_copy(ed.end[:, :], end[:, :]))
                        link(dve, dve.tensor_copy(ed.inhead[:, :], inhead[:, :]))
                        link(dve, dve.tensor_copy(ed.intail[:, :], intail[:, :]))
                        link(dve, dve.tensor_copy(ed.back[:, :], back[:, :]))
                        link(dve, dve.tensor_scalar(ed.dst[:, :], key, float(N - 1), None, ALU.min))
                        link(dve, dve.tensor_copy(ed.rel[:, :], rec[:, :, 2]))

                @block.tensor
                def _(pe):
                    pe.wait_ge(chain.sem, marks["diag"])
                    pe.matmul(ph[:, 0, 0:P], ones[:, :], diag[:, 0, :], start=True, stop=True)
                    pe.matmul(ph[:, 1, 0:P], ones[:, :], diag[:, 1, :], start=True, stop=True).then_inc(pe_step.sem, 1)
                    pe.wait_ge(chain.sem, marks["runs"])
                    pe.matmul(pc[:, 0, 0:C], o.carry[:, :], runs[:, 0, :], start=True, stop=True)
                    pe.matmul(pc[:, 1, 0:C], back[:, :], runs[:, 1, :], start=True, stop=True).then_inc(pe_step.sem, 1)
                pe_step.close(2)

        prepare(ed, by_dst, "pd", True)
        prepare(es, by_src, "ps", False)

        def all_tiles(eng, *stages):
            most = max(lead for lead, _ in stages)
            loops = (T - most) // SLOTS

            def one(n):
                for lead, work in stages:
                    if 0 <= n + lead < T:
                        work(*divmod(n + lead, SLOTS))
            for n in range(-most, 0):
                one(n)
            with eng.Fori(0, loops) as i:
                for k in range(SLOTS):
                    for lead, work in stages:
                        rounds_on, slot = divmod(k + lead, SLOTS)
                        work(i + rounds_on if rounds_on else i, slot)
            for n in range(loops * SLOTS, T):
                one(n)

        def edge_pass(name, o, table, tw, seg, aw, weight, matrix=None, bias=None, rel=None, with_aux=False, without=None):
            n_pe = 3 if matrix is not None else 1
            BUFS = 4
            with ExitStack() as tmp:
                rows = sb("rows_" + name, [P, SLOTS, tw], F32, tmp)
                gidx = sb("gidx_" + name, [P, SLOTS], I32, tmp)
                msg = sb("msg_" + name, [P, SLOTS, D], F32, tmp)
                acc = sb("acc_" + name, [P, SLOTS, aw], F32, tmp)
                headrow = sb("headrow_" + name, [P, aw], F32, tmp)
                ps = tmp.enter_context(nc.psum_tensor("ps_" + name, [P, 8, 512], F32))
                res, res_ready = acc, acc_ready
                if matrix is not None:
                    res, res_ready = sb("res_" + name, [P, SLOTS, aw], F32, tmp), row_ready
                    accT = sb("accT_" + name, [P, BUFS, D], F32, tmp)
                    carried = sb("carried_" + name, [P, aw], F32, tmp)
                if rel is not None:
                    prod = sb("prod_" + name, [P, BUFS, 1024], F32, tmp)
                    pair = sb("pair_" + name, [P, 2, 512], F32, tmp)
                out_ps = ps[:, 0:4, 0:D]
                turn_ps = rel_ps = ps[:, 4:8, :]

                def before_slot(c, k, i, n=BUFS):
                    q = c[(k - n) % SLOTS]
                    return q.sem, q.at(i + (k >= n))
                msg_used = prod_ready if rel is not None else acc_ready
                pair_ready = row_ready
                marks = {}
                block = tmp.enter_context(nc.Block())

                @block.gpsimd
                def _(pool):
                    def gather(i, k):
                        pool.wait_ge(idx_ready[k].sem, idx_ready[k].at(i + 1))
                        pool.nop(nofuse=True)
                        pool.indirect_dma_start(
                            out=rows[:, k, :], out_offset=None, in_=table[:, :],
                            in_offset=bass.IndirectOffsetOnAxis(ap=gidx[:, k:k + 1], axis=0),
                            bounds_check=N - 1, oob_is_err=False).then_inc(gathered[k].sem, 16)

                    def halve(i, k):
                        if k % 2:
                            return
                        pool.wait_ge(prod_ready[k].sem, prod_ready[k].at(i + 1))
                        pool.wait_ge(*before_slot(product, k, i))
                        pool.tensor_tensor(pair[:, k // 2 % 2, :], prod[:, k % BUFS, 0:512], prod[:, k % BUFS, 512:1024], ALU.add).then_inc(pair_ready[k].sem, 1)

                    if rel is not None:
                        all_tiles(pool, (SLOTS - 2, gather), (0, halve))
                    else:
                        all_tiles(pool, (0, gather))
                    for k in range(SLOTS):
                        pool.wait_ge(stored[k].sem, stored[k].at(16 * ITERS))
                    pool.wait_ge(ready.sem, ready.at(1))
                    pool.indirect_dma_start(
                        out=headrow[:, :], out_offset=None, in_=seg[:, :],
                        in_offset=bass.IndirectOffsetOnAxis(ap=o.head[:, 0:1], axis=0),
                        bounds_check=EP - 1, oob_is_err=False).then_inc(put_head.sem, 16)
                    pool.wait_ge(ready.sem, ready.at(2))
                    pool.indirect_dma_start(
                        out=seg[:, :], out_offset=bass.IndirectOffsetOnAxis(ap=o.head[:, 0:1], axis=0),
                        in_=headrow[:, :], in_offset=None, bounds_check=EP - 1, oob_is_err=False).then_inc(put_head.sem, 16)
                    pool.wait_ge(put_head.sem, put_head.at(32))

                @block.sync
                def _(sp):
                    def store(i, k):
                        sp.wait_ge(res_ready[k].sem, res_ready[k].at(i + 1))
                        sp.nop(nofuse=True)
                        sp.dma_start(seg[0:EP, :].rearrange("(p t) d -> t p d", t=T)[i * SLOTS + k], res[:, k, :]).then_inc(stored[k].sem, 16)
                    if without is not None:
                        sp.dma_start(seg[EP:EP + P, :], without[:, :]).then_inc(load[0].sem, 16)
                    all_tiles(sp, (0, store))
                    if without is not None:
                        sp.wait_ge(load[0].sem, load[0].at(16))
                    for k in range(SLOTS):
                        sp.wait_ge(stored[k].sem, stored[k].at(16 * ITERS))

                @block.scalar
                def _(act):
                    def weigh(i, k):
                        act.wait_ge(gathered[k].sem, gathered[k].at(i * 16 + 16))
                        act.wait_ge(msg_used[k].sem, msg_used[k].at(i))
                        w = rows[:, k, D:D + 1] if weight is None else weight[:, bass.ds(i * SLOTS + k, 1)]
                        act.activation(msg[:, k, :], rows[:, k, 0:D], ACT.Copy, scale=w).then_inc(msg_ready[k].sem, 1)

                    def next_index(i, k):
                        act.wait_ge(msg_ready[k].sem, msg_ready[k].at(i))
                        act.copy(gidx[:, k:k + 1], o.gather[:, bass.ds(i * SLOTS + k, 1)]).then_inc(idx_ready[k].sem, 1)

                    def turn_out(i, k):
                        act.wait_ge(turned[k].sem, turned[k].at(i + 1))
                        act.wait_ge(*before_slot(product, k, i))
                        act.copy(accT[:, k % BUFS, :], turn_ps[:, k % BUFS, 0:D]).then_inc(turned_sb[k].sem, 1)

                    if matrix is None:
                        all_tiles(act, (0, weigh), (SLOTS, next_index))
                    else:
                        all_tiles(act, (4, weigh), (SLOTS + 4, next_index), (0, turn_out))
                        act.wait_ge(pe_step.sem, pe_step.at(2))
                        act.copy(accT[:, 0, :], ps[:, 1, 0:D]).then_inc(act_step.sem, 1)

                @block.vector
                def _(dve):
                    link(dve, dve.memset(acc[:, :, :], 0.0))
                    dve.memset(headrow[:, :], 0.0).then_inc(ready.sem, 1)

                    def multiply(i, k):
                        dve.wait_ge(relw_ready[k].sem, relw_ready[k].at(i + 1))
                        dve.wait_ge(*before_slot(product if k % 2 else pair_ready, k, i))
                        dve.wait_ge(msg_ready[k].sem, msg_ready[k].at(i + 1))
                        for h in range(2):
                            ins = dve.tensor_tensor(
                                prod[:, k % BUFS, h * 512:(h + 1) * 512].rearrange("p (i b o) -> p i b o", i=2, o=4),
                                rel_ps[:, 2 * (k % 2) + h, :].rearrange("p (i b o) -> p i b o", i=2, o=4),
                                msg[:, k, :].rearrange("p (b i a) -> p i b a", i=4, a=1)[:, 2 * h:2 * h + 2].broadcast_to([P, 2, D // 4, 4]),
                                ALU.mult)
                        ins.then_inc(prod_ready[k].sem, 1)

                    def add(i, k):
                        t = bass.ds(i * SLOTS + k, 1)
                        last = acc_ready[(k - 1) % SLOTS]
                        if matrix is not None:
                            dve.wait_ge(turned[k].sem, turned[k].at(i))
                        if res is acc:
                            dve.wait_ge(stored[k].sem, stored[k].at(i * 16))
                        if rel is not None:
                            dve.wait_ge(product[k].sem, product[k].at(i + 1))
                        else:
                            dve.wait_ge(msg_ready[k].sem, msg_ready[k].at(i + 1))
                        dve.wait_ge(last.sem, last.at(i + (k > 0)))
                        new = out_ps[:, k % BUFS, :] if rel is not None else msg[:, k, :]
                        ins = dve.scalar_tensor_tensor(acc[:, k, 0:D], acc[:, (k - 1) % SLOTS, 0:D], o.same[:, t], new, ALU.mult, ALU.add)
                        if with_aux:
                            ins = dve.scalar_tensor_tensor(acc[:, k, D:aw], acc[:, (k - 1) % SLOTS, D:aw], o.same[:, t],
                                                           aux[:, t, :].rearrange("p a f -> p (a f)"), ALU.mult, ALU.add)
                        ins.then_inc(acc_ready[k].sem, 1)

                    def finish(i, k):
                        dve.wait_ge(stored[k].sem, stored[k].at(i * 16))
                        dve.wait_ge(product[k].sem, product[k].at(i + 1))
                        if with_aux:
                            dve.tensor_copy(res[:, k, D:aw], acc[:, k, D:aw])
                        if bias is not None:
                            ins = dve.tensor_tensor(res[:, k, 0:D], out_ps[:, k % BUFS, :], bias[:, 0:D], ALU.add)
                        else:
                            ins = dve.tensor_copy(res[:, k, 0:D], out_ps[:, k % BUFS, :])
                        ins.then_inc(row_ready[k].sem, 1)

                    if matrix is not None:
                        all_tiles(dve, (4, add), (0, finish))
                    elif rel is not None:
                        all_tiles(dve, (3, multiply), (0, add))
                    else:
                        all_tiles(dve, (0, add))
                    dve.wait_ge(put_head.sem, put_head.at(16))
                    dve.wait_ge(pe_step.sem, pe_step.at(1))
                    if matrix is not None:
                        link(dve, dve.tensor_copy(carried[:, :], ps[:, 2, 0:aw]))
                        marks["carried"] = chain.base
                        dve.wait_ge(pe_step.sem, pe_step.at(3))
                        link(dve, dve.tensor_tensor(headrow[:, 0:D], headrow[:, 0:D], ps[:, 3, 0:D], ALU.add))
                        if with_aux:
                            link(dve, dve.tensor_tensor(headrow[:, D:aw], headrow[:, D:aw], carried[:, D:aw], ALU.add))
                    else:
                        link(dve, dve.tensor_tensor(headrow[:, :], headrow[:, :], ps[:, 2, 0:aw], ALU.add))
                    dve.sem_inc(ready.sem, 1)

                @block.tensor
                def _(pe):
                    def turn(i, k):
                        pe.wait_ge(*before_slot(turned_sb, k, i))
                        pe.wait_ge(acc_ready[k].sem, acc_ready[k].at(i + 1))
                        for c in range(C2):
                            ins = pe.transpose(turn_ps[:, k % BUFS, c * P:(c + 1) * P], acc[:, k, c * P:(c + 1) * P], ident[:, :])
                        ins.then_inc(turned[k].sem, 1)

                    def multiply(i, k):
                        pe.wait_ge(*before_slot(row_ready, k, i))
                        pe.wait_ge(turned_sb[k].sem, turned_sb[k].at(i + 1))
                        for c in range(C2):
                            ins = pe.matmul(out_ps[:, k % BUFS, :], accT[:, k % BUFS, c * P:(c + 1) * P], matrix[:, c, :],
                                            start=(c == 0), stop=(c == C2 - 1))
                        ins.then_inc(product[k].sem, 1)

                    def spread(i, k):
                        pe.wait_ge(*before_slot(prod_ready, k, i, 2))
                        for h in range(2):
                            ins = pe.matmul(rel_ps[:, 2 * (k % 2) + h, :], rel_hot[:, bass.ds((i * SLOTS + k) * P, P)],
                                            rel[:, h * 512:(h + 1) * 512], start=True, stop=True)
                        ins.then_inc(relw_ready[k].sem, 1)

                    def block_sum(i, k):
                        pe.wait_ge(*before_slot(acc_ready, k, i))
                        done = prod_ready[k] if k % 2 else pair_ready[k]
                        src, parts = (prod[:, k % BUFS], 4) if k % 2 else (pair[:, k // 2 % 2], 2)
                        pe.wait_ge(done.sem, done.at(i + 1))
                        for j in range(parts):
                            ins = pe.matmul(out_ps[:, k % BUFS, :], ident[:, :], src[:, j * D:(j + 1) * D], start=(j == 0), stop=(j == parts - 1))
                        ins.then_inc(product[k].sem, 1)

                    if matrix is not None:
                        all_tiles(pe, (2, turn), (0, multiply))
                    elif rel is not None:
                        all_tiles(pe, (0, block_sum), (4, spread))
                    pe.wait_ge(acc_ready[SLOTS - 1].sem, acc_ready[SLOTS - 1].at(ITERS))
                    if matrix is not None:
                        for k in range(SLOTS - BUFS, SLOTS):
                            pe.wait_ge(row_ready[k].sem, row_ready[k].at(ITERS))
                    pe.matmul(ps[:, 2, 0:aw], o.carry[:, :], acc[:, SLOTS - 1, :], start=True, stop=True).then_inc(pe_step.sem, 1)
                    if matrix is not None:
                        pe.wait_ge(chain.sem, marks["carried"])
                        for c in range(C2):
                            ins = pe.transpose(ps[:, 1, c * P:(c + 1) * P], carried[:, c * P:(c + 1) * P], ident[:, :])
                        ins.then_inc(pe_step.sem, 1)
                        pe.wait_ge(act_step.sem, act_step.at(1))
                        for c in range(C2):
                            ins = pe.matmul(ps[:, 3, 0:D], accT[:, 0, c * P:(c + 1) * P], matrix[:, c, :], start=(c == 0), stop=(c == C2 - 1))
                        ins.then_inc(pe_step.sem, 1)

                for k in range(SLOTS):
                    for c in (idx_ready, acc_ready, msg_ready):
                        c[k].close(ITERS)
                    gathered[k].close(16 * ITERS)
                    stored[k].close(16 * ITERS)
                    if matrix is not None:
                        for c in (turned, turned_sb, product, row_ready):
                            c[k].close(ITERS)
                    if rel is not None:
                        for c in (relw_ready, prod_ready, product) + (() if k % 2 else (pair_ready,)):
                            c[k].close(ITERS)
                if without is not None:
                    load[0].close(16)
                put_head.close(32)
                ready.close(2)
                pe_step.close(n_pe)
                if matrix is not None:
                    act_step.close(1)

        def batches(eng, *stages):
            most = max(lead for lead, _ in stages)
            least = min(lead for lead, _ in stages)
            assert least >= 0

            def do(work, i, s, n):
                if isinstance(n, int) and n >= NBATCH:
                    work(i, s, n, REST, 1)
                else:
                    work(i, s, n, P, R)

            def one(n):
                for lead, work in stages:
                    if 0 <= n + lead <= NBATCH:
                        do(work, (n + lead) // BSLOTS, (n + lead) % BSLOTS, n + lead)
            for n in range(-most, 0):
                one(n)
            loops = (NBATCH - most) // BSLOTS
            with eng.Fori(0, loops) as i:
                for s in range(BSLOTS):
                    for lead, work in stages:
                        do(work, i + (s + lead) // BSLOTS if s + lead >= BSLOTS else i, (s + lead) % BSLOTS, i * BSLOTS + (s + lead))
            for n in range(loops * BSLOTS, NBATCH + 1):
                one(n)

        def rounds(s):
            return NBATCH // BSLOTS + (s <= NBATCH % BSLOTS)

        def node_pass(name, o, ins, target, kind, matrix=None, bias=None):
            ninp = len(ins) - 1
            norm = kind != "rgcn1" and kind != "gcn"
            own_row = kind in ("gcn", "gat")
            wide = DW if kind == "conv" else D
            with ExitStack() as tmp:
                inp = [[sb(f"in{j}{s}_{name}", [P, R, w], F32, tmp) for j, (_, w) in enumerate(ins)] for s in range(BSLOTS)]
                u = [sb(f"u{s}_{name}", [P, R, wide], F32, tmp) for s in range(BSLOTS)]
                stats = sb(f"stats_{name}", [P, 2, R, 6], F32, tmp)
                mv = sb(f"mv_{name}", [P, BSLOTS, R, 2], F32, tmp)
                dev = sb(f"dev_{name}", [P, BSLOTS, R], F32, tmp)
                scale = sb(f"scale_{name}", [P, BSLOTS, R, 2], F32, tmp)
                own = sb(f"own_{name}", [P, BSLOTS, R], F32, tmp)
                ends = sb(f"ends_{name}", [P, BSLOTS, R], I32, tmp)
                xT = sb(f"xT_{name}", [P, 2, PAIRS, 512], F32, tmp)
                ps = tmp.enter_context(nc.psum_tensor("ps_" + name, [P, 8, 512], F32))
                turn_ps, out_ps = ps[:, 0:PAIRS, :], ps[:, PAIRS:2 * PAIRS, :]
                eps = eps_col[:, 0:1] if kind == "sage" else eps_col[:, 1:2]
                block = tmp.enter_context(nc.Block())

                def view(a, n, pp, r):
                    if pp == P:
                        return a[0:NBATCH * BATCH, :].rearrange("(n p r) d -> n p (r d)", p=P, r=R)[n]
                    return a[NBATCH * BATCH:N, :]

                def pairs(r):
                    return [(g, min(2, r - 2 * g)) for g in range(-(-r // 2))]

                @block.sync
                def _(sp):
                    def fetch(i, s, n, pp, r):
                        sp.wait_ge(batch_done[s].sem, batch_done[s].at(i))
                        sp.nop(nofuse=True)
                        for j, (a, w) in list(enumerate(ins))[1:]:
                            sp.dma_start(inp[s][j][0:pp, 0:r, :].rearrange("p r d -> p (r d)"), view(a, n, pp, r)).then_inc(load[s].sem, 16)
                    batches(sp, (0, fetch))

                @block.gpsimd
                def _(pool):
                    def gather(i, s, n, pp, r):
                        pool.wait_ge(batch_done[s].sem, batch_done[s].at(i))
                        pool.nop(nofuse=True)
                        pool.tensor_copy(ends[0:pp, s, 0:r], o.ends[0:pp, bass.ds(n * R, r)]).then_inc(idx_ready[s].sem, 1)
                        pool.wait_ge(idx_ready[s].sem, idx_ready[s].at(i + 1))
                        pool.nop(nofuse=True)
                        for q in range(r):
                            pool.indirect_dma_start(
                                out=inp[s][0][0:pp, q, :], out_offset=None, in_=ins[0][0][:, :],
                                in_offset=bass.IndirectOffsetOnAxis(ap=ends[0:pp, s, q:q + 1], axis=0),
                                bounds_check=EP + P - 1, oob_is_err=False).then_inc(gathered[s].sem, 16)
                    batches(pool, (0, gather))

                if matrix is not None:
                    @block.tensor
                    def _(pe):
                        def turn(i, s, n, pp, r):
                            if not own_row:
                                pe.wait_ge(load[s].sem, load[s].at((i + 1) * (16 * ninp)))
                            for g, m in pairs(r):
                                if own_row:
                                    pe.wait_ge(pre_ready[g].sem, pre_ready[g].at(n + 1))
                                pe.wait_ge(turned_sb[g].sem, turned_sb[g].at(n))
                                for q in range(m):
                                    for c in range(C2):
                                        z = (2 * q + c) * P
                                        last = pe.transpose(turn_ps[:, g, z:z + pp], inp[s][1][0:pp, 2 * g + q, c * P:(c + 1) * P], ident[0:pp, 0:pp])
                                last.then_inc(turned[g].sem, 1)

                        def multiply(i, s, n, pp, r):
                            for g, m in pairs(r):
                                pe.wait_ge(row_ready[g].sem, row_ready[g].at(n))
                                pe.wait_ge(turned_sb[g].sem, turned_sb[g].at(n + 1))
                                for q in range(m):
                                    if bias is not None:
                                        pe.matmul(out_ps[0:pp, g, q * D:(q + 1) * D], onesb[0:3, 0:pp], bias[:, :], start=True, stop=False)
                                    for c in range(C2):
                                        z = (2 * q + c) * P
                                        last = pe.matmul(out_ps[0:pp, g, q * D:(q + 1) * D], xT[:, s % 2, g, z:z + pp], matrix[:, c, :],
                                                         start=(bias is None and c == 0), stop=(c == C2 - 1))
                                last.then_inc(product[g].sem, 1)
                        batches(pe, (0, multiply), (1, turn))

                @block.scalar
                def _(act):
                    def copy_out(i, s, n, pp, r):
                        for g, m in pairs(r):
                            act.wait_ge(turned[g].sem, turned[g].at(n + 1))
                            if not isinstance(n, int) or n > 0:
                                act.wait_ge(product[g].sem, product[g].at(n - 1))
                            if pp == P:
                                last = act.copy(xT[:, s % 2, g, 0:m * D], turn_ps[:, g, 0:m * D])
                            else:
                                last = act.copy(xT[:, s % 2, g, 0:m * D].rearrange("p (z q) -> p z q", q=P)[:, :, 0:pp],
                                                turn_ps[:, g, 0:m * D].rearrange("p (z q) -> p z q", q=P)[:, :, 0:pp])
                            last.then_inc(turned_sb[g].sem, 1)

                    def deviate(i, s, n, pp, r):
                        act.wait_ge(var_ready.sem, var_ready.at(n + 1))
                        act.activation(dev[0:pp, s, 0:r], mv[0:pp, s, 0:r, 1], ACT.Sqrt, bias=eps[0:pp, :]).then_inc(deviation.sem, 1)

                    def normalise(i, s, n, pp, r):
                        act.wait_ge(acc_ready[s].sem, acc_ready[s].at(i + 1))
                        for q in range(r):
                            last = act.activation(u[s][0:pp, q, 0:D], u[s][0:pp, q, 0:D], ACT.Identity,
                                                  bias=scale[0:pp, s, q, 1:2], scale=scale[0:pp, s, q, 0:1])
                        last.then_inc(batch_out[s].sem, 1)

                    def relu(i, s, n, pp, r):
                        act.wait_ge(acc_ready[s].sem, acc_ready[s].at(i + 1))
                        act.activation(u[s][0:pp, 0:r, :], u[s][0:pp, 0:r, :], ACT.Relu).then_inc(batch_out[s].sem, 1)

                    def store(i, s, n, pp, r):
                        act.wait_ge(batch_out[s].sem, batch_out[s].at(i + 1))
                        act.nop(nofuse=True)
                        act.dma_start(view(target, n, pp, r), u[s][0:pp, 0:r, :].rearrange("p r d -> p (r d)")).then_inc(stored[s].sem, 16)

                    if not norm:
                        batches(act, (2, copy_out), (0, relu), (0, store))
                    elif matrix is None:
                        batches(act, (1, deviate), (0, normalise), (0, store))
                    else:
                        batches(act, (3, copy_out), (1, deviate), (0, normalise), (0, store))
                    for s in range(BSLOTS):
                        act.wait_ge(stored[s].sem, stored[s].at(16 * rounds(s)))
                    if kind == "sage":
                        s = NBATCH % BSLOTS
                        act.wait_ge(acc_ready[s].sem, acc_ready[s].at(rounds(s)))
                        act.activation(cnt_nodes[:, :], cnt_nodes[:, :], ACT.Sqrt, bias=ones[:, 0:1]).then_inc(act_step.sem, 1)
                        act_step.close(1)

                @block.vector
                def _(dve):
                    def join(i, s, n, pp, r):
                        ag, own_in = inp[s][0], inp[s][1]
                        dve.wait_ge(load[s].sem, load[s].at((i + 1) * (16 * ninp)))
                        dve.wait_ge(gathered[s].sem, gathered[s].at(i * (16 * R) + 16 * r))
                        if kind == "gat":
                            dve.tensor_scalar(own[0:pp, s, 0:r], ag[0:pp, 0:r, D + 1], -1.0, 1.0, ALU.mult, ALU.add).then_inc(own_step.sem, 1)
                            dve.wait_ge(own_step.sem, own_step.at(n * 2 + 1))
                            dve.tensor_tensor(own[0:pp, s, 0:r], own[0:pp, s, 0:r], ag[0:pp, 0:r, D], ALU.add).then_inc(own_step.sem, 1)
                            dve.wait_ge(own_step.sem, own_step.at(n * 2 + 2))
                        for g, m in pairs(r):
                            for q in range(2 * g, 2 * g + m):
                                w = dinv[0:pp, bass.ds(n * R + q, 1)] if kind == "gcn" else own[0:pp, s, q:q + 1]
                                last = dve.scalar_tensor_tensor(own_in[0:pp, q, 0:D], own_in[0:pp, q, 0:D], w, ag[0:pp, q, 0:D], ALU.mult, ALU.add)
                            last.then_inc(pre_ready[g].sem, 1)

                    def combine(i, s, n, pp, r):
                        ag, us = inp[s][0], u[s]
                        if not own_row:
                            dve.wait_ge(load[s].sem, load[s].at((i + 1) * (16 * ninp)))
                            dve.wait_ge(gathered[s].sem, gathered[s].at(i * (16 * R) + 16 * r))
                        dve.wait_ge(stored[s].sem, stored[s].at(i * 16))
                        if kind == "sage":
                            dve.tensor_copy(cnt_nodes[0:pp, bass.ds(n * R, r)], ag[0:pp, 0:r, D])
                        if kind == "conv":
                            dve.nop(nofuse=True)
                            dve.tensor_copy(us[0:pp, 0:r, D], dinv[0:pp, bass.ds(n * R, r)])
                        for g, m in pairs(r):
                            a, b = 2 * g, 2 * g + m
                            o_ps = out_ps[0:pp, g, 0:m * D].rearrange("p (r d) -> p r d", d=D)
                            if matrix is not None:
                                dve.wait_ge(product[g].sem, product[g].at(n + 1))
                            if kind in ("sage", "rgcn1", "rgcn2"):
                                dve.tensor_tensor(us[0:pp, a:b, :], o_ps, ag[0:pp, a:b, 0:D], ALU.add).then_inc(row_ready[g].sem, 1)
                            if kind == "gcn":
                                for q in range(a, b):
                                    last = dve.scalar_tensor_tensor(us[0:pp, q, :], o_ps[:, q - a, :], dinv[0:pp, bass.ds(n * R + q, 1)],
                                                                    b_g1[0:pp, :], ALU.mult, ALU.add)
                                last.then_inc(row_ready[g].sem, 1)
                            if kind == "gat":
                                dve.scalar_tensor_tensor(us[0:pp, a:b, :], o_ps, 0.0, inp[s][2][0:pp, a:b, 0:D], ALU.max, ALU.add).then_inc(row_ready[g].sem, 1)
                            if kind == "conv":
                                dve.tensor_tensor(us[0:pp, a:b, 0:D], inp[s][1][0:pp, a:b, 0:D], ag[0:pp, a:b, 0:D], ALU.add).then_inc(row_ready[g].sem, 1)
                            if kind in ("sage", "rgcn1", "rgcn2"):
                                dve.wait_ge(row_ready[g].sem, row_ready[g].at(n + 1))
                            if kind == "sage":
                                dve.scalar_tensor_tensor(us[0:pp, a:b, :], us[0:pp, a:b, :], 0.0, inp[s][1][0:pp, a:b, 0:D], ALU.max, ALU.add).then_inc(sum_ready[g].sem, 1)
                            if kind == "rgcn1":
                                row = b_l1[0:pp, :].rearrange("p (a d) -> p a d", a=1).broadcast_to([pp, m, D])
                                dve.tensor_tensor(us[0:pp, a:b, :], us[0:pp, a:b, :], row, ALU.add).then_inc(sum_ready[g].sem, 1)
                            if kind == "rgcn2":
                                dve.tensor_tensor(us[0:pp, a:b, :], us[0:pp, a:b, :], inp[s][2][0:pp, a:b, 0:D], ALU.add).then_inc(sum_ready[g].sem, 1)
                        c = sum_ready if kind in ("sage", "rgcn1", "rgcn2") else row_ready
                        for g, m in pairs(r):
                            dve.wait_ge(c[g].sem, c[g].at(n + 1))
                            for q in range(2 * g, 2 * g + m):
                                if norm:
                                    last = dve.bn_stats(stats[0:pp, s % 2, q, :], us[0:pp, q, 0:D])
                        if not norm:
                            dve.sem_inc(acc_ready[s].sem, 1)
                        else:
                            last.then_inc(stats_ready.sem, 1)
                            dve.wait_ge(stats_ready.sem, stats_ready.at(n + 1))
                            dve.nop(nofuse=True)
                            for q in range(r):
                                last = dve.bn_aggr(mv[0:pp, s, q, :], stats[0:pp, s % 2, q, :])
                            last.then_inc(var_ready.sem, 1)
                        dve.sem_inc(batch_done[s].sem, 1)

                    def means(i, s, n, pp, r):
                        dve.wait_ge(deviation.sem, deviation.at(n + 1))
                        dve.nop(nofuse=True)
                        dve.reciprocal(scale[0:pp, s, 0:r, 0], dev[0:pp, s, 0:r]).then_inc(rstd_ready.sem, 1)
                        dve.wait_ge(rstd_ready.sem, rstd_ready.at(n + 1))
                        dve.scalar_tensor_tensor(scale[0:pp, s, 0:r, 1], mv[0:pp, s, 0:r, 0], -1.0, scale[0:pp, s, 0:r, 0],
                                                 ALU.mult, ALU.mult).then_inc(acc_ready[s].sem, 1)

                    if kind == "sage":
                        link(dve, dve.memset(cnt_nodes[:, :], 0.0))
                    if kind == "conv":
                        for s in range(BSLOTS):
                            link(dve, dve.memset(u[s][:, :, D:DW], 0.0))
                    work = [(1, combine), (0, means)] if norm else [(0, combine)]
                    if own_row:
                        work = [(work[0][0] + 2, join)] + work
                    batches(dve, *work)
                    if kind == "sage":
                        dve.wait_ge(act_step.sem, act_step.base)
                        link(dve, dve.reciprocal(dinv[:, :], cnt_nodes[:, :]))

                for s in range(BSLOTS):
                    load[s].close(16 * ninp * rounds(s))
                    stored[s].close(16 * rounds(s))
                    for c in (batch_done, batch_out, acc_ready, idx_ready):
                        c[s].close(rounds(s))
                    gathered[s].close(16 * (R * rounds(s) - (R - 1) * (s == NBATCH % BSLOTS)))
                for g in range(PAIRS):
                    steps = NBATCH + (g == 0)
                    row_ready[g].close(steps)
                    if matrix is not None:
                        for c in (turned, turned_sb, product):
                            c[g].close(steps)
                    if own_row:
                        pre_ready[g].close(steps)
                    if kind in ("sage", "rgcn1", "rgcn2"):
                        sum_ready[g].close(steps)
                if norm:
                    for c in (deviation, stats_ready, var_ready, rstd_ready):
                        c.close(NBATCH + 1)
                if kind == "gat":
                    own_step.close(2 * (NBATCH + 1))

        def one_hot_relations():
            with ExitStack() as tmp:
                hot = sb("hot_rel", [P, SLOTS, 96], BF16, tmp)
                BANKS = SLOTS // 2
                ps = tmp.enter_context(nc.psum_tensor("ps_rel", [P, BANKS, 1024], BF16))
                block = tmp.enter_context(nc.Block())

                @block.vector
                def _(dve):
                    with dve.Fori(0, ITERS) as i:
                        for k in range(SLOTS):
                            dve.wait_ge(turned[k].sem, turned[k].at(i))
                            dve.tensor_scalar(hot[:, k, :], rel_iota[:, :], ed.rel[:, bass.ds(i * SLOTS + k, 1)], None, ALU.is_equal).then_inc(msg_ready[k].sem, 1)

                @block.tensor
                def _(pe):
                    with pe.Fori(0, ITERS) as i:
                        for k in range(SLOTS):
                            other = turned_sb[(k - BANKS) % SLOTS]
                            pe.wait_ge(other.sem, other.at(i + (k >= BANKS)))
                            pe.wait_ge(msg_ready[k].sem, msg_ready[k].at(i + 1))
                            pe.transpose(ps[0:96, k % BANKS, 0:P], hot[:, k, :], identb[:, :]).then_inc(turned[k].sem, 1)

                @block.scalar
                def _(act):
                    with act.Fori(0, ITERS) as i:
                        for k in range(SLOTS):
                            act.wait_ge(turned[k].sem, turned[k].at(i + 1))
                            act.copy(rel_hot[:, bass.ds((i * SLOTS + k) * P, P)], ps[0:96, k % BANKS, 0:P]).then_inc(turned_sb[k].sem, 1)
                for k in range(SLOTS):
                    for c in (turned, turned_sb, msg_ready):
                        c[k].close(ITERS)

        def attention():
            BIG = 1e30
            with ExitStack() as tmp:
                rowa = sb("rowa", [P, SLOTS, 2, D], F32, tmp)
                junk = sb("att_junk", [P, SLOTS, 3, D], BF16, tmp)
                gidx = sb("gidx_att", [P, SLOTS, 2], I32, tmp)
                score = sb("score", [P, 3, T], F32, tmp)
                e, es_, m, f, b, t1, pen, penn = (sb("att_" + n, [P, T], F32, tmp) for n in ("e", "es", "m", "f", "b", "t1", "pen", "penn"))
                diag = sb("att_diag", [P, 2, P], F32, tmp)
                col = sb("att_c", [P, 4], F32, tmp)
                msk = sb("att_msk", [P, P], F32, tmp)
                ps = tmp.enter_context(nc.psum_tensor("ps_att", [P, 4, 512], F32))
                marks = {}
                block = tmp.enter_context(nc.Block())

                @block.gpsimd
                def _(pool):
                    with pool.Fori(0, ITERS) as i:
                        for k in range(SLOTS):
                            pool.wait_ge(idx_ready[k].sem, idx_ready[k].at(i + 1))
                            pool.nop(nofuse=True)
                            for j in range(2):
                                pool.indirect_dma_start(
                                    out=rowa[:, k, j, :], out_offset=None, in_=y3[:, :],
                                    in_offset=bass.IndirectOffsetOnAxis(ap=gidx[:, k, j:j + 1], axis=0),
                                    bounds_check=N - 1, oob_is_err=False).then_inc(gathered[k].sem, 16)

                @block.vector
                def _(dve):
                    for k in range(SLOTS):
                        dve.tensor_copy(gidx[:, k, 0:1], ed.gather[:, k:k + 1])
                        dve.tensor_copy(gidx[:, k, 1:2], ed.dst[:, k:k + 1]).then_inc(idx_ready[k].sem, 1)

                    def tile(i, k, more=True):
                        dve.wait_ge(gathered[k].sem, gathered[k].at(i * 32 + 32))
                        for f, (j, v) in enumerate(((0, va), (1, va), (1, vb))):
                            dve.scalar_tensor_tensor(junk[:, k, f, :], rowa[:, k, j, :], 1.0, v[:, :], ALU.mult, ALU.mult,
                                                     accum_out=score[:, f, bass.ds(i * SLOTS + k, 1)])
                        if more:
                            dve.tensor_copy(gidx[:, k, 0:1], ed.gather[:, bass.ds(i * SLOTS + SLOTS + k, 1)])
                            ins = dve.tensor_copy(gidx[:, k, 1:2], ed.dst[:, bass.ds(i * SLOTS + SLOTS + k, 1)])
                            ins.then_inc(idx_ready[k].sem, 1)
                    with dve.Fori(0, ITERS - 1) as i:
                        for k in range(SLOTS):
                            tile(i, k)
                    for k in range(SLOTS):
                        tile(ITERS - 1, k, more=False)
                    link(dve, dve.tensor_copy(col[:, :], part[:, :].broadcast_to([P, 4])))
                    for o_, j in ((e, 0), (es_, 1)):
                        link(dve, dve.tensor_tensor(t1[:, :], score[:, j, :], score[:, 2, :], ALU.add))
                        link(dve, dve.scalar_tensor_tensor(o_[:, :], t1[:, :], 0.2, t1[:, :], ALU.mult, ALU.max))
                    link(dve, dve.tensor_scalar(pen[:, :], ed.same[:, :], -1.0, BIG, ALU.add, ALU.mult))
                    link(dve, dve.tensor_scalar(penn[:, :], ed.samen[:, :], -1.0, BIG, ALU.add, ALU.mult))
                    link(dve, dve.tensor_tensor_scan(f[:, :], pen[:, :], e[:, :], -BIG, ALU.add, ALU.max))
                    link(dve, dve.tensor_tensor_scan(b[:, ::-1], penn[:, ::-1], e[:, ::-1], -BIG, ALU.add, ALU.max))
                    link(dve, dve.tensor_scalar(diag[:, 0, :], ident[:, :], f[:, T - 1:T], None, ALU.mult))
                    link(dve, dve.tensor_scalar(diag[:, 1, :], ident[:, :], b[:, 0:1], None, ALU.mult))
                    marks["diag"] = chain.base
                    link(dve, dve.tensor_tensor(m[:, :], f[:, :], b[:, :], ALU.max))
                    link(dve, dve.tensor_tensor(m[:, :], m[:, :], es_[:, :], ALU.max))
                    dve.wait_ge(pe_step.sem, pe_step.at(1))
                    for j, (mask, inside) in enumerate(((ed.back, ed.inhead), (ed.carry, ed.intail))):
                        link(dve, dve.tensor_scalar(msk[:, :], mask[:, :], -1.0, BIG, ALU.add, ALU.mult))
                        link(dve, dve.tensor_tensor(msk[:, :], msk[:, :], ps[:, j, 0:P], ALU.add))
                        link(dve, dve.tensor_reduce(col[:, j:j + 1], msk[:, :], AX.X, ALU.max))
                        link(dve, dve.tensor_scalar(t1[:, :], inside[:, :], -1.0, BIG, ALU.add, ALU.mult))
                        link(dve, dve.scalar_tensor_tensor(m[:, :], t1[:, :], col[:, j:j + 1], m[:, :], ALU.add, ALU.max))
                    link(dve, dve.tensor_tensor(e[:, :], e[:, :], m[:, :], ALU.subtract))
                    link(dve, dve.tensor_tensor(es_[:, :], es_[:, :], m[:, :], ALU.subtract))
                    marks["sub"] = chain.base
                    dve.wait_ge(act_step.sem, act_step.at(2))
                    link(dve, dve.tensor_tensor_scan(f[:, :], ed.same[:, :], e[:, :], 0.0, ALU.mult, ALU.add))
                    link(dve, dve.tensor_tensor_scan(b[:, ::-1], ed.samen[:, ::-1], e[:, ::-1], 0.0, ALU.mult, ALU.add))
                    marks["sums"] = chain.base
                    link(dve, dve.tensor_tensor(m[:, :], b[:, :], e[:, :], ALU.subtract))
                    link(dve, dve.tensor_tensor(m[:, :], m[:, :], f[:, :], ALU.add))
                    link(dve, dve.tensor_tensor(m[:, :], m[:, :], es_[:, :], ALU.add))
                    dve.wait_ge(pe_step.sem, pe_step.at(2))
                    link(dve, dve.tensor_copy(col[:, 2:4], ps[:, 2, 0:2]))
                    link(dve, dve.scalar_tensor_tensor(m[:, :], ed.inhead[:, :], col[:, 2:3], m[:, :], ALU.mult, ALU.add))
                    link(dve, dve.scalar_tensor_tensor(m[:, :], ed.intail[:, :], col[:, 3:4], m[:, :], ALU.mult, ALU.add))
                    link(dve, dve.tensor_scalar(m[:, :], m[:, :], 1e-16, None, ALU.add))
                    link(dve, dve.reciprocal(t1[:, :], m[:, :]))
                    link(dve, dve.tensor_tensor(w_rel[:, :], e[:, :], t1[:, :], ALU.mult))
                    link(dve, dve.tensor_tensor(t1[:, :], es_[:, :], t1[:, :], ALU.mult))
                    link(dve, dve.tensor_tensor(aux[:, :, 0], t1[:, :], ed.end[:, :], ALU.mult))
                    link(dve, dve.tensor_copy(aux[:, :, 1], ed.end[:, :]))

                @block.scalar
                def _(act):
                    act.wait_ge(chain.sem, marks["sub"])
                    act.activation(e[:, :], e[:, :], ACT.Exp).then_inc(act_step.sem, 1)
                    act.activation(es_[:, :], es_[:, :], ACT.Exp).then_inc(act_step.sem, 1)

                @block.tensor
                def _(pe):
                    pe.wait_ge(chain.sem, marks["diag"])
                    for j in range(2):
                        ins = pe.matmul(ps[:, j, 0:P], ones[:, :], diag[:, j, :], start=True, stop=True)
                    ins.then_inc(pe_step.sem, 1)
                    pe.wait_ge(chain.sem, marks["sums"])
                    pe.matmul(ps[:, 2, 0:1], ed.carry[:, :], f[:, T - 1:T], start=True, stop=True, skip_group_check=True)
                    pe.matmul(ps[:, 2, 1:2], ed.back[:, :], b[:, 0:1], start=True, stop=True, skip_group_check=True).then_inc(pe_step.sem, 1)
                for k in range(SLOTS):
                    idx_ready[k].close(ITERS)
                    gathered[k].close(32 * ITERS)
                pe_step.close(2)
                act_step.close(2)

        rel_scope = ctx.enter_context(ExitStack())
        rel_hot = sb("rel_hot", [96, T * P], BF16, rel_scope)
        one_hot_relations()
        edge_pass("e0", ed, x_in, D, seg_d, DW, ed.weight, matrix=mats["wl"], bias=b_l0, with_aux=True, without=b_l0)
        node_pass("n0", ed, ((seg_d, DW), (x_in, D)), x1, "sage", matrix=mats["wr"])
        edge_pass("e1", ed, x1, D, seg_d, DW, w_rel, rel=rel_w[0], without=no_sum)
        node_pass("n1", ed, ((seg_d, DW), (x1, D)), y1, "rgcn1", matrix=mats["root1"])
        edge_pass("e2", ed, y1, D, seg_d, DW, w_rel, rel=rel_w[1])
        rel_scope.close()
        node_pass("n2", ed, ((seg_d, DW), (y1, D), (x1, D)), x2, "rgcn2", matrix=mats["root2"], bias=bias3["bias2"])
        edge_pass("e3", es, x2, D, seg_s, D, es.weight, matrix=mats["l2"], bias=b_l2)
        node_pass("n3", es, ((seg_s, D), (x2, D)), x3, "conv")
        edge_pass("e4", ed, x3, DW, seg_d, DW, None)
        node_pass("n4", ed, ((seg_d, DW), (x3, DW)), y3, "gcn", matrix=mats["g1"])
        attention()
        edge_pass("e5", ed, y3, D, seg_d, DW, w_rel, with_aux=True)
        node_pass("n5", ed, ((seg_d, DW), (y3, D), (x3, DW)), out, "gat", matrix=mats["g2"], bias=bias3["b2"])


_INS = ["x", "src", "dst", "edge_type_16", "L0_gnn_W_l", "L0_gnn_b_l", "L0_gnn_W_r", "L1_gnn_W1", "L1_gnn_root1",
        "L1_gnn_bias1", "L1_gnn_W2", "L1_gnn_root2", "L1_gnn_bias2", "L2_gnn_W", "L2_gnn_b", "L3_gnn_W1",
        "L3_gnn_b1", "L3_gnn_W2", "L3_gnn_att_src", "L3_gnn_att_dst", "L3_gnn_b2"]


def kernel(**inputs):
    import numpy as _np
    import concourse.bacc as _bacc
    from concourse import mybir as _mybir
    from concourse.bass_utils import run_bass_kernel_spmd as _run

    nc = _bacc.Bacc("TRN2", target_bir_lowering=False, num_devices=1)
    arrays, aps = {}, {}
    for name in _INS:
        a = _np.ascontiguousarray(inputs[name])
        arrays[f"in_{name}_dram"] = a
        aps[name] = nc.dram_tensor(f"in_{name}_dram", a.shape, _mybir.dt.from_np(a.dtype), kind="ExternalInput").ap()
    out = nc.dram_tensor("out_0_dram", inputs["x"].shape, _mybir.dt.float32, kind="ExternalOutput").ap()
    gnn_kernel(nc, aps, out)
    r = _run(nc, [arrays], core_ids=[0])
    return r.results[0]["out_0_dram"]
```
